# Optimizing a Trainium2 kernel written in Bass

```python
import numpy as np
import jax
import jax.numpy as jnp

def _softmax(x, axis=-1):
    return jax.nn.softmax(x, axis=axis)

def _gelu(x):
    return jax.nn.gelu(x, approximate=True)

def _silu(x):
    return jax.nn.silu(x)

def _sigmoid(x):
    return jax.nn.sigmoid(x)

def _layernorm(x, axis=-1, eps=1e-05):
    m = jnp.mean(x, axis=axis, keepdims=True)
    v = jnp.var(x, axis=axis, keepdims=True)
    return (x - m) / jnp.sqrt(v + eps)

def _scatter_add(tgt, idx, src, axis=0):
    return tgt.at[idx].add(src)

def _segment_sum(src, seg, n):
    return jax.ops.segment_sum(src, seg, n)
kernel_name = 'mk_decoder_preln_d2_seqx_r4_6d35db'

def setup_inputs(seed: int=0):
    np.random.seed(seed)
    _w = jnp.asarray

    def _rec_inputs():
        import jax
        import jax.numpy as jnp
        _rk = jax.random.key(seed)
        x = 0.0002417 + 0.9998 * jax.random.normal(jax.random.fold_in(_rk, 1), (16, 256, 256), jnp.float32)
        _lenS = 256 - jax.random.randint(jax.random.fold_in(_rk, 7), (16,), 0, max(1, 256 // 4) + 1, jnp.int32)
        _lenS2 = 77 - jax.random.randint(jax.random.fold_in(_rk, 8), (16,), 0, max(1, 77 // 4) + 1, jnp.int32)
        _ctx_1024P = jax.random.normal(jax.random.fold_in(_rk, 11), (16, 16, 256), jnp.float32)
        _ctx_1024c = jax.random.dirichlet(jax.random.fold_in(_rk, 511), 0.3 * jnp.ones((16,), jnp.float32), (16, 77))
        _ctx_1024t = jnp.einsum('bsk,bkd->bsd', _ctx_1024c, _ctx_1024P)
        _ctx_1024t = _ctx_1024t * jax.lax.rsqrt(jnp.mean(jnp.square(_ctx_1024t)) + 1e-12) * 0.953939
        ctx_1024 = 7.22013e-05 + 1.00017 * (_ctx_1024t + 0.3 * jax.random.normal(jax.random.fold_in(_rk, 611), (16, 77, 256), jnp.float32))
        _validS = jnp.arange(256)[None, :] < _lenS[:, None]
        _validS2 = jnp.arange(77)[None, :] < _lenS2[:, None]
        _causal = jnp.tril(jnp.ones((256, 256), dtype=bool))
        mask_BxS2_bk1 = jnp.broadcast_to(_validS2[:, :], (16, 77))
        mask_SxS2_bk1 = jnp.broadcast_to(_validS2[0:1, :], (256, 77))
        return (x, ctx_1024, mask_BxS2_bk1, mask_SxS2_bk1)
    x, ctx_1024, mask_BxS2_bk1, mask_SxS2_bk1 = _rec_inputs()

    def _L0_attn_setup():
        import jax, jax.numpy as jnp
        import numpy as np
        B, L, D = (2, 512, 256)
        H = 16
        HD = D // H
        WINDOW = 64

        def _window_mask(seq_len, window_size, dtype):
            half = window_size // 2
            i = jnp.arange(seq_len)[:, None]
            j = jnp.arange(seq_len)[None, :]
            allowed = jnp.abs(i - j) <= half
            return jnp.where(allowed, jnp.zeros((), dtype), jnp.asarray(-jnp.inf, dtype))
        key = jax.random.key(seed)
        k1, k2, k3 = jax.random.split(key, 3)
        s = 0.02
        return {'x': jax.random.normal(k1, (B, L, D), dtype=jnp.float32), 'w_qkv': jax.random.normal(k2, (D, 3 * D), dtype=jnp.float32) * s, 'b_qkv': jnp.zeros((3 * D,), dtype=jnp.float32), 'w_out': jax.random.normal(k3, (D, D), dtype=jnp.float32) * s, 'b_out': jnp.zeros((D,), dtype=jnp.float32)}
    _L0_attn_all = _L0_attn_setup()
    _L0_attn_in = {k: v for k, v in _L0_attn_all.items() if k in ('w_qkv', 'b_qkv', 'w_out', 'b_out')}
    del _L0_attn_all

    def _L0_xattn_setup():
        import jax, jax.numpy as jnp
        import numpy as np
        D_MODEL = 256
        NUM_HEADS = 16
        DEPTH = D_MODEL // NUM_HEADS
        B, S = (4, 512)
        NEG_INF = float('-inf')

        def _split_heads(x, b):
            return x.reshape(b, -1, NUM_HEADS, DEPTH).transpose(0, 2, 1, 3)
        key = jax.random.key(seed)
        ks = jax.random.split(key, 12)
        inp = {'value': jax.random.normal(ks[0], (B, S, D_MODEL), jnp.float32), 'key': jax.random.normal(ks[1], (B, S, D_MODEL), jnp.float32), 'query': jax.random.normal(ks[2], (B, S, D_MODEL), jnp.float32), 'key_padding_mask': jnp.arange(S)[None, :] < 3 * S // 4}
        inp['key_padding_mask'] = jnp.broadcast_to(inp['key_padding_mask'], (B, S))
        scale = 1.0 / np.sqrt(D_MODEL)
        inp['Wq'] = jax.random.normal(ks[3], (D_MODEL, D_MODEL), jnp.float32) * scale
        inp['bq'] = jnp.zeros((D_MODEL,), jnp.float32)
        inp['Wk'] = jax.random.normal(ks[4], (D_MODEL, D_MODEL), jnp.float32) * scale
        inp['bk'] = jnp.zeros((D_MODEL,), jnp.float32)
        inp['Wv'] = jax.random.normal(ks[5], (D_MODEL, D_MODEL), jnp.float32) * scale
        inp['bv'] = jnp.zeros((D_MODEL,), jnp.float32)
        inp['Wo'] = jax.random.normal(ks[6], (D_MODEL, D_MODEL), jnp.float32) * scale
        inp['bo'] = jnp.zeros((D_MODEL,), jnp.float32)
        return inp
    _L0_xattn_all = _L0_xattn_setup()
    _L0_xattn_in = {k: v for k, v in _L0_xattn_all.items() if k in ('Wq', 'bq', 'Wk', 'bk', 'Wv', 'bv', 'Wo', 'bo')}
    del _L0_xattn_all

    def _L0_ffn_setup():
        import jax, jax.numpy as jnp
        import numpy as np
        B, S, E, H, NE, TOP_K = (4, 512, 256, 512, 8, 2)
        key = jax.random.key(seed)
        ks = jax.random.split(key, 5)
        s = 0.02
        return {'x': jax.random.normal(ks[0], (B, S, E), jnp.float32), 'w1': jax.random.normal(ks[1], (NE, E, H), jnp.float32) * s, 'b1': jnp.zeros((NE, H), jnp.float32), 'w2': jax.random.normal(ks[2], (NE, H, H), jnp.float32) * s, 'b2': jnp.zeros((NE, H), jnp.float32), 'w3': jax.random.normal(ks[3], (NE, H, E), jnp.float32) * s, 'b3': jnp.zeros((NE, E), jnp.float32), 'gate_w': jax.random.normal(ks[4], (E, NE), jnp.float32) * s, 'gate_b': jnp.zeros((NE,), jnp.float32)}
    _L0_ffn_all = _L0_ffn_setup()
    _L0_ffn_in = {k: v for k, v in _L0_ffn_all.items() if k in ('w1', 'b1', 'w2', 'b2', 'w3', 'b3', 'gate_w', 'gate_b')}
    del _L0_ffn_all

    def _L1_attn_setup():
        import jax, jax.numpy as jnp
        import numpy as np
        D_MODEL = 256
        N_HEADS = 16
        D_HEAD = D_MODEL // N_HEADS
        BLOCK = 128
        B, T = (2, 512)

        def _flash_attention(Q, K, V, block_size, scale):
            Bb, H, Tt, d = Q.shape
            n_blocks = Tt // block_size
            Kb = K.reshape(Bb, H, n_blocks, block_size, d).transpose(2, 0, 1, 3, 4)
            Vb = V.reshape(Bb, H, n_blocks, block_size, d).transpose(2, 0, 1, 3, 4)
            starts = jnp.arange(n_blocks) * block_size
            q_pos = jnp.arange(Tt)

            def step(carry, xs):
                m, l, acc = carry
                kb, vb, st = xs
                scores = scale * jnp.einsum('bhtd,bhsd->bhts', Q, kb)
                kv_pos = st + jnp.arange(block_size)
                future = kv_pos[None, :] > q_pos[:, None]
                scores = jnp.where(future[None, None], -jnp.inf, scores)
                m_new = jnp.maximum(m, jnp.max(scores, axis=-1, keepdims=True))
                p = jnp.exp(scores - m_new)
                corr = jnp.exp(m - m_new)
                l = corr * l + jnp.sum(p, axis=-1, keepdims=True)
                acc = corr * acc + jnp.einsum('bhts,bhsd->bhtd', p, vb)
                return ((m_new, l, acc), None)
            m0 = jnp.full((Bb, H, Tt, 1), -jnp.inf, dtype=jnp.float32)
            l0 = jnp.zeros((Bb, H, Tt, 1), dtype=jnp.float32)
            a0 = jnp.zeros((Bb, H, Tt, d), dtype=jnp.float32)
            (m, l, acc), _ = jax.lax.scan(step, (m0, l0, a0), (Kb, Vb, starts))
            return acc / jnp.maximum(l, 1e-12)
        key = jax.random.key(seed)
        ks = jax.random.split(key, 5)
        x = jax.random.normal(ks[0], (B, T, D_MODEL), dtype=jnp.float32)

        def init_w(k):
            return jax.random.normal(k, (D_MODEL, D_MODEL), dtype=jnp.float32) / np.sqrt(D_MODEL).astype(np.float32)
        return {'x': x, 'Wq': init_w(ks[1]), 'Wk': init_w(ks[2]), 'Wv': init_w(ks[3]), 'Wo': init_w(ks[4])}
    _L1_attn_all = _L1_attn_setup()
    _L1_attn_in = {k: v for k, v in _L1_attn_all.items() if k in ('Wq', 'Wk', 'Wv', 'Wo')}
    del _L1_attn_all

    def _L1_xattn_setup():
        import jax, jax.numpy as jnp
        import numpy as np
        D = 256
        H = 16
        HD = D // H
        SCALE = 1.0 / np.sqrt(HD)

        def _split_heads(x):
            B, S, _ = x.shape
            return x.reshape(B, S, H, HD).transpose(0, 2, 1, 3)
        key = jax.random.key(seed)
        ks = jax.random.split(key, 12)
        B, S = (4, 512)
        inp = {'queries': jax.random.normal(ks[0], (B, S, D), jnp.float32), 'keys': jax.random.normal(ks[1], (B, S, D), jnp.float32), 'values': jax.random.normal(ks[2], (B, S, D), jnp.float32), 'mask': jax.random.randint(ks[3], (S, S), 0, 2).astype(bool), 'Wq': jax.random.normal(ks[4], (D, D), jnp.float32) * 0.02, 'bq': jax.random.normal(ks[5], (D,), jnp.float32) * 0.02, 'Wk': jax.random.normal(ks[6], (D, D), jnp.float32) * 0.02, 'bk': jax.random.normal(ks[7], (D,), jnp.float32) * 0.02, 'Wv': jax.random.normal(ks[8], (D, D), jnp.float32) * 0.02, 'bv': jax.random.normal(ks[9], (D,), jnp.float32) * 0.02, 'Wo': jax.random.normal(ks[10], (D, D), jnp.float32) * 0.02, 'bo': jax.random.normal(ks[11], (D,), jnp.float32) * 0.02}
        return inp
    _L1_xattn_all = _L1_xattn_setup()
    _L1_xattn_in = {k: v for k, v in _L1_xattn_all.items() if k in ('Wq', 'bq', 'Wk', 'bk', 'Wv', 'bv', 'Wo', 'bo')}
    del _L1_xattn_all

    def _L1_ffn_setup():
        import jax, jax.numpy as jnp
        import numpy as np
        BLOCK = 32
        W_BITS = 4
        ACT_BITS = 16

        def act_qdq(x):
            qmax = 2.0 ** (ACT_BITS - 1) - 1.0
            scale = jnp.maximum(jnp.max(jnp.abs(x)) / qmax, 1e-12)
            return jnp.clip(jnp.round(x / scale), -qmax - 1.0, qmax) * scale

        def fixed_qdq_u16(x):
            scale = 1.0 / 65536.0
            return jnp.clip(jnp.round(x / scale), 0.0, 65535.0) * scale

        def lpbq_dequant(w):
            O, I = w.shape
            qmax = 2.0 ** (W_BITS - 1) - 1.0
            wb = w.reshape(O, I // BLOCK, BLOCK)
            s = jnp.maximum(jnp.max(jnp.abs(wb), axis=-1, keepdims=True) / qmax, 1e-12)
            wq = jnp.clip(jnp.round(wb / s), -qmax - 1.0, qmax) * s
            return wq.reshape(O, I)
        key = jax.random.key(seed)
        k1, k2, k3, k4 = jax.random.split(key, 4)
        B, S, H, I = (2, 1024, 256, 768)
        x = jax.random.normal(k1, (B, S, H), jnp.float32)
        w_gate = jax.random.normal(k2, (I, H), jnp.float32) * 0.02
        w_up = jax.random.normal(k3, (I, H), jnp.float32) * 0.02
        w_down = jax.random.normal(k4, (H, I), jnp.float32) * 0.02
        return {'x': x, 'w_gate': w_gate, 'w_up': w_up, 'w_down': w_down}
    _L1_ffn_all = _L1_ffn_setup()
    _L1_ffn_in = {k: v for k, v in _L1_ffn_all.items() if k in ('w_gate', 'w_up', 'w_down')}
    del _L1_ffn_all
    return {'x': x, 'ctx_1024': ctx_1024, 'mask_BxS2_bk1': mask_BxS2_bk1, 'mask_SxS2_bk1': mask_SxS2_bk1, 'L0_attn_w_qkv': _L0_attn_in['w_qkv'], 'L0_attn_b_qkv': _L0_attn_in['b_qkv'], 'L0_attn_w_out': _L0_attn_in['w_out'], 'L0_attn_b_out': _L0_attn_in['b_out'], 'L0_xattn_Wq': _L0_xattn_in['Wq'], 'L0_xattn_bq': _L0_xattn_in['bq'], 'L0_xattn_Wk': _L0_xattn_in['Wk'], 'L0_xattn_bk': _L0_xattn_in['bk'], 'L0_xattn_Wv': _L0_xattn_in['Wv'], 'L0_xattn_bv': _L0_xattn_in['bv'], 'L0_xattn_Wo': _L0_xattn_in['Wo'], 'L0_xattn_bo': _L0_xattn_in['bo'], 'L0_ffn_w1': _L0_ffn_in['w1'], 'L0_ffn_b1': _L0_ffn_in['b1'], 'L0_ffn_w2': _L0_ffn_in['w2'], 'L0_ffn_b2': _L0_ffn_in['b2'], 'L0_ffn_w3': _L0_ffn_in['w3'], 'L0_ffn_b3': _L0_ffn_in['b3'], 'L0_ffn_gate_w': _L0_ffn_in['gate_w'], 'L0_ffn_gate_b': _L0_ffn_in['gate_b'], 'L1_attn_Wq': _L1_attn_in['Wq'], 'L1_attn_Wk': _L1_attn_in['Wk'], 'L1_attn_Wv': _L1_attn_in['Wv'], 'L1_attn_Wo': _L1_attn_in['Wo'], 'L1_xattn_Wq': _L1_xattn_in['Wq'], 'L1_xattn_bq': _L1_xattn_in['bq'], 'L1_xattn_Wk': _L1_xattn_in['Wk'], 'L1_xattn_bk': _L1_xattn_in['bk'], 'L1_xattn_Wv': _L1_xattn_in['Wv'], 'L1_xattn_bv': _L1_xattn_in['bv'], 'L1_xattn_Wo': _L1_xattn_in['Wo'], 'L1_xattn_bo': _L1_xattn_in['bo'], 'L1_ffn_w_gate': _L1_ffn_in['w_gate'], 'L1_ffn_w_up': _L1_ffn_in['w_up'], 'L1_ffn_w_down': _L1_ffn_in['w_down']}

def reference(x, ctx_1024, mask_BxS2_bk1, mask_SxS2_bk1, L0_attn_w_qkv, L0_attn_b_qkv, L0_attn_w_out, L0_attn_b_out, L0_xattn_Wq, L0_xattn_bq, L0_xattn_Wk, L0_xattn_bk, L0_xattn_Wv, L0_xattn_bv, L0_xattn_Wo, L0_xattn_bo, L0_ffn_w1, L0_ffn_b1, L0_ffn_w2, L0_ffn_b2, L0_ffn_w3, L0_ffn_b3, L0_ffn_gate_w, L0_ffn_gate_b, L1_attn_Wq, L1_attn_Wk, L1_attn_Wv, L1_attn_Wo, L1_xattn_Wq, L1_xattn_bq, L1_xattn_Wk, L1_xattn_bk, L1_xattn_Wv, L1_xattn_bv, L1_xattn_Wo, L1_xattn_bo, L1_ffn_w_gate, L1_ffn_w_up, L1_ffn_w_down):
    import jax
    import jax.numpy as jnp

    def _L0_attn_ref(x, w_qkv, b_qkv, w_out, b_out):
        import jax, jax.numpy as jnp
        import numpy as np
        B, L, D = (2, 512, 256)
        H = 16
        HD = D // H
        WINDOW = 64

        def _window_mask(seq_len, window_size, dtype):
            half = window_size // 2
            i = jnp.arange(seq_len)[:, None]
            j = jnp.arange(seq_len)[None, :]
            allowed = jnp.abs(i - j) <= half
            return jnp.where(allowed, jnp.zeros((), dtype), jnp.asarray(-jnp.inf, dtype))
        b, l, d = x.shape
        qkv = x @ w_qkv + b_qkv
        qkv = qkv.reshape(b, l, 3, H, HD)
        q = jnp.transpose(qkv[:, :, 0], (0, 2, 1, 3))
        k = jnp.transpose(qkv[:, :, 1], (0, 2, 1, 3))
        v = jnp.transpose(qkv[:, :, 2], (0, 2, 1, 3))
        scale = 1.0 / np.sqrt(HD)
        scores = jnp.einsum('bhqd,bhkd->bhqk', q, k) * scale
        scores = scores + _window_mask(l, WINDOW, scores.dtype)[None, None]
        attn = jax.nn.softmax(scores, axis=-1)
        out = jnp.einsum('bhqk,bhkd->bhqd', attn, v)
        out = jnp.transpose(out, (0, 2, 1, 3)).reshape(b, l, d)
        return out @ w_out + b_out

    def _L0_xattn_ref(value, key, query, key_padding_mask, Wq, bq, Wk, bk, Wv, bv, Wo, bo):
        import jax, jax.numpy as jnp
        import numpy as np
        D_MODEL = 256
        NUM_HEADS = 16
        DEPTH = D_MODEL // NUM_HEADS
        B, S = (4, 512)
        NEG_INF = float('-inf')

        def _split_heads(x, b):
            return x.reshape(b, -1, NUM_HEADS, DEPTH).transpose(0, 2, 1, 3)
        b = query.shape[0]
        q = _split_heads(query @ Wq + bq, b)
        k = _split_heads(key @ Wk + bk, b)
        v = _split_heads(value @ Wv + bv, b)
        logits = jnp.einsum('bhqd,bhkd->bhqk', q, k) / jnp.sqrt(jnp.asarray(DEPTH, q.dtype))
        logits = jnp.where(key_padding_mask[:, None, None, :], logits, NEG_INF)
        attn = jax.nn.softmax(logits, axis=-1)
        out = jnp.einsum('bhqk,bhkd->bhqd', attn, v)
        out = out.transpose(0, 2, 1, 3).reshape(b, -1, D_MODEL)
        return out @ Wo + bo

    def _L0_ffn_ref(x, w1, b1, w2, b2, w3, b3, gate_w, gate_b):
        import jax, jax.numpy as jnp
        import numpy as np
        B, S, E, H, NE, TOP_K = (4, 512, 256, 512, 8, 2)
        gate_weights = jax.nn.softmax(x @ gate_w + gate_b, axis=-1)
        topk_vals, topk_idx = jax.lax.top_k(gate_weights, TOP_K)
        h = jax.nn.gelu(jnp.einsum('bse,neh->bsnh', x, w1) + b1, approximate=False)
        h = jax.nn.gelu(jnp.einsum('bsnh,nhk->bsnk', h, w2) + b2, approximate=False)
        expert_out = jnp.einsum('bsnh,nhe->bsne', h, w3) + b3
        gathered = jnp.take_along_axis(expert_out, topk_idx[..., None], axis=2)
        return jnp.sum(topk_vals[..., None] * gathered, axis=2)

    def _L1_attn_ref(x, Wq, Wk, Wv, Wo):
        import jax, jax.numpy as jnp
        import numpy as np
        D_MODEL = 256
        N_HEADS = 16
        D_HEAD = D_MODEL // N_HEADS
        BLOCK = 128
        B, T = (2, 512)

        def _flash_attention(Q, K, V, block_size, scale):
            Bb, H, Tt, d = Q.shape
            n_blocks = Tt // block_size
            Kb = K.reshape(Bb, H, n_blocks, block_size, d).transpose(2, 0, 1, 3, 4)
            Vb = V.reshape(Bb, H, n_blocks, block_size, d).transpose(2, 0, 1, 3, 4)
            starts = jnp.arange(n_blocks) * block_size
            q_pos = jnp.arange(Tt)

            def step(carry, xs):
                m, l, acc = carry
                kb, vb, st = xs
                scores = scale * jnp.einsum('bhtd,bhsd->bhts', Q, kb)
                kv_pos = st + jnp.arange(block_size)
                future = kv_pos[None, :] > q_pos[:, None]
                scores = jnp.where(future[None, None], -jnp.inf, scores)
                m_new = jnp.maximum(m, jnp.max(scores, axis=-1, keepdims=True))
                p = jnp.exp(scores - m_new)
                corr = jnp.exp(m - m_new)
                l = corr * l + jnp.sum(p, axis=-1, keepdims=True)
                acc = corr * acc + jnp.einsum('bhts,bhsd->bhtd', p, vb)
                return ((m_new, l, acc), None)
            m0 = jnp.full((Bb, H, Tt, 1), -jnp.inf, dtype=jnp.float32)
            l0 = jnp.zeros((Bb, H, Tt, 1), dtype=jnp.float32)
            a0 = jnp.zeros((Bb, H, Tt, d), dtype=jnp.float32)
            (m, l, acc), _ = jax.lax.scan(step, (m0, l0, a0), (Kb, Vb, starts))
            return acc / jnp.maximum(l, 1e-12)
        Bx, Tx, _ = x.shape
        scale = 1.0 / np.sqrt(D_HEAD).astype(np.float32)

        def proj(W):
            y = jnp.einsum('btm,nm->btn', x, W)
            return y.reshape(Bx, Tx, N_HEADS, D_HEAD).transpose(0, 2, 1, 3)
        Q, K, V = (proj(Wq), proj(Wk), proj(Wv))
        O = _flash_attention(Q.astype(jnp.float32), K.astype(jnp.float32), V.astype(jnp.float32), BLOCK, scale)
        O = O.astype(x.dtype).transpose(0, 2, 1, 3).reshape(Bx, Tx, D_MODEL)
        return jnp.einsum('btm,nm->btn', O, Wo)

    def _L1_xattn_ref(queries, keys, values, mask, Wq, bq, Wk, bk, Wv, bv, Wo, bo):
        import jax, jax.numpy as jnp
        import numpy as np
        D = 256
        H = 16
        HD = D // H
        SCALE = 1.0 / np.sqrt(HD)

        def _split_heads(x):
            B, S, _ = x.shape
            return x.reshape(B, S, H, HD).transpose(0, 2, 1, 3)
        q = _split_heads(queries @ Wq + bq)
        k = _split_heads(keys @ Wk + bk)
        v = _split_heads(values @ Wv + bv)
        scores = jnp.einsum('bhqd,bhkd->bhqk', q, k) * SCALE
        neg = jnp.finfo(scores.dtype).min
        scores = jnp.where(mask[None, None, :, :], scores, neg)
        probs = jax.nn.softmax(scores, axis=-1)
        ctx = jnp.einsum('bhqk,bhkd->bhqd', probs, v)
        B, _, Sq, _ = ctx.shape
        combined = ctx.transpose(0, 2, 1, 3).reshape(B, Sq, D)
        return combined @ Wo + bo

    def _L1_ffn_ref(x, w_gate, w_up, w_down):
        import jax, jax.numpy as jnp
        import numpy as np
        BLOCK = 32
        W_BITS = 4
        ACT_BITS = 16

        def act_qdq(x):
            qmax = 2.0 ** (ACT_BITS - 1) - 1.0
            scale = jnp.maximum(jnp.max(jnp.abs(x)) / qmax, 1e-12)
            return jnp.clip(jnp.round(x / scale), -qmax - 1.0, qmax) * scale

        def fixed_qdq_u16(x):
            scale = 1.0 / 65536.0
            return jnp.clip(jnp.round(x / scale), 0.0, 65535.0) * scale

        def lpbq_dequant(w):
            O, I = w.shape
            qmax = 2.0 ** (W_BITS - 1) - 1.0
            wb = w.reshape(O, I // BLOCK, BLOCK)
            s = jnp.maximum(jnp.max(jnp.abs(wb), axis=-1, keepdims=True) / qmax, 1e-12)
            wq = jnp.clip(jnp.round(wb / s), -qmax - 1.0, qmax) * s
            return wq.reshape(O, I)
        x = act_qdq(x)
        up = act_qdq(x @ lpbq_dequant(w_up).T)
        gate = act_qdq(x @ lpbq_dequant(w_gate).T)
        sig = fixed_qdq_u16(jax.nn.sigmoid(gate))
        gate = act_qdq(gate * sig)
        o = act_qdq(gate * up)
        return o @ lpbq_dequant(w_down).T
    x = x + _L0_attn_ref(_layernorm(x, axis=-1), L0_attn_w_qkv, L0_attn_b_qkv, L0_attn_w_out, L0_attn_b_out)
    x = x + _L0_xattn_ref(ctx_1024, ctx_1024, _layernorm(x, axis=-1), mask_BxS2_bk1, L0_xattn_Wq, L0_xattn_bq, L0_xattn_Wk, L0_xattn_bk, L0_xattn_Wv, L0_xattn_bv, L0_xattn_Wo, L0_xattn_bo)
    x = x + _L0_ffn_ref(_layernorm(x, axis=-1), L0_ffn_w1, L0_ffn_b1, L0_ffn_w2, L0_ffn_b2, L0_ffn_w3, L0_ffn_b3, L0_ffn_gate_w, L0_ffn_gate_b)
    x = x + _L1_attn_ref(_layernorm(x, axis=-1), L1_attn_Wq, L1_attn_Wk, L1_attn_Wv, L1_attn_Wo)
    x = x + _L1_xattn_ref(_layernorm(x, axis=-1), ctx_1024, ctx_1024, mask_SxS2_bk1, L1_xattn_Wq, L1_xattn_bq, L1_xattn_Wk, L1_xattn_bk, L1_xattn_Wv, L1_xattn_bv, L1_xattn_Wo, L1_xattn_bo)
    x = x + _L1_ffn_ref(_layernorm(x, axis=-1), L1_ffn_w_gate, L1_ffn_w_up, L1_ffn_w_down)
    return x

_drawn_inputs = setup_inputs


def setup_inputs(seed=0):
    import zlib

    import numpy as np

    out = dict(_drawn_inputs(seed))
    spreads = {'L0_attn_b_qkv': (0.0, 0.1),
     'L0_attn_b_out': (0.0, 0.1),
     'L0_xattn_bq': (0.0, 0.327),
     'L0_xattn_bk': (0.0, 2.0),
     'L0_xattn_bv': (0.0, 0.1),
     'L0_xattn_bo': (0.0, 0.1),
     'L0_ffn_b1': (0.0, 0.8),
     'L0_ffn_b2': (0.0, 0.8),
     'L0_ffn_b3': (0.0, 1.438),
     'L0_ffn_gate_b': (0.0, 0.602)}
    factors = {'L0_attn_w_qkv': 4.274,
     'L0_ffn_w1': 8.0,
     'L0_ffn_w2': 8.0,
     'L0_ffn_w3': 8.0,
     'L0_ffn_gate_w': 3.12,
     'L1_xattn_Wq': 44.855,
     'L1_xattn_bq': 64.0,
     'L1_xattn_Wk': 44.398,
     'L1_xattn_bk': 64.0,
     'L1_xattn_bv': 64.0,
     'L1_xattn_bo': 24.167,
     'L1_xattn_Wv': 4.776,
     'L1_xattn_Wo': 4.245,
     'L1_ffn_w_gate': 8.0,
     'L1_ffn_w_up': 8.0,
     'L1_ffn_w_down': 8.0}
    for name, (base, spread) in spreads.items():
        noise = np.random.default_rng([zlib.crc32(name.encode()), seed]).standard_normal(out[name].shape)
        drawn = base * np.exp(spread * noise) if base else spread * noise
        out[name] = jnp.asarray(drawn.astype(out[name].dtype))
    for name, factor in factors.items():
        out[name] = (out[name] * factor).astype(out[name].dtype)
    return out
```

```python
import concourse.bass as bass
from concourse import mybir
from contextlib import ExitStack, contextmanager

F32 = mybir.dt.float32
F32R = mybir.dt.float32r
BF16 = mybir.dt.bfloat16
I16 = mybir.dt.int16
U16 = mybir.dt.uint16
U8 = mybir.dt.uint8
I32 = mybir.dt.int32
U32 = mybir.dt.uint32
ALU = mybir.AluOpType
ACT = mybir.ActivationFunctionType
AX = mybir.AxisListType

B, S, D = 16, 256, 256
S2 = 77
S2P = S2 + 1
H = 16
HD = D // H
P = 128
KC = D // P
ST = S // P
TILES = B * ST
EPS = 1e-5
MASKED = -float(2 ** 100)
VW = 32


def wait(engine, semaphore, value):
    if isinstance(value, int) and value <= 0:
        return
    engine.wait_ge(semaphore, value)


@contextmanager
def semaphores(nc, phase):
    taken = []

    def sem(name):
        taken.append(nc.alloc_semaphore(f"{phase}_{name}"))
        return taken[-1]

    yield sem
    nc.clear_and_free_semaphores(taken)
    nc.all_engine_barrier()


def inverse_deviation(nc, pool, ln, par, chain, n, done):
    nc.gpsimd.tensor_tensor(ln["var_eps"][par][:], ln["mv"][par][:, :, 1], ln["eps"][:], ALU.add).then_inc(chain, 1)
    pool.wait_ge(chain, n + 1)
    nc.gpsimd.tensor_tensor(ln["rstd"][par][:], ln["var_eps"][par][:], ln["half"][:], ALU.pow).then_inc(done, 1)


def gate(engine, passed):
    engine.sem_inc(passed, 1)


def layernorm_tiles(sb):
    ln = {n: [sb(f"{n}{i}", [P, ST] + rest, F32) for i in range(2)]
          for n, rest in (("stats", [6]), ("mv", [2]), ("var_eps", []), ("rstd", []))}
    ln |= {n: sb(n, [P, ST], F32) for n in ("eps", "half")}
    return ln


def statistics(nc, dve, ln, par, rows, bn, passed, stat, b):
    for s in range(ST):
        op = nc.vector.bn_stats(ln["stats"][par][:, s, :], rows(b, s))
    op.then_inc(bn, 1)
    dve.wait_ge(bn, b + 1)
    gate(dve, passed)
    for s in range(ST):
        op = nc.vector.bn_aggr(ln["mv"][par][:, s, :], ln["stats"][par][:, s, :])
    op.then_inc(stat, 1)


def normalise(nc, ln, par, rows, out, normed, b):
    for s in range(ST):
        op = nc.vector.tensor_scalar(out[:, s, :], rows(b, s), ln["mv"][par][:, s, 0:1],
                                     ln["rstd"][par][:, s:s + 1], ALU.subtract, ALU.mult)
    op.then_inc(normed, 1)


def attention(nc, kind, x_sb, ident, ident_bf, w, scratch, ctxT=None, masks=None):
    cross = kind in ("cross_pad", "cross_mask")
    NK = S2 if cross else S
    NKC = S2P if cross else S
    KTILES = 1 if cross else ST
    KROWS = S2 if cross else P

    if kind == "window":
        R = 32
        W1 = P + R
        direct = [(0, 0, W1, 0), (1, S - W1, W1, W1)]
        transposed = [(0, 0, W1, 0), (1, S - W1, W1, W1)]
        mask_at, mask_n = (0, 0), 2 * W1
    elif kind == "causal":
        direct = [(1, 0, S, 0), (0, 0, P, S)]
        transposed = [(1, P, P, 0), (0, 0, S, P)]
        mask_at, mask_n = (P, 0), 2 * P
    else:
        direct = [(0, 0, NKC, 0), (1, 0, NKC, NKC)]
        transposed = [(0, 0, S, 0)]
        mask_at, mask_n = (0, 0), 0
    EW = max(c + n for _, _, n, c in transposed)

    with ExitStack() as ctx:
        def sb(name, shape, dt):
            return ctx.enter_context(nc.sbuf_tensor(f"{kind}_{name}", shape, dt))

        def pb(name, shape):
            return ctx.enter_context(nc.psum_tensor(f"{kind}_{name}", shape, F32))

        sem = ctx.enter_context(semaphores(nc, kind))

        wq = sb("wq", [P, KC, D], F32)
        wk = sb("wk", [P, KC, D], F32)
        wv = sb("wv", [P, KC, D], F32)
        wo = sb("wo", [P, KC, D], F32)
        bq = sb("bq", [P, KC], F32)
        bk = sb("bk", [P, KC], F32)
        bv = sb("bv", [P, KC], F32)
        bo = sb("bo", [1, D], F32)
        bv_wide = sb("bv_wide", [P, KC, P], F32)
        ones_row = sb("ones_row", [1, P], F32)
        out_bias = sb("out_bias", [P, D], F32)
        q_stack = [sb(f"q_stack{i}", [P, H, S], F32R) for i in range(2)]
        k_stack = [sb(f"k_stack{i}", [P, H, NKC], F32R) for i in range(2)]
        v_aug = [sb(f"v_aug{i}", [P, KTILES, H, VW], F32) for i in range(2)]
        v_stage = sb("v_stage", [P, KTILES * H, HD], F32)
        prob = sb("prob", [P, 4, EW], F32)
        ln = layernorm_tiles(sb)
        xn = [sb(f"xn{i}", [P, ST, D], F32) for i in range(2)]
        xT = sb("xT", [P, KC, S], F32)
        q_parts = sb("q_parts", [P, 2, KC, S], F32R)
        k_parts = sb("k_parts", [P, 2, KC, NK], F32R)
        m_tok = [sb(f"m_tok{i}", [P, ST, H], F32) for i in range(2)]
        m_parts = sb("m_parts", [H // 2, 2, S], F32R)
        o_aug = sb("o_aug", [P, 4, S], F32)
        recip = sb("recip", [P, ST * H], F32)
        o_tok = sb("o_tok", [P, ST, H, HD], F32)
        oT = sb("oT", [P, KC, S], F32)
        if cross:
            ctx_b = [sb(f"ctx_b{i}", [P, KC, S2], F32) for i in range(2)]
        if kind == "window":
            mask1 = mask2 = sb("mask", [P, mask_n], BF16)
        elif kind == "causal":
            mask1 = sb("mask1", [P, mask_n], BF16)
            mask2 = sb("mask2", [P, mask_n], BF16)
        elif kind == "cross_mask":
            mask_u8 = sb("mask_u8", [P, ST, S2], U8)
            maskT_u8 = sb("maskT_u8", [S2, S], U8)
            mask1 = sb("mask1", [P, ST * NKC], BF16)
            mask2 = sb("mask2", [P, S], BF16)
            mask_n = 1
        else:
            pad_u8 = sb("pad_u8", [B, S2], U8)
            pad_f = sb("pad_f", [B, S2], F32)

        ps1 = pb("ps1", [P, 2, 512])
        ps2 = pb("ps2", [P, 2, 512])
        pso = pb("pso", [P, 2, 512])
        misc = pb("misc", [P, 2, 512])

        loaded = sem("loaded")
        consts = sem("consts")
        scaled = sem("scaled")
        bias_mm = sem("bias_mm")
        bias_done = sem("bias_done")
        padrow = sem("padrow")
        bn = sem("bn")
        stat = sem("stat")
        pool_chain = sem("pool_chain")
        scaled_by = sem("scaled_by")
        dve_passed = sem("dve_passed")
        pool_passed = sem("pool_passed")
        normed = sem("normed")
        biased = sem("biased")
        ctx_ready = sem("ctx_ready")
        xT_mm = sem("xT_mm")
        xT_ev = sem("xT_ev")
        q_mm = sem("q_mm")
        q_hi = sem("q_hi")
        q_lo = sem("q_lo")
        k_mm = sem("k_mm")
        k_hi = sem("k_hi")
        k_lo = sem("k_lo")
        v_mm = sem("v_mm")
        v_ev = sem("v_ev")
        v_in = sem("v_in")
        parts_out = sem("parts_out")
        stacked = [sem(f"stacked{i}") for i in range(2)]
        s1_mm = sem("s1_mm")
        s1_max = sem("s1_max")
        m_mm = sem("m_mm")
        m_hi = sem("m_hi")
        m_lo = sem("m_lo")
        m_out = sem("m_out")
        m_in = [sem(f"m_in{i}") for i in range(2)]
        s2_mm = sem("s2_mm")
        expd = sem("expd")
        pv_mm = sem("pv_mm")
        o_ev = sem("o_ev")
        o_mm = sem("o_mm")
        recip_done = sem("recip_done")
        o_norm = sem("o_norm")
        oT_mm = sem("oT_mm")
        oT_ev = sem("oT_ev")
        proj_mm = sem("proj_mm")
        added = sem("added")

        N_LOAD = 16 * (4 + (4 if w["bq"] is not None else 0)
                       + {"cross_mask": 2, "cross_pad": 1}.get(kind, 0))
        bank = lambda k: misc[:, k, :]
        xT_ps = bank(0).rearrange("p (k t) -> p k t", k=KC)
        q_ps = bank(1).rearrange("p (k t) -> p k t", k=KC)
        k_ps = bank(0)[:, 0:KC * NK].rearrange("p (k t) -> p k t", k=KC)
        v_ps = bank(1)[:, 0:KTILES * D].rearrange("p (k h d) -> p (k h) d", k=KTILES, d=HD)
        o_heads = misc[:, :, :].rearrange("p s (h d) -> p (s h) d", d=VW)
        parts_w = [scratch["q"], scratch["k"]]
        STACK_DMAS = 4 + 4 + 1 + (kind == "cross_pad")
        FIRST, LAST = 4, 14
        STEPS = B + 3

        def steps(engine, step):
            for t in range(FIRST):
                step(t, t % 2)
            with engine.Fori(0, (LAST - FIRST) // 2) as turn:
                for k in range(2):
                    step(turn * 2 + (FIRST + k), k)
            for t in range(LAST, STEPS):
                step(t, t % 2)

        def active(t, lag):
            return not isinstance(t, int) or 0 <= t - lag < B

        def upto(t, lag, n=1):
            if isinstance(t, int):
                return n * max(0, min(B, t - lag + 1))
            return n * (t - lag + 1)

        def row_of(b, s):
            return x_sb[:, bass.ds(b * ST + s, 1), :].squeeze(1)

        def x_at(b):
            return x_sb[:, bass.ds(b * ST, ST), :]

        with nc.Block() as block:
            @block.sync
            def _(sp):
                for name, tile in (("wq", wq), ("wk", wk), ("wv", wv), ("wo", wo)):
                    sp.dma_start(tile[:], w[name].rearrange("(k p) n -> p k n", p=P)).then_inc(loaded, 16)
                if w["bq"] is not None:
                    for name, tile in (("bq", bq), ("bk", bk), ("bv", bv)):
                        with nc.allow_non_contiguous_dma(reason="a bias a partition"):
                            sp.dma_start(tile[:], w[name].rearrange("(k p) -> p k", p=P)).then_inc(loaded, 16)
                    sp.dma_start(bo[:], w["bo"].rearrange("(o n) -> o n", o=1)).then_inc(loaded, 16)
                if kind == "cross_mask":
                    sp.dma_start(mask_u8[:], masks.rearrange("(s p) k -> p s k", p=P)).then_inc(loaded, 16)
                    with nc.allow_non_contiguous_dma(reason="a small mask, transposed"):
                        sp.dma_start(maskT_u8[:], masks.rearrange("q k -> k q")).then_inc(loaded, 16)
                if kind == "cross_pad":
                    sp.dma_start(pad_u8[:], masks).then_inc(loaded, 16)
                    sp.wait_ge(scaled, 3)
                    sp.dma_start(scratch["pad"], pad_f[:]).then_inc(padrow, 16)
                    sp.wait_ge(padrow, 16)
                sp.wait_ge(consts, 1)

                def m_bounce(b, hf, n):
                    wait(sp, m_lo, n + 1)
                    wait(sp, m_hi, n + 1)
                    sp.dma_start(scratch["m"][hf].rearrange("c h t -> h c t"),
                                 m_parts[:].bitcast(F32)).then_inc(m_out, 16)
                    sp.wait_ge(m_out, (n + 1) * 16)
                    return hf

                def step(t, par):
                    a, b, c = t, t - 1, t - 2
                    if active(t, 2):
                        m_bounce(c, 1, 2 * c + 1)
                        sp.dma_start(q_stack[par][64:66, 8:16, :].bitcast(F32), scratch["m"][1])\
                          .then_inc(m_in[1], 16)
                    if active(t, 0):
                        sp.wait_ge(q_lo, a + 1)
                        sp.wait_ge(q_hi, a + 1)
                        for part in range(2):
                            sp.dma_start(parts_w[0][par, part].rearrange("(k p) t -> p k t", p=P),
                                         q_parts[:, part].bitcast(F32)).then_inc(parts_out, 16)
                        sp.wait_ge(k_lo, a + 1)
                        sp.wait_ge(k_hi, a + 1)
                        for part in range(2):
                            sp.dma_start(parts_w[1][par, part].rearrange("(k p) t -> p k t", p=P),
                                         k_parts[:, part].bitcast(F32)).then_inc(parts_out, 16)
                        sp.wait_ge(parts_out, (a + 1) * 64)
                    for hf in range(2):
                        if active(t, 0):
                            if active(t, 2):
                                sp.wait_ge(s2_mm, c * H + 8 * (hf + 1))
                            hs = slice(8 * hf, 8 * hf + 8)
                            fs = slice(P * hf, P * hf + P)
                            sp.dma_start(q_stack[par][64:66, hs, :].bitcast(F32),
                                         q_stack[par][68:70, hs, :].bitcast(F32)).then_inc(stacked[hf], 16)
                            for n in range(4):
                                rows = slice(HD * n, HD * n + HD)
                                sp.dma_start(q_stack[par][rows, hs, :].bitcast(F32),
                                             parts_w[0][par, n % 2, fs].rearrange("(h d) t -> d h t", d=HD))\
                                  .then_inc(stacked[hf], 16)
                                sp.dma_start(k_stack[par][rows, hs, 0:NK].bitcast(F32),
                                             parts_w[1][par, n // 2, fs].rearrange("(h d) t -> d h t", d=HD))\
                                  .then_inc(stacked[hf], 16)
                            if kind == "cross_pad":
                                row = scratch["pad"][bass.ds(a, 1), :] if not isinstance(a, int) else scratch["pad"][a:a + 1, :]
                                sp.dma_start(k_stack[par][66:67, hs, 0:NK].bitcast(F32),
                                             row.unsqueeze(1).to_broadcast([1, 8, S2]))\
                                  .then_inc(stacked[hf], 16)
                        if hf == 0 and active(t, 1):
                            m_bounce(b, 0, 2 * b)
                            sp.dma_start(q_stack[1 - par][64:66, 0:8, :].bitcast(F32), scratch["m"][0])\
                              .then_inc(m_in[0], 16)

                steps(sp, step)

            @block.gpsimd
            def _(pool):
                for i in range(2):
                    nc.gpsimd.memset(q_stack[i][:].bitcast(F32), 0.0)
                    nc.gpsimd.memset(k_stack[i][:].bitcast(F32), 0.0)
                for i in range(2):
                    nc.gpsimd.memset(v_aug[i][:], 0.0)
                nc.gpsimd.memset(ones_row[:], 1.0)
                if cross:
                    nc.gpsimd.memset(prob[:], 0.0)
                if w["bq"] is None:
                    nc.gpsimd.memset(bq[:], 0.0)
                    nc.gpsimd.memset(bk[:], 0.0)
                if kind == "cross_mask":
                    nc.gpsimd.memset(mask1[:], 0.0)
                    nc.gpsimd.memset(mask2[:], 0.0)
                if kind in ("window", "causal"):
                    nc.gpsimd.memset(mask1[:], 0.0)
                    if kind == "causal":
                        nc.gpsimd.memset(mask2[:], 0.0)
                nc.gpsimd.memset(ln["eps"][:], EPS)
                nc.gpsimd.memset(ln["half"][:], -0.5).then_inc(pool_chain, 1)
                pool.wait_ge(pool_chain, 1)
                for i in range(2):
                    last = nc.gpsimd.memset(v_aug[i][0:KROWS, :, :, HD:HD + 1], 1.0)
                last.then_inc(pool_chain, 1)
                pool.wait_ge(pool_chain, 2)
                selects = 0
                if kind == "window":
                    for first, off in ((0, 0), (W1, R)):
                        m = mask1[:, first:first + W1]
                        nc.gpsimd.affine_select(out=m, in_=m, compare_op=ALU.is_ge, fill=MASKED,
                                                base=R - off, pattern=[[1, W1]], channel_multiplier=-1)\
                          .then_inc(pool_chain, 1)
                        selects += 1
                        pool.wait_ge(pool_chain, 2 + selects)
                        nc.gpsimd.affine_select(out=m, in_=m, compare_op=ALU.is_ge, fill=MASKED,
                                                base=R + off, pattern=[[-1, W1]], channel_multiplier=1)\
                          .then_inc(pool_chain, 1)
                        selects += 1
                if kind == "causal":
                    for m, sign in ((mask1, 1), (mask2, -1)):
                        nc.gpsimd.affine_select(out=m[:], in_=m[:], compare_op=ALU.is_ge, fill=MASKED, base=0,
                                                pattern=[[0, 2], [-sign, P]], channel_multiplier=sign)\
                          .then_inc(pool_chain, 1)
                        selects += 1
                pool.wait_ge(pool_chain, 2 + selects)
                pool.sem_inc(consts, 1)

                def layernorm(b, par):
                    pool.wait_ge(stat, b + 1)
                    inverse_deviation(nc, pool, ln, par, pool_chain, 2 + selects + b, scaled_by)

                def add_bias(b):
                    pool.wait_ge(normed, b + 1)
                    pool.wait_ge(bias_done, 1)
                    gate(pool, pool_passed)
                    for s in range(ST):
                        op = nc.gpsimd.tensor_tensor(row_of(b, s), row_of(b, s), out_bias[:], ALU.add)
                    op.then_inc(biased, 1)

                def step(t, par):
                    if cross and active(t, 0):
                        if not isinstance(t, int) or t >= 2:
                            pool.wait_ge(v_mm, t - 1)
                            gate(pool, pool_passed)
                        at = t * S2
                        nc.gpsimd.tensor_copy(ctx_b[par][:], ctxT[:, :, bass.ds(at, S2)]).then_inc(ctx_ready, 1)
                    if w["bq"] is not None and active(t, 0):
                        add_bias(t)
                    if active(t, -1):
                        layernorm(t + 1, 1 - par)
                    if active(t, 0):
                        pool.wait_ge(v_ev, t + 1)
                        if active(t, 2):
                            pool.wait_ge(pv_mm, (t - 1) * H)
                        gate(pool, pool_passed)
                        nc.gpsimd.tensor_copy(v_aug[par][0:KROWS].rearrange("p k h d -> p (k h) d")[:, :, 0:HD],
                                              v_stage[0:KROWS]).then_inc(v_in, 1)

                layernorm(0, 0)
                steps(pool, step)

            @block.vector
            def _(dve):
                dve.wait_ge(loaded, N_LOAD)
                dve.wait_ge(consts, 1)
                for i in range(2):
                    nc.vector.memset(k_stack[i][64:66, :, :].bitcast(F32), 1.0)
                    if kind == "cross_pad":
                        nc.vector.memset(q_stack[i][64:67, :, :].bitcast(F32), 1.0)
                nc.vector.tensor_scalar(wq[:], wq[:], HD ** -0.5, None, ALU.mult)
                if w["bq"] is not None:
                    nc.vector.tensor_scalar(bq[:], bq[:], HD ** -0.5, None, ALU.mult)
                    nc.vector.tensor_copy(bv_wide[:], bv[:].unsqueeze(2).to_broadcast([P, KC, P]))
                if kind == "cross_mask":
                    nc.vector.tensor_scalar(mask1[:].rearrange("p (s k) -> p s k", s=ST)[:, :, 0:S2], mask_u8[:],
                                            -1.0, -MASKED, ALU.add, ALU.mult)
                    nc.vector.tensor_scalar(mask2[0:S2, :], maskT_u8[:], -1.0, -MASKED, ALU.add, ALU.mult)
                nc.vector.memset(recip[:], 0.0).then_inc(scaled, 2)
                dve.wait_ge(scaled, 2)
                if kind == "cross_pad":
                    nc.vector.tensor_scalar(pad_f[:], pad_u8[:], -1.0, -MASKED, ALU.add, ALU.mult).then_inc(scaled, 1)
                if w["bq"] is not None:
                    dve.wait_ge(bias_mm, 1)
                    nc.vector.tensor_copy(out_bias[:], bank(0)[:, 0:D]).then_inc(bias_done, 1)

                def low_part(out, psum, bias, hi, parts_ready, done, batch):
                    dve.wait_ge(parts_ready, batch + 1)
                    if not isinstance(batch, int) or batch >= 1:
                        dve.wait_ge(parts_out, batch * 64)
                    for k in range(KC):
                        op = nc.vector.scalar_tensor_tensor(out[:, k, :], psum[:, k, :], bias[:, k:k + 1],
                                                            hi[:, k, :].bitcast(F32), ALU.add, ALU.subtract)
                    op.then_inc(done, 1)

                def step(t, par):
                    if active(t, 2):
                        m_low_at(t - 2, 1)
                    for g in range(H):
                        if active(t, 1):
                            n = (t - 1) * H + g
                            dve.wait_ge(s1_mm, n + 1)
                            if g == 0 and active(t, 3):
                                dve.wait_ge(m_mm, (t - 3) * 2 + 2)
                            m = m_tok[1 - par]
                            if kind == "causal":
                                nc.vector.reduce_max(m[:, 1, g:g + 1], ps1[:, g % 2, 0:S], AX.X)
                                op = nc.vector.reduce_max(m[:, 0, g:g + 1], ps1[:, g % 2, S:S + P], AX.X)
                            else:
                                wd = direct[1][3]
                                src = ps1[:, g % 2, 0:2 * wd].rearrange("p (s k) -> p s k", s=2)
                                op = nc.vector.reduce_max(m[:, :, g], src[:, :, 0:min(wd, NK)], AX.X)
                            op.then_inc(s1_max, 1)
                        if g == 3 and active(t, 0):
                            low_part(q_parts[:, 1], q_ps, bq, q_parts[:, 0], q_hi, q_lo, t)
                        if g == 5 and active(t, 0):
                            low_part(k_parts[:, 1], k_ps, bk, k_parts[:, 0], k_hi, k_lo, t)
                        if g == 7 and active(t, 0):
                            dve.wait_ge(v_mm, t + 1)
                            if active(t - 1, 0):
                                wait(dve, v_in, t)
                            nc.vector.tensor_copy(v_stage[0:KROWS], v_ps[0:KROWS]).then_inc(v_ev, 1)
                        if g == 9 and active(t, 1):
                            m_low_at(t - 1, 0)
                        if g == 10 and active(t, -1):
                            statistics(nc, dve, ln, 1 - par, row_of, bn, dve_passed, stat, t + 1)
                        if g == 14 and active(t, -1):
                            dve.wait_ge(scaled_by, t + 2)
                            if active(t, 1):
                                dve.wait_ge(xT_mm, t)
                            normalise(nc, ln, 1 - par, row_of, xn[1 - par], normed, t + 1)
                        if g == 12 and active(t, 3):
                            d = t - 3
                            dve.wait_ge(o_mm, d + 1)
                            nc.vector.reciprocal(recip[:].unsqueeze(2), o_heads[:, :, HD:HD + 1]).then_inc(recip_done, 1)
                            dve.wait_ge(recip_done, d + 1)
                            nc.vector.tensor_tensor(o_tok[:].rearrange("p s h d -> p (s h) d"), o_heads[:, :, 0:HD],
                                                    recip[:].unsqueeze(2).to_broadcast([P, ST * H, HD]), ALU.mult)\
                              .then_inc(o_norm, 1)
                    if active(t, 3):
                        d = t - 3
                        if w["bq"] is not None:
                            dve.wait_ge(biased, d + 1)
                        dve.wait_ge(proj_mm, d + 1)
                        nc.vector.tensor_tensor(x_at(d), x_at(d), bank(1).rearrange("p (s n) -> p s n", s=ST), ALU.add)\
                          .then_inc(added, 1)

                def m_low_at(b, hf):
                    n = b * 2 + hf
                    dve.wait_ge(m_hi, n + 1)
                    nc.vector.scalar_tensor_tensor(m_parts[:, 1, :], bank(hf)[0:8, 0:S], -1.0,
                                                   m_parts[:, 0, :].bitcast(F32), ALU.mult, ALU.subtract)\
                      .then_inc(m_lo, 1)

                statistics(nc, dve, ln, 0, row_of, bn, dve_passed, stat, 0)
                dve.wait_ge(scaled_by, 1)
                normalise(nc, ln, 0, row_of, xn[0], normed, 0)
                steps(dve, step)

            @block.scalar
            def _(act):
                def high_part(out, psum, bias, mm, done, batch):
                    act.wait_ge(mm, batch + 1)
                    if not isinstance(batch, int) or batch >= 1:
                        act.wait_ge(parts_out, batch * 64)
                    for k in range(KC):
                        op = nc.scalar.activation(out[:, k, :], psum[:, k, :], ACT.Identity, bias=bias[:, k:k + 1])
                    op.then_inc(done, 1)

                def m_high(b, hf):
                    n = b * 2 + hf
                    act.wait_ge(m_mm, n + 1)
                    wait(act, m_out, n * 16)
                    nc.scalar.activation(m_parts[:, 0, :], bank(hf)[0:8, 0:S], ACT.Copy, scale=-1.0)\
                      .then_inc(m_hi, 1)

                act.wait_ge(scaled, 2)
                act.wait_ge(consts, 1)

                def step(t, par):
                    if active(t, 2):
                        m_high(t - 2, 1)
                    if active(t, 3):
                        d = t - 3
                        act.wait_ge(pv_mm, (d + 1) * H)
                        if active(t, 4):
                            act.wait_ge(o_mm, d)
                        nc.scalar.activation(o_aug[:].rearrange("p i t -> p (i t)"),
                                             pso[:].rearrange("p i t -> p (i t)"), ACT.Copy).then_inc(o_ev, 1)
                    for g in range(H):
                        if active(t, 2):
                            n = (t - 2) * H + g
                            act.wait_ge(s2_mm, n + 1)
                            if not isinstance(t, int) or n >= 4:
                                act.wait_ge(pv_mm, n - 3)
                            nc.scalar.activation(prob[0:KROWS, g % 4, :], ps2[0:KROWS, g % 2, 0:EW], ACT.Exp)\
                              .then_inc(expd, 1)
                        if g == 1 and active(t, 0):
                            act.wait_ge(xT_mm, t + 1)
                            nc.scalar.activation(xT[:], xT_ps, ACT.Copy).then_inc(xT_ev, 1)
                        if g == 3 and active(t, 0):
                            high_part(q_parts[:, 0], q_ps, bq, q_mm, q_hi, t)
                        if g == 5 and active(t, 0):
                            high_part(k_parts[:, 0], k_ps, bk, k_mm, k_hi, t)
                        if g == 9 and active(t, 1):
                            m_high(t - 1, 0)
                        if g == 13 and active(t, 3):
                            act.wait_ge(oT_mm, t - 2)
                            nc.scalar.activation(oT[:], xT_ps, ACT.Copy).then_inc(oT_ev, 1)

                steps(act, step)

            @block.tensor
            def _(pe):
                pe.wait_ge(scaled, 2)
                pe.wait_ge(consts, 1)
                if w["bq"] is not None:
                    for k in range(KC):
                        nc.tensor.matmul(bank(0)[:, 0:D], bv_wide[:, k, :], wo[:, k, :], start=(k == 0), stop=False)
                    nc.tensor.matmul(bank(0)[:, 0:D], ones_row[:], bo[:], start=False, stop=True).then_inc(bias_mm, 1)
                    pe.wait_ge(bias_done, 1)

                def scores(b, par, g):
                    n = b * H + g
                    if g % 8 == 0:
                        pe.wait_ge(stacked[g // 8], (b + 1) * 16 * STACK_DMAS)
                    if not (isinstance(b, int) and n < 2):
                        pe.wait_ge(s1_max, n - 1)
                    dst = ps1[:, g % 2, :]
                    if mask_n:
                        at = mask_at[0]
                        nc.tensor.matmul(dst[:, at:at + mask1.shape[1]], ident_bf[:], mask1[:], start=True, stop=False,
                                         skip_group_check=True)
                    for i, (qt, k0, nk, col) in enumerate(direct):
                        op = nc.tensor.matmul(dst[:, col:col + nk], q_stack[par][:, g, qt * P:qt * P + P],
                                              k_stack[par][:, g, k0:k0 + nk], start=(not mask_n), stop=True,
                                              skip_group_check=True)
                    op.then_inc(s1_mm, 1)

                def shifted(c, par, g):
                    n = c * H + g
                    if g % 8 == 0:
                        pe.wait_ge(m_in[g // 8], (c + 1) * 16)
                    if not (isinstance(c, int) and n < 2):
                        pe.wait_ge(expd, n - 1)
                    dst = ps2[:, g % 2, :]
                    if mask_n:
                        at = mask_at[1]
                        nc.tensor.matmul(dst[0:KROWS, at:at + mask2.shape[1]], ident_bf[:, 0:KROWS], mask2[:],
                                         start=True, stop=False, skip_group_check=True)
                    for i, (kt, q0, nq, col) in enumerate(transposed):
                        op = nc.tensor.matmul(dst[0:KROWS, col:col + nq],
                                              k_stack[par][:, g, kt * P:kt * P + KROWS],
                                              q_stack[par][:, g, q0:q0 + nq], start=(not mask_n), stop=True,
                                              skip_group_check=True)
                    op.then_inc(s2_mm, 1)

                def pv(c, par, g):
                    n = c * H + g
                    pe.wait_ge(expd, n + 1)
                    if g == 0:
                        pe.wait_ge(v_in, c + 1)
                        if not isinstance(c, int) or c >= 1:
                            pe.wait_ge(o_ev, c)
                    i, j = g // 4, g % 4
                    dst = pso[32 * j:32 * j + 32, i // 2, (i % 2) * S:(i % 2) * S + S]
                    order = sorted(transposed)
                    for m, (kt, q0, nq, col) in enumerate(order):
                        op = nc.tensor.matmul(dst[:, q0:q0 + nq], v_at(c, par)[:, kt, g, :], prob[:, g % 4, col:col + nq],
                                              start=(m == 0), stop=(m == len(order) - 1), skip_group_check=True)
                    op.then_inc(pv_mm, 1)

                def v_at(c, par):
                    return v_aug[par]

                def max_out(b, par, hf):
                    pe.wait_ge(s1_max, b * H + 8 * (hf + 1))
                    for s in range(ST):
                        op = nc.tensor.transpose(bank(hf)[0:8, s * P:s * P + P], m_tok[par][:, s, 8 * hf:8 * hf + 8],
                                                 ident[:])
                    op.then_inc(m_mm, 1)

                def step(t, par):
                    a, b, c, d = t, t - 1, t - 2, t - 3
                    if active(t, 2):
                        wait(pe, added, upto(t - 1, 3))
                        wait(pe, v_ev, upto(t - 1, 0))
                        max_out(c, par, 1)
                    for g in range(H):
                        if active(t, 1):
                            scores(b, 1 - par, g)
                        if active(t, 2):
                            if g >= 1:
                                pv(c, par, g - 1)
                            shifted(c, par, g)
                        if g == 1 and active(t, 0):
                            pe.wait_ge(normed, a + 1)
                            wait(pe, oT_ev, upto(t - 1, 3))
                            wait(pe, m_lo, upto(t - 1, 1, 2) - 1)
                            for k in range(KC):
                                for s in range(ST):
                                    op = nc.tensor.transpose(xT_ps[:, k, s * P:s * P + P],
                                                             xn[par][:, s, k * P:k * P + P], ident[:])
                            op.then_inc(xT_mm, 1)
                        if g == 2 and active(t, 0):
                            pe.wait_ge(xT_ev, a + 1)
                            wait(pe, m_lo, upto(t, 2, 2))
                            wait(pe, v_ev, upto(t - 1, 0))
                            for f in range(KC):
                                for k in range(KC):
                                    op = nc.tensor.matmul(q_ps[:, f, :], wq[:, k, f * P:f * P + P], xT[:, k, :],
                                                          start=(k == 0), stop=(k == KC - 1))
                            op.then_inc(q_mm, 1)
                        if g == 4 and active(t, 0):
                            if cross:
                                pe.wait_ge(ctx_ready, a + 1)
                            for f in range(KC):
                                for k in range(KC):
                                    rhs = ctx_b[par][:, k, :] if cross else xT[:, k, :]
                                    op = nc.tensor.matmul(k_ps[:, f, :], wk[:, k, f * P:f * P + P], rhs,
                                                          start=(k == 0), stop=(k == KC - 1))
                            op.then_inc(k_mm, 1)
                        if g == 6 and active(t, 0):
                            pe.wait_ge(q_lo, a + 1)
                            for s in range(KTILES):
                                for k in range(KC):
                                    lhs = ctx_b[par][:, k, :] if cross else xT[:, k, s * P:s * P + P]
                                    op = nc.tensor.matmul(bank(1)[0:KROWS, s * D:s * D + D], lhs, wv[:, k, :],
                                                          start=(k == 0), stop=(k == KC - 1))
                            op.then_inc(v_mm, 1)
                        if g == 8 and active(t, 1):
                            wait(pe, k_lo, upto(t, 0))
                            wait(pe, oT_ev, upto(t - 1, 3))
                            max_out(b, 1 - par, 0)
                        if g == 10 and active(t, 3):
                            pe.wait_ge(o_ev, d + 1)
                            wait(pe, m_lo, upto(t, 1, 2) - (1 if active(t, 1) else 0))
                            wait(pe, v_ev, upto(t, 0))
                            wait(pe, added, upto(t - 1, 3))
                            wait(pe, oT_ev, upto(t - 1, 3))
                            for s in range(ST):
                                for i in range(4):
                                    op = nc.tensor.transpose(bank(s)[:, i * P:i * P + P], o_aug[:, i, s * P:s * P + P],
                                                             ident[:])
                            op.then_inc(o_mm, 1)
                        if g == 12 and active(t, 3):
                            pe.wait_ge(o_norm, d + 1)
                            of = o_tok[:].rearrange("p s h d -> p s (h d)")
                            for k in range(KC):
                                for s in range(ST):
                                    op = nc.tensor.transpose(xT_ps[:, k, s * P:s * P + P], of[:, s, k * P:k * P + P],
                                                             ident[:])
                            op.then_inc(oT_mm, 1)
                        if g == 14 and active(t, 3):
                            pe.wait_ge(oT_ev, d + 1)
                            for s in range(ST):
                                for k in range(KC):
                                    op = nc.tensor.matmul(bank(1)[:, s * D:s * D + D], oT[:, k, s * P:s * P + P],
                                                          wo[:, k, :], start=(k == 0), stop=(k == KC - 1))
                            op.then_inc(proj_mm, 1)
                    if active(t, 2):
                        pv(c, par, H - 1)

                steps(pe, step)


def context_columns(nc, tag, ctx_dram, ctxT, ident):
    ROWS = B * S2
    NT = (ROWS + P - 1) // P
    with ExitStack() as ctx:
        rows = ctx.enter_context(nc.sbuf_tensor(f"{tag}_ctx_rows", [P, NT, D], F32))
        ps = ctx.enter_context(nc.psum_tensor(f"{tag}_ctx_ps", [P, 2, 512], F32))
        sem = ctx.enter_context(semaphores(nc, f"{tag}_ctx"))
        loaded, turned, copied = sem("loaded"), sem("turned"), sem("copied")
        last = ROWS - (NT - 1) * P
        with nc.Block() as block:
            @block.sync
            def _(sp):
                sp.dma_start(rows[:, 0:NT - 1, :], ctx_dram[0:(NT - 1) * P, :].rearrange("(t p) d -> p t d", p=P))\
                  .then_inc(loaded, 16)
                sp.dma_start(rows[0:last, NT - 1, :], ctx_dram[(NT - 1) * P:ROWS, :]).then_inc(loaded, 16)

            @block.tensor
            def _(pe):
                pe.wait_ge(loaded, 32)
                for t in range(NT):
                    n = min(P, ROWS - t * P)
                    if t >= 2:
                        pe.wait_ge(copied, t - 1)
                    for k in range(KC):
                        op = nc.tensor.transpose(ps[:, t % 2, k * P:k * P + n], rows[0:n, t, k * P:k * P + P], ident[0:n, 0:n])
                    op.then_inc(turned, 1)

            @block.vector
            def _(dve):
                for t in range(NT):
                    n = min(P, ROWS - t * P)
                    dve.wait_ge(turned, t + 1)
                    nc.vector.tensor_copy(ctxT[:, :, t * P:t * P + n], ps[:, t % 2, 0:D].rearrange("p (k t) -> p k t", k=KC)[:, :, 0:n]).then_inc(copied, 1)


NE, FH = 8, 512
FB = FH // P
TM = 256
TS = TM // P
PAIRS = 2 * B * S
MT = PAIRS // TM + NE
W1_AT = 0
W2_AT = W1_AT + KC * FH
W3_AT = W2_AT + FB * FH
B1_AT = W3_AT + FB * D
B2_AT = B1_AT + FB
B3_AT = B2_AT + FB
WPACK = B3_AT + D
ROUND = 1.5 * 2.0 ** 23


def experts(nc, a, x_sb, ident, slots_dram, y_dram, zero_filled):
    with ExitStack() as ctx:
        def sb(name, shape, dt):
            return ctx.enter_context(nc.sbuf_tensor(f"moe_{name}", shape, dt))

        sem = ctx.enter_context(semaphores(nc, "moe"))

        pos = sb("pos", [P, TILES, 2], U32)
        gate2 = sb("gate2", [P, TILES, 8], F32)
        tile_expert = sb("tile_expert", [P, MT], I32)

        with ExitStack() as inner:
            def isb(name, shape, dt):
                return inner.enter_context(nc.sbuf_tensor(f"moe_{name}", shape, dt))

            xn = isb("xn", [P, TILES, D], F32)
            gw = isb("gw", [P, KC, NE], F32)
            gb = isb("gb", [P, NE], F32)
            ones = isb("ones", [P, P], F32)
            before = isb("before", [P, P], F32)
            iota_e = isb("iota_e", [P, NE], F32)
            iota_t = isb("iota_t", [P, MT], F32)
            ln = layernorm_tiles(isb)
            xb = [isb(f"xb{i}", [P, ST, D], F32) for i in range(2)]
            xT = [isb(f"xT{i}", [P, KC, S], F32) for i in range(2)]
            g = isb("g", [P, TILES, NE], F32)
            red = isb("red", [P, TILES], F32)
            best = isb("best", [P, TILES, 8], U32)
            best_f = isb("best_f", [P, TILES, 2], F32)
            hot = isb("hot", [P, 2, TILES, NE], F32)
            both = isb("both", [P, TILES, NE], F32)
            total = isb("total", [P, TILES, NE], F32)
            upto_t = isb("upto_t", [P, TILES, NE], F32)
            slot = isb("slot", [P, TILES, NE], F32)
            n_tiles = isb("n_tiles", [P, NE], F32)
            end_tile = isb("end_tile", [P, NE], F32)
            start_tile = isb("start_tile", [P, NE], F32)
            te = isb("te", [P, MT], F32)
            pos_f = isb("pos_f", [P, TILES, 2], F32)
            turned_ps = inner.enter_context(nc.psum_tensor("moe_turned_ps", [P, 2, 512], F32))
            logit_ps = inner.enter_context(nc.psum_tensor("moe_logit_ps", [P, 512], F32))
            rank_ps = inner.enter_context(nc.psum_tensor("moe_rank_ps", [P, 2, 512], F32))
            loaded, consts, stat, bn, chain, normed, turned, copied, logits, dchain, expd, hot_done, ranked, placed, sent = (
                sem(n) for n in ("loaded", "consts", "stat", "bn", "chain", "normed", "turned", "copied", "logits",
                                 "dchain", "expd", "hot_done", "ranked", "placed", "sent"))
            kept, factors, dve_passed = sem("kept"), sem("factors"), sem("dve_passed")

            row_of = lambda b, s: x_sb[:, bass.ds(b * ST + s, 1), :].squeeze(1)

            with nc.Block() as block:
                @block.sync
                def _(sp):
                    with nc.allow_non_contiguous_dma(reason="eight columns"):
                        sp.dma_start(gw[:], a["L0_ffn_gate_w"].rearrange("(k p) e -> p k e", p=P)).then_inc(loaded, 16)
                        sp.dma_start(gb[:], a["L0_ffn_gate_b"].rearrange("(o e) -> o e", o=1).to_broadcast([P, NE]))\
                          .then_inc(loaded, 16)

                @block.gpsimd
                def _(pool):
                    nc.gpsimd.memset(ln["eps"][:], EPS)
                    nc.gpsimd.memset(ln["half"][:], -0.5)
                    nc.gpsimd.memset(ones[:], 1.0)
                    nc.gpsimd.iota(iota_e[:], pattern=[[1, NE]], base=0, channel_multiplier=0,
                                   allow_small_or_imprecise_dtypes=True)
                    nc.gpsimd.iota(iota_t[:], pattern=[[1, MT]], base=0, channel_multiplier=0,
                                   allow_small_or_imprecise_dtypes=True)
                    nc.gpsimd.memset(before[:], 1.0).then_inc(chain, 1)
                    pool.wait_ge(chain, 1)
                    nc.gpsimd.affine_select(out=before[:], in_=before[:], compare_op=ALU.is_gt, fill=0.0, base=0,
                                            pattern=[[1, P]], channel_multiplier=-1).then_inc(consts, 1)
                    with pool.Fori(0, B // 2) as turn:
                        for par in range(2):
                            b = turn * 2 + par
                            pool.wait_ge(stat, b + 1)
                            inverse_deviation(nc, pool, ln, par, chain, b + 1, factors)
                    pool.wait_ge(placed, 1)
                    pool.wait_ge(kept, B)
                    pool.wait_ge(zero_filled[0], zero_filled[1])
                    for t in range(TILES):
                        for k in range(2):
                            nc.gpsimd.indirect_dma_start(
                                out=slots_dram, out_offset=bass.IndirectOffsetOnAxis(ap=pos[:, t, k:k + 1], axis=0),
                                in_=xn[:, t, :], in_offset=None).then_inc(sent, 16)
                    pool.wait_ge(sent, 16 * 2 * TILES)

                @block.tensor
                def _(pe):
                    pe.wait_ge(loaded, 32)
                    with pe.Fori(0, B // 2) as turn:
                        for par in range(2):
                            b = turn * 2 + par
                            pe.wait_ge(normed, b + 1)
                            rows = xb[par]
                            for k in range(KC):
                                for s in range(ST):
                                    op = nc.tensor.transpose(turned_ps[:, par, k * S + s * P:k * S + s * P + P],
                                                             rows[:, s, k * P:k * P + P], ident[:])
                            op.then_inc(turned, 1)
                            pe.wait_ge(copied, b + 1)
                            for s in range(ST):
                                for k in range(KC):
                                    op = nc.tensor.matmul(logit_ps[:, bass.ds(b * (ST * NE) + s * NE, NE)],
                                                          xT[par][:, k, s * P:s * P + P], gw[:, k, :],
                                                          start=(k == 0), stop=(k == KC - 1))
                            op.then_inc(logits, 1)
                    pe.wait_ge(hot_done, 1)
                    pe.wait_ge(consts, 1)
                    flat = both[:].rearrange("p t e -> p (t e)")
                    nc.tensor.matmul(rank_ps[:, 0, 0:TILES * NE], before[:], flat, start=True, stop=True)
                    nc.tensor.matmul(rank_ps[:, 1, 0:TILES * NE], ones[:], flat, start=True, stop=True)\
                      .then_inc(ranked, 1)

                @block.scalar
                def _(act):
                    with act.Fori(0, B // 2) as turn:
                        for par in range(2):
                            b = turn * 2 + par
                            act.wait_ge(normed, b + 1)
                            nc.scalar.activation(xn[:, bass.ds(b * ST, ST), :], xb[par][:], ACT.Copy).then_inc(kept, 1)
                            act.wait_ge(turned, b + 1)
                            nc.scalar.activation(xT[par][:].rearrange("p k t -> p (k t)"), turned_ps[:, par, :], ACT.Copy)\
                              .then_inc(copied, 1)
                    act.wait_ge(dchain, EXP_AT)
                    nc.scalar.activation(g[:], g[:], ACT.Exp).then_inc(expd, 1)

                @block.vector
                def _(dve):
                    def rows_normed(b, par, more):
                        if more:
                            statistics(nc, dve, ln, 1 - par, row_of, bn, dve_passed, stat, b + 1)
                        dve.wait_ge(factors, b + 1)
                        if not isinstance(b, int) or b >= 2:
                            dve.wait_ge(kept, b - 1)
                            dve.wait_ge(copied, b - 1)
                        normalise(nc, ln, par, row_of, xb[par], normed, b)

                    statistics(nc, dve, ln, 0, row_of, bn, dve_passed, stat, 0)
                    rows_normed(0, 0, True)
                    rows_normed(1, 1, True)
                    with dve.Fori(0, (B - 4) // 2) as turn:
                        for par in range(2):
                            rows_normed(turn * 2 + (2 + par), par, True)
                    rows_normed(B - 2, 0, True)
                    rows_normed(B - 1, 1, False)
                    count = [0]

                    def link(op):
                        count[0] += 1
                        op.then_inc(dchain, 1)
                        dve.wait_ge(dchain, count[0])

                    wide = lambda m: m[:].unsqueeze(2).to_broadcast([P, TILES, NE])
                    dve.wait_ge(logits, B)
                    dve.wait_ge(loaded, 32)
                    dve.wait_ge(consts, 1)
                    link(nc.vector.tensor_tensor(g[:], logit_ps[:, 0:TILES * NE].rearrange("p (t e) -> p t e", e=NE),
                                                 gb[:].unsqueeze(1).to_broadcast([P, TILES, NE]), ALU.add))
                    link(nc.vector.reduce_max(red[:], g[:], AX.X))
                    link(nc.vector.tensor_tensor(g[:], g[:], wide(red), ALU.subtract))
                    assert count[0] == EXP_AT
                    dve.wait_ge(expd, 1)
                    link(nc.vector.reduce_sum(red[:], g[:], AX.X))
                    link(nc.vector.reciprocal(red[:], red[:]))
                    link(nc.vector.tensor_tensor(g[:], g[:], wide(red), ALU.mult))
                    for t in range(TILES):
                        op = nc.vector.max(gate2[:, t, :], g[:, t, :])
                    link(op)
                    for t in range(TILES):
                        op = nc.vector.max_index(best[:, t, :], gate2[:, t, :], g[:, t, :])
                    link(op)
                    link(nc.vector.tensor_copy(best_f[:], best[:, :, 0:2]))
                    for k in range(2):
                        op = nc.vector.tensor_tensor(hot[:, k], iota_e[:].unsqueeze(1).to_broadcast([P, TILES, NE]),
                                                     best_f[:, :, k:k + 1].to_broadcast([P, TILES, NE]), ALU.is_equal)
                    link(op)
                    nc.vector.tensor_tensor(both[:], hot[:, 0], hot[:, 1], ALU.add).then_inc(hot_done, 1)
                    dve.wait_ge(ranked, 1)
                    in_bank = lambda k: rank_ps[:, k, 0:TILES * NE].rearrange("p (t e) -> p t e", e=NE)
                    link(nc.vector.tensor_copy(total[:], in_bank(1)))
                    for e in range(NE):
                        op = nc.vector.tensor_tensor_scan(upto_t[:, :, e], ones[:, 0:TILES], total[:, :, e], 0.0,
                                                          ALU.mult, ALU.add)
                    link(op)
                    link(nc.vector.tensor_scalar(n_tiles[:], upto_t[:, TILES - 1, :], 1.0 / TM, (TM - 1) / 2.0 / TM,
                                                 ALU.mult, ALU.add))
                    link(nc.vector.tensor_scalar(n_tiles[:], n_tiles[:], ROUND, -ROUND, ALU.add, ALU.add))
                    link(nc.vector.tensor_tensor_scan(end_tile[:], ones[:, 0:NE], n_tiles[:], 0.0, ALU.mult, ALU.add))
                    link(nc.vector.tensor_tensor(start_tile[:], end_tile[:], n_tiles[:], ALU.subtract))
                    link(nc.vector.tensor_tensor(slot[:], upto_t[:], total[:], ALU.subtract))
                    link(nc.vector.tensor_tensor(slot[:], slot[:], in_bank(0), ALU.add))
                    link(nc.vector.scalar_tensor_tensor(slot[:], start_tile[:].unsqueeze(1).to_broadcast([P, TILES, NE]),
                                                        float(TM), slot[:], ALU.mult, ALU.add))
                    for k in range(2):
                        op = nc.vector.tensor_tensor(hot[:, k], hot[:, k], slot[:], ALU.mult)
                    link(op)
                    for k in range(2):
                        op = nc.vector.reduce_sum(pos_f[:, :, k], hot[:, k], AX.X)
                    link(op)
                    nc.vector.tensor_copy(pos[:], pos_f[:]).then_inc(placed, 1)
                    link(nc.vector.tensor_scalar(te[:], iota_t[:], start_tile[:, 1:2], None, ALU.is_ge))
                    for e in range(2, NE):
                        link(nc.vector.scalar_tensor_tensor(te[:], iota_t[:], start_tile[:, e:e + 1], te[:],
                                                            ALU.is_ge, ALU.add))
                    nc.vector.tensor_copy(tile_expert[:], te[:])

        with ExitStack() as inner:
            def isb(name, shape, dt):
                return inner.enter_context(nc.sbuf_tensor(f"moe_{name}", shape, dt))

            def ipb(name, banks):
                return inner.enter_context(nc.psum_tensor(f"moe_{name}", [P, banks, 512], F32))

            weights = [isb(f"weights{i}", [P, WPACK], F32) for i in range(2)]
            rows = [isb(f"rows{i}", [P, TS, D], F32) for i in range(2)]
            rowsT = isb("rowsT", [P, KC, TM], F32)
            h1 = isb("h1", [P, FB, TM], F32)
            h2 = isb("h2", [P, FB, TM], F32)
            y = [isb(f"y{i}", [P, TS, D], F32) for i in range(2)]
            turned_ps = ipb("rows_ps", 1)
            h1_ps = ipb("h1_ps", 2)
            h2_ps = ipb("h2_ps", 2)
            y_ps = ipb("y_ps", 2)
            w_in = [sem(f"w_in{i}") for i in range(2)]
            turned, copied, l1, act1, l2, act2, l3, y_done = (
                sem(n) for n in ("t_turned", "t_copied", "l1", "act1", "l2", "act2", "l3", "y_done"))
            y_out = [sem(f"y_out{i}") for i in range(2)]

            def views(w):
                return (w[:, W1_AT:W2_AT].rearrange("p (k f) -> p k f", k=KC),
                        w[:, W2_AT:W3_AT].rearrange("p (k f) -> p k f", k=FB),
                        w[:, W3_AT:B1_AT].rearrange("p (k f) -> p k f", k=FB),
                        w[:, B1_AT:B2_AT], w[:, B2_AT:B3_AT], w[:, B3_AT:WPACK])

            def tiles(engine, tile):
                tile(0, 0)
                tile(1, 1)
                with engine.Fori(0, (MT - 4) // 2) as turn:
                    for k in range(2):
                        tile(turn * 2 + (2 + k), k)
                tile(MT - 2, 0)
                tile(MT - 1, 1)

            later = lambda j, n: not isinstance(j, int) or j >= n

            with nc.Block() as block:
                @block.sync
                def _(sp):
                    def tile(j, par):
                        if later(j, 2):
                            sp.wait_ge(y_done, j - 1)
                        e = sp.value_load(tile_expert[0:1, bass.ds(j, 1)], min_val=0, max_val=NE - 1)
                        sp.dma_start(weights[par][:], a["moe_w"][bass.ds(e, 1)].squeeze(0)).then_inc(w_in[par], 16)
                        sp.dma_start(rows[par][:], slots_dram[bass.ds(j * TM, TM), :].rearrange("(s p) d -> p s d", p=P))\
                          .then_inc(w_in[par], 16)

                    tiles(sp, tile)

                @block.gpsimd
                def _(pool):
                    def tile(j, par):
                        pool.wait_ge(y_done, j + 1)
                        pool.dma_start(y_dram[bass.ds(j * TM, TM), :].rearrange("(s p) d -> p s d", p=P), y[par][:])\
                            .then_inc(y_out[par], 16)

                    tiles(pool, tile)
                    for i in range(2):
                        pool.wait_ge(y_out[i], 8 * MT)

                @block.tensor
                def _(pe):
                    def layer1(j, par):
                        w1 = views(weights[par])[0]
                        pe.wait_ge(w_in[par], (j // 2 + 1) * 32 if isinstance(j, int) else (j - par) * 16 + 32)
                        for k in range(KC):
                            for s in range(TS):
                                op = nc.tensor.transpose(turned_ps[:, 0, k * TM + s * P:k * TM + s * P + P],
                                                         rows[par][:, s, k * P:k * P + P], ident[:])
                        op.then_inc(turned, 1)

                    def layer1_products(j, par):
                        w1 = views(weights[par])[0]
                        pe.wait_ge(copied, j + 1)
                        for f in range(FB):
                            for k in range(KC):
                                op = nc.tensor.matmul(h1_ps[:, f // 2, (f % 2) * TM:(f % 2) * TM + TM],
                                                      w1[:, k, f * P:f * P + P], rowsT[:, k, :],
                                                      start=(k == 0), stop=(k == KC - 1))
                            op.then_inc(l1, 1)

                    def tile(j, par):
                        _, w2, w3, _, _, _ = views(weights[par])
                        more = not isinstance(j, int) or j + 1 < MT
                        if isinstance(j, int) and j == 0:
                            layer1(0, 0)
                            layer1_products(0, 0)
                        if more:
                            layer1(j + 1, 1 - par)
                        pe.wait_ge(act1, FB * (j + 1))
                        for f in range(FB):
                            for k in range(FB):
                                op = nc.tensor.matmul(h2_ps[:, f // 2, (f % 2) * TM:(f % 2) * TM + TM],
                                                      w2[:, k, f * P:f * P + P], h1[:, k, :],
                                                      start=(k == 0), stop=(k == FB - 1))
                            op.then_inc(l2, 1)
                        if more:
                            layer1_products(j + 1, 1 - par)
                        pe.wait_ge(act2, FB * (j + 1))
                        if later(j, 2):
                            pe.wait_ge(y_done, j - 1)
                        for s in range(TS):
                            for k in range(FB):
                                op = nc.tensor.matmul(y_ps[:, par, s * D:s * D + D], h2[:, k, s * P:s * P + P],
                                                      w3[:, k, :], start=(k == 0), stop=(k == FB - 1))
                        op.then_inc(l3, 1)

                    tiles(pe, tile)

                @block.scalar
                def _(act):
                    def gelu(j, out, psum, bias, mm, done):
                        for f in range(FB):
                            act.wait_ge(mm, FB * j + (f // 2 * 2 + 2))
                            nc.scalar.activation(out[:, f, :], psum[:, f // 2, (f % 2) * TM:(f % 2) * TM + TM],
                                                 ACT.Gelu, bias=bias[:, f:f + 1]).then_inc(done, 1)

                    def tile(j, par):
                        more = not isinstance(j, int) or j + 1 < MT
                        if isinstance(j, int) and j == 0:
                            gelu(0, h1, h1_ps, views(weights[0])[3], l1, act1)
                        gelu(j, h2, h2_ps, views(weights[par])[4], l2, act2)
                        if more:
                            gelu(j + 1, h1, h1_ps, views(weights[1 - par])[3], l1, act1)

                    tiles(act, tile)

                @block.vector
                def _(dve):
                    def columns(j):
                        dve.wait_ge(turned, j + 1)
                        nc.vector.tensor_copy(rowsT[:].rearrange("p k t -> p (k t)"), turned_ps[:, 0, :]).then_inc(copied, 1)

                    def tile(j, par):
                        if isinstance(j, int) and j == 0:
                            columns(0)
                        if not isinstance(j, int) or j + 1 < MT:
                            columns(j + 1)
                        dve.wait_ge(l3, j + 1)
                        if later(j, 2):
                            dve.wait_ge(y_out[par], (j - par) * 8)
                        b3 = views(weights[par])[5]
                        nc.vector.tensor_tensor(y[par][:], y_ps[:, par, :].rearrange("p (s d) -> p s d", s=TS),
                                                b3.unsqueeze(1).to_broadcast([P, TS, D]), ALU.add).then_inc(y_done, 1)

                    tiles(dve, tile)

        with ExitStack() as inner:
            RING = 8
            got = [inner.enter_context(nc.sbuf_tensor(f"moe_got{i}", [P, D], F32)) for i in range(RING)]
            here = [sem(f"here{i}") for i in range(RING)]
            summed = sem("summed")
            with nc.Block() as block:
                @block.gpsimd
                def _(pool):
                    for n in range(2 * TILES):
                        if n >= RING:
                            pool.wait_ge(summed, n - RING + 1)
                        nc.gpsimd.indirect_dma_start(
                            out=got[n % RING][:], out_offset=None, in_=y_dram,
                            in_offset=bass.IndirectOffsetOnAxis(ap=pos[:, n // 2, n % 2:n % 2 + 1], axis=0))\
                            .then_inc(here[n % RING], 16)

                @block.vector
                def _(dve):
                    for n in range(2 * TILES):
                        t, k = n // 2, n % 2
                        dve.wait_ge(here[n % RING], 16 * (n // RING + 1))
                        if n >= 1:
                            dve.wait_ge(summed, n)
                        nc.vector.scalar_tensor_tensor(x_sb[:, t, :], got[n % RING][:], gate2[:, t, k:k + 1],
                                                       x_sb[:, t, :], ALU.mult, ALU.add).then_inc(summed, 1)


EXP_AT = 3


FI = 768
IB = FI // P
TOK = B * S
CH = 512
NCH = TOK // CH
QBLOCK = 32
QMAX = 32767.0
LEAST = 1e-12


def quantised_ffn(nc, a, ident, x_dram, out_dram):
    with ExitStack() as ctx:
        def sb(name, shape, dt):
            return ctx.enter_context(nc.sbuf_tensor(f"ffn_{name}", shape, dt))

        sem = ctx.enter_context(semaphores(nc, "ffn"))

        xT = sb("xT", [P, KC, TOK], F32)
        w_gate = sb("w_gate", [P, KC, FI], F32)
        w_up = sb("w_up", [P, KC, FI], F32)
        w_down = sb("w_down", [P, IB, D], F32)
        peak = sb("peak", [P, NCH * IB * 2], F32)
        top = sb("top", [P, 1], F32)
        whole = sb("whole", [P, 1], F32)
        scales = sb("scales", [P, 5], F32)
        inverse = sb("inverse", [P, 5], F32)
        both_scales = sb("both_scales", [P, 1], F32)
        X_, GATE, GATED, UP, PROD = range(5)
        RMAX = bass.bass_isa.ReduceOp.max

        with ExitStack() as inner:
            def isb(name, shape, dt):
                return inner.enter_context(nc.sbuf_tensor(f"ffn_{name}", shape, dt))

            NB = FI // P * D // QBLOCK
            raw = isb("raw", [P, 3, FI // P * D], F32)
            wmax = isb("wmax", [P, 3 * NB], F32)
            wscale = isb("wscale", [P, 3 * NB], F32)
            winv = isb("winv", [P, 3 * NB], F32)
            xin = [isb(f"xin{i}", [P, ST, D], F32) for i in range(2)]
            xn = [isb(f"xn{i}", [P, ST, D], F32) for i in range(2)]
            ln = layernorm_tiles(isb)
            w_ps = inner.enter_context(nc.psum_tensor("ffn_w_ps", [P, 2, 512], F32))
            x_ps = inner.enter_context(nc.psum_tensor("ffn_x_ps", [P, 2, 512], F32))
            w_in, dchain, quantised, w_turned, w_kept, chain, bn, stat, normed, turned, kept, peaked = (
                sem(n) for n in ("w_in", "dchain", "quantised", "w_turned", "w_kept", "chain", "bn", "stat", "normed",
                                 "turned", "kept", "peaked"))
            x_in = [sem(f"x_in{i}") for i in range(2)]
            factors, dve_passed = sem("factors"), sem("dve_passed")
            rows_in = [lambda b, s: xin[0][:, s, :], lambda b, s: xin[1][:, s, :]]
            NTURN = 3 * FI // P * D // P // 4

            def turned_block(n):
                m, r = n // (IB * KC), n % (IB * KC)
                if m < 2:
                    f, k = r // KC, r % KC
                    return raw[:, m, f * D + k * P:f * D + k * P + P], (w_gate, w_up)[m][:, k, f * P:f * P + P]
                o, k = r // IB, r % IB
                return raw[:, 2, o * FI + k * P:o * FI + k * P + P], w_down[:, k, o * P:o * P + P]

            with nc.Block() as block:
                @block.sync
                def _(sp):
                    sp.dma_start(raw[:, 0, :].rearrange("p (f n) -> p f n", n=D),
                                 a["L1_ffn_w_gate"].rearrange("(f p) n -> p f n", p=P)).then_inc(w_in, 16)
                    sp.dma_start(raw[:, 1, :].rearrange("p (f n) -> p f n", n=D),
                                 a["L1_ffn_w_up"].rearrange("(f p) n -> p f n", p=P)).then_inc(w_in, 16)
                    sp.dma_start(raw[:, 2, :].rearrange("p (f n) -> p f n", n=FI),
                                 a["L1_ffn_w_down"].rearrange("(f p) n -> p f n", p=P)).then_inc(w_in, 16)

                    def load(b, par):
                        sp.dma_start(xin[par][:], x_dram[bass.ds(b * S, S), :].rearrange("(s p) d -> p s d", p=P))\
                          .then_inc(x_in[par], 16)

                    load(0, 0)
                    load(1, 1)
                    with sp.Fori(0, (B - 2) // 2) as turn:
                        for par in range(2):
                            b = turn * 2 + (2 + par)
                            sp.wait_ge(normed, b - 1)
                            load(b, par)

                @block.gpsimd
                def _(pool):
                    nc.gpsimd.memset(ln["eps"][:], EPS)
                    nc.gpsimd.memset(ln["half"][:], -0.5).then_inc(chain, 1)
                    pool.wait_ge(chain, 1)
                    with pool.Fori(0, B // 2) as turn:
                        for par in range(2):
                            b = turn * 2 + par
                            pool.wait_ge(stat, b + 1)
                            inverse_deviation(nc, pool, ln, par, chain, b + 1, factors)

                @block.tensor
                def _(pe):
                    with pe.Fori(0, B // 2) as turn:
                        for par in range(2):
                            b = turn * 2 + par
                            pe.wait_ge(normed, b + 1)
                            for k in range(KC):
                                for s in range(ST):
                                    op = nc.tensor.transpose(x_ps[:, par, k * S + s * P:k * S + s * P + P],
                                                             xn[par][:, s, k * P:k * P + P], ident[:])
                            op.then_inc(turned, 1)
                    pe.wait_ge(quantised, 1)
                    for n in range(NTURN):
                        if n >= 2:
                            pe.wait_ge(w_kept, n - 1)
                        for q in range(4):
                            op = nc.tensor.transpose(w_ps[:, n % 2, q * P:q * P + P], turned_block(4 * n + q)[0], ident[:])
                        op.then_inc(w_turned, 1)

                @block.scalar
                def _(act):
                    with act.Fori(0, B // 2) as turn:
                        for par in range(2):
                            b = turn * 2 + par
                            act.wait_ge(turned, b + 1)
                            nc.scalar.activation(xT[:, :, bass.ds(b * S, S)],
                                                 x_ps[:, par, :].rearrange("p (k t) -> p k t", k=KC), ACT.Copy)\
                              .then_inc(kept, 1)
                    for n in range(NTURN):
                        act.wait_ge(w_turned, n + 1)
                        for q in range(4):
                            op = nc.scalar.activation(turned_block(4 * n + q)[1], w_ps[:, n % 2, q * P:q * P + P], ACT.Copy)
                        op.then_inc(w_kept, 1)

                @block.vector
                def _(dve):
                    dve.wait_ge(x_in[0], 16)
                    def rows_normed(b, par, more):
                        if more:
                            dve.wait_ge(x_in[1 - par], (b + par) * 8 + 16)
                            statistics(nc, dve, ln, 1 - par, rows_in[1 - par], bn, dve_passed, stat, b + 1)
                        dve.wait_ge(factors, b + 1)
                        if not isinstance(b, int) or b >= 2:
                            dve.wait_ge(kept, b - 1)
                        normalise(nc, ln, par, rows_in[par], xn[par], normed, b)

                    statistics(nc, dve, ln, 0, rows_in[0], bn, dve_passed, stat, 0)
                    rows_normed(0, 0, True)
                    rows_normed(1, 1, True)
                    with dve.Fori(0, (B - 4) // 2) as turn:
                        for par in range(2):
                            rows_normed(turn * 2 + (2 + par), par, True)
                    rows_normed(B - 2, 0, True)
                    rows_normed(B - 1, 1, False)
                    count = [0]

                    def link(op):
                        count[0] += 1
                        op.then_inc(dchain, 1)
                        dve.wait_ge(dchain, count[0])

                    dve.wait_ge(w_in, 48)
                    blocks = raw[:].rearrange("p m (n q) -> p (m n) q", q=QBLOCK)
                    wide = lambda m: m[:].unsqueeze(2).to_broadcast([P, 3 * NB, QBLOCK])
                    link(nc.vector.tensor_reduce(wmax[:], blocks, AX.X, ALU.max, apply_absolute_value=True))
                    link(nc.vector.tensor_scalar(wscale[:], wmax[:], 1.0 / 7.0, LEAST, ALU.mult, ALU.max))
                    link(nc.vector.reciprocal(winv[:], wscale[:]))
                    link(nc.vector.tensor_tensor(blocks, blocks, wide(winv), ALU.mult))
                    link(nc.vector.tensor_scalar(blocks, blocks, ROUND, -ROUND, ALU.add, ALU.add))
                    link(nc.vector.tensor_scalar(blocks, blocks, -8.0, 7.0, ALU.max, ALU.min))
                    nc.vector.tensor_tensor(blocks, blocks, wide(wscale), ALU.mult).then_inc(quantised, 1)
                    dve.wait_ge(kept, B)
                    for c in range(NCH):
                        op = nc.vector.tensor_reduce(peak[:, c:c + 1], xT[:, :, c * CH:(c + 1) * CH], AX.XY, ALU.max,
                                                     apply_absolute_value=True)
                    op.then_inc(peaked, 1)

        def scale_steps(dve, link, found, reduced, at, n_peaks, unit):
            nc.vector.reduce_max(top[:], peak[:, 0:n_peaks], AX.X).then_inc(found, 1)
            dve.wait_ge(reduced, 1)
            one = scales[:, at:at + 1]
            link(nc.vector.tensor_scalar(one, whole[:], unit, None, ALU.mult))
            link(nc.vector.tensor_scalar(one, one, 1.0 / QMAX, LEAST, ALU.mult, ALU.max))
            link(nc.vector.reciprocal(inverse[:, at:at + 1], one))

        def reduce_step(pool, found, reduced):
            pool.wait_ge(found, 1)
            nc.gpsimd.partition_all_reduce(whole[:], top[:], P, RMAX).then_inc(reduced, 1)

        def linker(dve, chain, count):
            def link(op):
                count[0] += 1
                op.then_inc(chain, 1)
                dve.wait_ge(chain, count[0])
            return link

        BANKS = 4
        PAIR = 2
        GROUPS = IB // PAIR
        NG = NCH * GROUPS

        wide_f = sb("wide", [P, IB, TOK], F32)
        gate_q = sb("gate_q", [P, IB, TOK], I16)
        sig = [sb(f"sig{i}", [P, PAIR, CH], F32) for i in range(2)]
        sig_q = sb("sig_q", [P, PAIR, CH], U16)
        prod_ps = ctx.enter_context(nc.psum_tensor("ffn_prod_ps", [P, BANKS, 512], F32))

        def products(pe, w, mm, ev):
            with pe.Fori(0, NCH // 2) as turn:
                for i in range(2 * IB):
                    c, f = i // IB, i % IB
                    pe.wait_ge(ev, turn * (2 * IB) + (i + 1))
                    for k in range(KC):
                        op = nc.tensor.matmul(prod_ps[:, i % BANKS, :], w[:, k, f * P:f * P + P],
                                              xT[:, k, bass.ds(turn * (2 * CH) + c * CH, CH)],
                                              start=(k == 0), stop=(k == KC - 1))
                    op.then_inc(mm, 1)

        def take_products(act, turn, i, mm, ev):
            c, f = i // IB, i % IB
            act.wait_ge(mm, turn * (2 * IB) + (i + 1))
            nc.scalar.activation(wide_f[:, f, bass.ds(turn * (2 * CH) + c * CH, CH)], prod_ps[:, i % BANKS, :],
                                 ACT.Copy, scale=scales[:, X_:X_ + 1]).then_inc(ev, 1)

        with ExitStack() as stage, nc.Block() as block:
            found, reduced, chain, xq, mm, ev = (
                sem(f"gate_{n}") for n in ("found", "reduced", "chain", "xq", "mm", "ev"))

            @block.gpsimd
            def _(pool):
                reduce_step(pool, found, reduced)

            @block.vector
            def _(dve):
                link = linker(dve, chain, [0])
                scale_steps(dve, link, found, reduced, X_, NCH, 1.0)
                link(nc.vector.tensor_scalar(xT[:], xT[:], inverse[:, X_:X_ + 1], ROUND, ALU.mult, ALU.add))
                nc.vector.tensor_scalar(xT[:], xT[:], -ROUND, QMAX, ALU.add, ALU.min).then_inc(xq, 1)
                with dve.Fori(0, NCH) as c:
                    for g in range(GROUPS):
                        dve.wait_ge(ev, c * IB + (PAIR * (g + 1) + BANKS))
                        nc.vector.tensor_reduce(peak[:, bass.ds(c * GROUPS + g, 1)],
                                                wide_f[:, PAIR * g:PAIR * g + PAIR, bass.ds(c * CH, CH)],
                                                AX.XY, ALU.max, apply_absolute_value=True)

            @block.tensor
            def _(pe):
                pe.wait_ge(xq, 1)
                products(pe, w_gate, mm, ev)

            @block.scalar
            def _(act):
                act.sem_inc(ev, BANKS)
                act.wait_ge(xq, 1)
                with act.Fori(0, NCH // 2) as turn:
                    for i in range(2 * IB):
                        take_products(act, turn, i, mm, ev)

        with ExitStack() as stage, nc.Block() as block:
            found, reduced, chain, gq, mm, ev, sg, step_done, used = (
                sem(f"up_{n}")
                for n in ("found", "reduced", "chain", "gq", "mm", "ev", "sg", "step_done", "used"))

            @block.gpsimd
            def _(pool):
                reduce_step(pool, found, reduced)

            @block.vector
            def _(dve):
                link = linker(dve, chain, [0])
                scale_steps(dve, link, found, reduced, GATE, NG, 1.0)
                with dve.Fori(0, NCH) as c:
                    cols = bass.ds(c * CH, CH)
                    nc.vector.tensor_scalar(gate_q[:, :, cols], wide_f[:, :, cols], inverse[:, GATE:GATE + 1], None,
                                            ALU.mult).then_inc(gq, 1)
                dve.wait_ge(gq, NCH)
                with dve.Fori(0, NCH // 2) as turn:
                    for i in range(2 * GROUPS):
                        c, g = i // GROUPS, i % GROUPS
                        n = turn * (2 * GROUPS) + i
                        cols = bass.ds(turn * (2 * CH) + c * CH, CH)
                        fs = slice(PAIR * g, PAIR * g + PAIR)
                        dve.wait_ge(sg, n + 1)
                        nc.vector.tensor_scalar(sig_q[:], sig[i % 2][:], 65536.0, None, ALU.mult).then_inc(step_done, 1)
                        dve.wait_ge(step_done, n * 2 + 1)
                        nc.vector.scalar_tensor_tensor(sig[i % 2][:], gate_q[:, fs, cols], scales[:, GATE:GATE + 1],
                                                       sig_q[:], ALU.mult, ALU.mult).then_inc(step_done, 1)
                        dve.wait_ge(step_done, n * 2 + 2)
                        nc.vector.tensor_reduce(peak[:, bass.ds(n, 1)], sig[i % 2][:], AX.XY, ALU.max,
                                                apply_absolute_value=True).then_inc(used, 1)
                        dve.wait_ge(ev, turn * (2 * IB) + (PAIR * (i + 1) + BANKS))
                        nc.vector.tensor_reduce(peak[:, bass.ds(n + NG, 1)], wide_f[:, fs, cols], AX.XY, ALU.max,
                                                apply_absolute_value=True)

            @block.tensor
            def _(pe):
                products(pe, w_up, mm, ev)

            @block.scalar
            def _(act):
                act.sem_inc(ev, BANKS)
                act.sem_inc(used, 2)
                with act.Fori(0, NCH // 2) as turn:
                    for i in range(2 * IB):
                        c, f = i // IB, i % IB
                        if f == 0:
                            act.wait_ge(gq, turn * 2 + (c + 1))
                        take_products(act, turn, i, mm, ev)
                        if f % PAIR == PAIR - 1:
                            g = i // PAIR
                            act.wait_ge(used, turn * (2 * GROUPS) + (g + 1))
                            nc.scalar.activation(sig[g % 2][:],
                                                 gate_q[:, f + 1 - PAIR:f + 1, bass.ds(turn * (2 * CH) + c * CH, CH)],
                                                 ACT.Sigmoid, scale=scales[:, GATE:GATE + 1]).then_inc(sg, 1)

        pool_of = xT[:].rearrange("p k t -> p (k t)")
        up_q = pool_of[:, 0:PAIR * CH // 2].bitcast(I16).rearrange("p (f t) -> p f t", f=PAIR)

        with ExitStack() as stage, nc.Block() as block:
            found, reduced, found2, reduced2, chain, ready, sg, step_done, used = (
                sem(f"product_{n}")
                for n in ("found", "reduced", "found2", "reduced2", "chain", "ready", "sg", "step_done", "used"))
            top2 = stage.enter_context(nc.sbuf_tensor("ffn_top2", [P, 1], F32))
            whole2 = stage.enter_context(nc.sbuf_tensor("ffn_whole2", [P, 1], F32))

            @block.gpsimd
            def _(pool):
                reduce_step(pool, found, reduced)
                pool.wait_ge(found2, 1)
                nc.gpsimd.partition_all_reduce(whole2[:], top2[:], P, RMAX).then_inc(reduced2, 1)

            @block.vector
            def _(dve):
                link = linker(dve, chain, [0])
                nc.vector.reduce_max(top2[:], peak[:, NG:2 * NG], AX.X).then_inc(found2, 1)
                scale_steps(dve, link, found, reduced, GATED, NG, 1.0 / 65536)
                dve.wait_ge(reduced2, 1)
                one = scales[:, UP:UP + 1]
                link(nc.vector.tensor_scalar(one, whole2[:], 1.0 / QMAX, LEAST, ALU.mult, ALU.max))
                link(nc.vector.reciprocal(inverse[:, UP:UP + 1], one))
                link(nc.vector.tensor_tensor(both_scales[:], scales[:, GATED:GATED + 1], one, ALU.mult))
                with dve.Fori(0, NCH // 2) as turn:
                    for i in range(2 * GROUPS):
                        c, g = i // GROUPS, i % GROUPS
                        n = turn * (2 * GROUPS) + i
                        cols = bass.ds(turn * (2 * CH) + c * CH, CH)
                        fs = slice(PAIR * g, PAIR * g + PAIR)
                        m = n * 4
                        dve.wait_ge(sg, n + 1)
                        nc.vector.tensor_scalar(sig_q[:], sig[i % 2][:], 65536.0, None, ALU.mult).then_inc(step_done, 1)
                        nc.vector.tensor_scalar(up_q, wide_f[:, fs, cols], inverse[:, UP:UP + 1], None,
                                                ALU.mult)
                        dve.wait_ge(step_done, m + 1)
                        nc.vector.scalar_tensor_tensor(sig[i % 2][:], gate_q[:, fs, cols], scales[:, GATE:GATE + 1],
                                                       sig_q[:], ALU.mult, ALU.mult).then_inc(step_done, 1)
                        dve.wait_ge(step_done, m + 2)
                        nc.vector.tensor_scalar(gate_q[:, fs, cols], sig[i % 2][:], inverse[:, GATED:GATED + 1],
                                                1.0 / 65536, ALU.mult, ALU.mult).then_inc(step_done, 1)
                        dve.wait_ge(step_done, m + 3)
                        nc.vector.tensor_tensor(wide_f[:, fs, cols], gate_q[:, fs, cols], up_q, ALU.mult)\
                          .then_inc(step_done, 1)
                        dve.wait_ge(step_done, m + 4)
                        nc.vector.tensor_reduce(peak[:, bass.ds(n, 1)], wide_f[:, fs, cols], AX.XY, ALU.max,
                                                apply_absolute_value=True).then_inc(used, 1)

            @block.scalar
            def _(act):
                act.sem_inc(used, 2)
                with act.Fori(0, NCH // 2) as turn:
                    for i in range(2 * GROUPS):
                        c, g = i // GROUPS, i % GROUPS
                        act.wait_ge(used, turn * (2 * GROUPS) + (i + 1))
                        nc.scalar.activation(sig[i % 2][:],
                                             gate_q[:, PAIR * g:PAIR * g + PAIR, bass.ds(turn * (2 * CH) + c * CH, CH)],
                                             ACT.Sigmoid, scale=scales[:, GATE:GATE + 1]).then_inc(sg, 1)

        at = [0]

        def piece(*shape):
            n = 1
            for d in shape:
                n *= d
            v = pool_of[:, at[0]:at[0] + n]
            at[0] += n
            return v.rearrange("p (a b) -> p a b", b=shape[-1])

        prod_q = [piece(IB, S) for _ in range(2)]
        x_rows = [piece(ST, D) for _ in range(2)]
        y_rows = [piece(ST, D) for _ in range(2)]
        with ExitStack() as stage, nc.Block() as block:
            found, reduced, chain, rounded, quant, mm, ev = (
                sem(f"down_{n}")
                for n in ("found", "reduced", "chain", "rounded", "quant", "mm", "ev"))
            x_in = [sem(f"down_x_in{i}") for i in range(2)]
            y_out = [sem(f"down_y_out{i}") for i in range(2)]

            @block.sync
            def _(sp):
                with sp.Fori(0, B // 2) as turn:
                    for par in range(2):
                        b = turn * 2 + par
                        sp.wait_ge(ev, b + 1)
                        sp.dma_start(x_rows[par], x_dram[bass.ds(b * S, S), :].rearrange("(s p) d -> p s d", p=P))\
                          .then_inc(x_in[par], 16)

            @block.gpsimd
            def _(pool):
                reduce_step(pool, found, reduced)

            @block.vector
            def _(dve):
                dve.sem_inc(ev, 2)
                link = linker(dve, chain, [0])
                scale_steps(dve, link, found, reduced, PROD, NG, both_scales[:, 0:1])
                link(nc.vector.tensor_tensor(inverse[:, PROD:PROD + 1], inverse[:, PROD:PROD + 1], both_scales[:], ALU.mult))

                def quantise(b, par):
                    cols = bass.ds(b * S, S)
                    nc.vector.tensor_scalar(wide_f[:, :, cols], wide_f[:, :, cols], inverse[:, PROD:PROD + 1], ROUND,
                                            ALU.mult, ALU.add).then_inc(rounded, 1)
                    dve.wait_ge(rounded, b + 1)
                    if not isinstance(b, int) or b >= 2:
                        dve.wait_ge(mm, b - 1)
                    nc.vector.tensor_scalar(prod_q[par], wide_f[:, :, cols], -ROUND, QMAX, ALU.add, ALU.min)\
                      .then_inc(quant, 1)

                def finish(b, par):
                    dve.wait_ge(mm, b + 1)
                    dve.wait_ge(x_in[par], (b - par) * 8 + 16)
                    if not isinstance(b, int) or b >= 2:
                        dve.wait_ge(y_out[par], (b - par) * 8)
                    nc.vector.scalar_tensor_tensor(y_rows[par], prod_ps[:, par, :].rearrange("p (s d) -> p s d", s=ST),
                                                   scales[:, PROD:PROD + 1], x_rows[par], ALU.mult, ALU.add)\
                      .then_inc(ev, 1)

                quantise(0, 0)
                quantise(1, 1)
                finish(0, 0)
                quantise(2, 0)
                finish(1, 1)
                with dve.Fori(0, (B - 4) // 2) as turn:
                    for par in range(2):
                        b = turn * 2 + (2 + par)
                        quantise(b + 1, 1 - par)
                        finish(b, par)
                quantise(B - 1, 1)
                finish(B - 2, 0)
                finish(B - 1, 1)

            @block.tensor
            def _(pe):
                with pe.Fori(0, B // 2) as turn:
                    for par in range(2):
                        b = turn * 2 + par
                        pe.wait_ge(quant, b + 1)
                        pe.wait_ge(ev, b + 1)
                        for s in range(ST):
                            for k in range(IB):
                                op = nc.tensor.matmul(prod_ps[:, par, s * D:s * D + D], prod_q[par][:, k, s * P:s * P + P],
                                                      w_down[:, k, :], start=(k == 0), stop=(k == IB - 1))
                        op.then_inc(mm, 1)

            @block.scalar
            def _(act):
                with act.Fori(0, B // 2) as turn:
                    for par in range(2):
                        b = turn * 2 + par
                        act.wait_ge(ev, b + 3)
                        act.dma_start(out_dram[bass.ds(b * S, S), :].rearrange("(s p) d -> p s d", p=P), y_rows[par])\
                           .then_inc(y_out[par], 16)
                for i in range(2):
                    act.wait_ge(y_out[i], 8 * B)


def program(nc, a, out, phases=(1, 2, 3, 4, 5, 6)):
    with ExitStack() as top:
        ident = top.enter_context(nc.sbuf_tensor("ident", [P, P], F32))
        ident_bf = top.enter_context(nc.sbuf_tensor("ident_bf", [P, P], BF16))
        setup = top.enter_context(nc.semaphore("setup"))
        x_flat = a["x"].rearrange("b s d -> (b s) d")
        out_flat = out.rearrange("b s d -> (b s) d")
        x_dram = nc.dram_tensor("x_before_ffn_dram", [B * S, D], F32).ap() if 6 in phases else out_flat
        with nc.Block() as block:
            @block.gpsimd
            def _(pool):
                for m in (ident, ident_bf):
                    nc.gpsimd.memset(m[:], 0.0).then_inc(setup, 1)
                pool.wait_ge(setup, 2)
                for m in (ident, ident_bf):
                    nc.gpsimd.affine_select(out=m[:], in_=m[:], compare_op=ALU.not_equal, fill=1.0, base=0,
                                            pattern=[[-1, P]], channel_multiplier=1).then_inc(setup, 1)
        if phases != [6]:
            layers(nc, a, ident, ident_bf, x_flat, x_dram, phases)
            x_flat = x_dram
        if 6 in phases:
            quantised_ffn(nc, a, ident, x_flat, out_flat)


def layers(nc, a, ident, ident_bf, x_flat, x_dram, phases):
    with ExitStack() as ctx:
        x_sb = ctx.enter_context(nc.sbuf_tensor("x_sb", [P, TILES, D], F32))
        x_loaded = ctx.enter_context(nc.semaphore("x_loaded"))
        stored = ctx.enter_context(nc.semaphore("stored"))
        x_view = x_flat.rearrange("(t p) d -> p t d", p=P)
        out_view = x_dram.rearrange("(t p) d -> p t d", p=P)
        with nc.Block() as block:
            @block.sync
            def _(sp):
                for n in range(4):
                    tiles = slice(n * TILES // 4, (n + 1) * TILES // 4)
                    sp.dma_start(x_sb[:, tiles, :], x_view[:, tiles, :]).then_inc(x_loaded, 16)
                sp.wait_ge(x_loaded, 64)

        scratch = lambda kind, nk: {
            "q": nc.dram_tensor(f"{kind}_q_parts_dram", [2, 2, D, S], F32).ap(),
            "k": nc.dram_tensor(f"{kind}_k_parts_dram", [2, 2, D, nk], F32).ap(),
            "m": nc.dram_tensor(f"{kind}_m_parts_dram", [2, 2, H // 2, S], F32).ap(),
            "pad": nc.dram_tensor(f"{kind}_pad_dram", [B, S2], F32).ap(),
        }
        w = {"wq": a["L0_attn_w_qkv"][:, 0:D], "wk": a["L0_attn_w_qkv"][:, D:2 * D],
             "wv": a["L0_attn_w_qkv"][:, 2 * D:3 * D], "wo": a["L0_attn_w_out"],
             "bq": a["L0_attn_b_qkv"][0:D], "bk": a["L0_attn_b_qkv"][D:2 * D],
             "bv": a["L0_attn_b_qkv"][2 * D:3 * D], "bo": a["L0_attn_b_out"]}
        if 1 in phases:
            attention(nc, "window", x_sb, ident, ident_bf, w, scratch("window", S))
        if 3 in phases:
            slots_dram = nc.dram_tensor("moe_slots_dram", [MT * TM, D], F32).ap()
            y_dram = nc.dram_tensor("moe_y_dram", [MT * TM, D], F32).ap()
        names = {"wq": "Wq", "wk": "Wk", "wv": "Wv", "wo": "Wo", "bq": "bq", "bk": "bk", "bv": "bv", "bo": "bo"}
        zero_filled = ctx.enter_context(nc.semaphore("zero_filled"))
        for phase, kind, layer, mask in ((2, "cross_pad", "L0_xattn", "mask_BxS2_bk1"),
                                         (3, "experts", None, None), (4, "causal", "L1_attn", None),
                                         (5, "cross_mask", "L1_xattn", "mask_SxS2_bk1")):
            if phase not in phases:
                continue
            if kind == "experts":
                with nc.sbuf_tensor("zeros", [P, 2 * D], F32) as zeros:
                    with nc.Block() as block:
                        @block.vector
                        def _(dve):
                            nc.vector.memset(zeros[:], 0.0).then_inc(zero_filled, 16)

                        @block.sync
                        def _(sp):
                            sp.wait_ge(zero_filled, 16)
                            for n in range(MT):
                                sp.dma_start(slots_dram[n * TM:(n + 1) * TM, :].rearrange("(s p) d -> p s d", p=P),
                                             zeros[:].rearrange("p (s d) -> p s d", s=TS)).then_inc(zero_filled, 16)
                    experts(nc, a, x_sb, ident, slots_dram, y_dram, (zero_filled, 16 * (MT + 1)))
                continue
            w = {k: a.get(f"{layer}_{n}") for k, n in names.items()}
            if kind == "causal":
                attention(nc, kind, x_sb, ident, ident_bf, w, scratch(kind, S))
            else:
                with nc.sbuf_tensor(f"{kind}_ctxT", [P, KC, B * S2], F32) as ctxT:
                    context_columns(nc, kind, a["ctx_1024"].rearrange("b s d -> (b s) d"), ctxT, ident)
                    attention(nc, kind, x_sb, ident, ident_bf, w, scratch(kind, S2), ctxT, a[mask])
        with nc.Block() as block:
            @block.sync
            def _(sp):
                for n in range(4):
                    tiles = slice(n * TILES // 4, (n + 1) * TILES // 4)
                    sp.dma_start(out_view[:, tiles, :], x_sb[:, tiles, :]).then_inc(stored, 16)
                sp.wait_ge(stored, 64)


def pack(inputs):
    import numpy as np

    a = {n: np.asarray(v) for n, v in inputs.items()}
    rows = lambda w: w.reshape(NE, w.shape[1] // P, P, w.shape[2]).transpose(0, 2, 1, 3).reshape(NE, P, -1)
    cols = lambda b: b.reshape(NE, FB, P).transpose(0, 2, 1)
    a["moe_w"] = np.concatenate(
        [rows(a.pop("L0_ffn_w1")), rows(a.pop("L0_ffn_w2")), rows(a.pop("L0_ffn_w3")), cols(a.pop("L0_ffn_b1")),
         cols(a.pop("L0_ffn_b2")), np.broadcast_to(a.pop("L0_ffn_b3")[:, None, :], (NE, P, D))], axis=2)
    for n in ("Wq", "Wk", "Wv", "Wo"):
        a[f"L1_attn_{n}"] = a[f"L1_attn_{n}"].T
    return {n: np.ascontiguousarray(v) for n, v in a.items()}


_SHAPE = (16, 256, 256)


def kernel(**inputs):
    import numpy as np
    import concourse.bacc as bacc
    from concourse.bass_utils import run_bass_kernel_spmd

    nc = bacc.Bacc("TRN2", target_bir_lowering=False, num_devices=1)
    arrays = pack(inputs)
    arguments = {n: nc.dram_tensor(f"{n}_in", v.shape, mybir.dt.from_np(v.dtype), kind="ExternalInput").ap()
                 for n, v in arrays.items()}
    out = nc.dram_tensor("x_out", _SHAPE, F32, kind="ExternalOutput").ap()
    program(nc, arguments, out)
    result = run_bass_kernel_spmd(nc, [{f"{n}_in": v for n, v in arrays.items()}], core_ids=[0])
    return result.results[0]["x_out"]
```

```python
import concourse.bass as bass
from concourse import mybir
from contextlib import ExitStack, contextmanager

F32 = mybir.dt.float32
F32R = mybir.dt.float32r
BF16 = mybir.dt.bfloat16
I16 = mybir.dt.int16
U16 = mybir.dt.uint16
U8 = mybir.dt.uint8
I32 = mybir.dt.int32
U32 = mybir.dt.uint32
ALU = mybir.AluOpType
ACT = mybir.ActivationFunctionType
AX = mybir.AxisListType

B, S, D = 16, 256, 256
S2 = 77
S2P = S2 + 1
H = 16
HD = D // H
P = 128
KC = D // P
ST = S // P
TILES = B * ST
EPS = 1e-5
MASKED = -float(2 ** 100)
CTX_TILES = (B * S2 + P - 1) // P
MAX_ROW = HD * 4
PAD_ROW = 96
VW = 32


def wait(engine, semaphore, value):
    if isinstance(value, int) and value <= 0:
        return
    engine.wait_ge(semaphore, value)


@contextmanager
def semaphores(nc, phase):
    taken = []

    def sem(name):
        taken.append(nc.alloc_semaphore(f"{phase}_{name}"))
        return taken[-1]

    yield sem
    nc.clear_and_free_semaphores(taken)
    nc.all_engine_barrier()


def inverse_deviation(nc, pool, ln, par, chain, n, done):
    nc.gpsimd.tensor_tensor(ln["var_eps"][par][:], ln["mv"][par][:, :, 1], ln["eps"][:], ALU.add).then_inc(chain, 1)
    pool.wait_ge(chain, n + 1)
    nc.gpsimd.tensor_tensor(ln["rstd"][par][:], ln["var_eps"][par][:], ln["half"][:], ALU.pow).then_inc(done, 1)


def gate(engine, passed):
    engine.sem_inc(passed, 1)


def layernorm_tiles(sb):
    ln = {n: [sb(f"{n}{i}", [P, ST] + rest, F32) for i in range(2)]
          for n, rest in (("stats", [6]), ("mv", [2]), ("var_eps", []), ("rstd", []))}
    ln |= {n: sb(n, [P, ST], F32) for n in ("eps", "half")}
    return ln


def statistics(nc, dve, ln, par, rows, bn, passed, stat, b):
    for s in range(ST):
        op = nc.vector.bn_stats(ln["stats"][par][:, s, :], rows(b, s))
    op.then_inc(bn, 1)
    dve.wait_ge(bn, b + 1)
    gate(dve, passed)
    for s in range(ST):
        op = nc.vector.bn_aggr(ln["mv"][par][:, s, :], ln["stats"][par][:, s, :])
    op.then_inc(stat, 1)


def normalise(nc, ln, par, rows, out, normed, b):
    for s in range(ST):
        op = nc.vector.tensor_scalar(out[:, s, :], rows(b, s), ln["mv"][par][:, s, 0:1],
                                     ln["rstd"][par][:, s:s + 1], ALU.subtract, ALU.mult)
    op.then_inc(normed, 1)


def attention(nc, kind, x_sb, q_stack, k_stack, v_aug, ident, ident_bf, w, scratch, context=None, masks=None):
    cross = kind in ("cross_pad", "cross_mask")
    NK = S2 if cross else S
    NKC = S2P if cross else S
    KTILES = 1 if cross else ST
    KROWS = S2 if cross else P

    if kind == "window":
        R = 32
        W1 = P + R
        direct = [(0, 0, W1, 0), (1, S - W1, W1, W1)]
        transposed = [(0, 0, W1, 0), (1, S - W1, W1, W1)]
        mask_at, mask_n = (0, 0), 2 * W1
    elif kind == "causal":
        direct = [(1, 0, S, 0), (0, 0, P, S)]
        transposed = [(1, P, P, 0), (0, 0, S, P)]
        mask_at, mask_n = (P, 0), 2 * P
    else:
        direct = [(0, 0, NKC, 0), (1, 0, NKC, NKC)]
        transposed = [(0, 0, S, 0)]
        mask_at, mask_n = (0, 0), 0
    EW = max(c + n for _, _, n, c in transposed)

    with ExitStack() as ctx:
        def sb(name, shape, dt):
            return ctx.enter_context(nc.sbuf_tensor(f"{kind}_{name}", shape, dt))

        def pb(name, shape):
            return ctx.enter_context(nc.psum_tensor(f"{kind}_{name}", shape, F32))

        sem = ctx.enter_context(semaphores(nc, kind))

        wq = sb("wq", [P, KC, D], F32)
        wk = sb("wk", [P, KC, D], F32)
        wv = sb("wv", [P, KC, D], F32)
        wo = sb("wo", [P, KC, D], F32)
        bq = sb("bq", [P, KC], F32)
        bk = sb("bk", [P, KC], F32)
        bv = sb("bv", [P, KC], F32)
        bo = sb("bo", [1, D], F32)
        bv_wide = sb("bv_wide", [P, KC, P], F32)
        ones_row = sb("ones_row", [1, P], F32)
        out_bias = sb("out_bias", [P, D], F32)
        v_stage = sb("v_stage", [P, KTILES * H, HD], F32)
        prob = sb("prob", [P, 4, EW], F32)
        ln = layernorm_tiles(sb)
        xn = [sb(f"xn{i}", [P, ST, D], F32) for i in range(2)]
        xT = sb("xT", [P, KC, S], F32)
        q_parts = sb("q_parts", [P, 2, KC, S], F32R)
        k_parts = sb("k_parts", [P, 2, KC, NK], F32R)
        m_tok = [sb(f"m_tok{i}", [P, ST, H], F32) for i in range(2)]
        m_parts = sb("m_parts", [H // 2, 2, S], F32R)
        o_aug = sb("o_aug", [P, 4, S], F32)
        recip = sb("recip", [P, ST * H], F32)
        o_tok = sb("o_tok", [P, ST, H, HD], F32)
        oT = sb("oT", [P, KC, S], F32)
        if cross:
            ctx_b = [sb(f"ctx_b{i}", [P, KC, S2], F32) for i in range(2)]
            ctx_rows = sb("ctx_rows", [P, CTX_TILES, D], F32)
            ctxT = sb("ctxT", [P, KC, B * S2], F32)
        if kind == "window":
            mask1 = mask2 = sb("mask", [P, mask_n], BF16)
        elif kind == "causal":
            mask1 = sb("mask1", [P, mask_n], BF16)
            mask2 = sb("mask2", [P, mask_n], BF16)
        elif kind == "cross_mask":
            mask_u8 = sb("mask_u8", [P, ST, S2], U8)
            maskT_u8 = sb("maskT_u8", [S2, S], U8)
            mask1 = sb("mask1", [P, ST * NKC], BF16)
            mask2 = sb("mask2", [P, S], BF16)
            mask_n = 1
        else:
            pad_u8 = sb("pad_u8", [B, S2], U8)
            pad_f = sb("pad_f", [B, S2], F32)

        ps1 = pb("ps1", [P, 2, 512])
        ps2 = pb("ps2", [P, 2, 512])
        pso = pb("pso", [P, 2, 512])
        misc = pb("misc", [P, 2, 512])

        loaded = sem("loaded")
        consts = sem("consts")
        scaled = sem("scaled")
        bias_mm = sem("bias_mm")
        bias_done = sem("bias_done")
        padrow = sem("padrow")
        bn = sem("bn")
        stat = sem("stat")
        pool_chain = sem("pool_chain")
        scaled_by = sem("scaled_by")
        dve_passed = sem("dve_passed")
        pool_passed = sem("pool_passed")
        normed = sem("normed")
        biased = sem("biased")
        ctx_loaded = sem("ctx_loaded")
        ctx_turned = sem("ctx_turned")
        ctx_copied = sem("ctx_copied")
        ctx_ready = sem("ctx_ready")
        xT_mm = sem("xT_mm")
        xT_ev = sem("xT_ev")
        q_mm = sem("q_mm")
        q_hi = sem("q_hi")
        q_lo = sem("q_lo")
        k_mm = sem("k_mm")
        k_hi = sem("k_hi")
        k_lo = sem("k_lo")
        v_mm = sem("v_mm")
        v_ev = sem("v_ev")
        v_in = sem("v_in")
        parts_out = sem("parts_out")
        stacked = [sem(f"stacked{i}") for i in range(2)]
        s1_mm = sem("s1_mm")
        s1_max = sem("s1_max")
        m_mm = sem("m_mm")
        m_hi = sem("m_hi")
        m_lo = sem("m_lo")
        m_out = sem("m_out")
        m_in = [sem(f"m_in{i}") for i in range(2)]
        s2_mm = sem("s2_mm")
        expd = sem("expd")
        pv_mm = sem("pv_mm")
        o_ev = sem("o_ev")
        o_mm = sem("o_mm")
        recip_done = sem("recip_done")
        o_norm = sem("o_norm")
        oT_mm = sem("oT_mm")
        oT_ev = sem("oT_ev")
        proj_mm = sem("proj_mm")
        added = sem("added")

        N_LOAD = 16 * (4 + (4 if w["bq"] is not None else 0)
                       + {"cross_mask": 2, "cross_pad": 1}.get(kind, 0))
        bank = lambda k: misc[:, k, :]
        xT_ps = bank(0).rearrange("p (k t) -> p k t", k=KC)
        q_ps = bank(1).rearrange("p (k t) -> p k t", k=KC)
        k_ps = bank(0)[:, 0:KC * NK].rearrange("p (k t) -> p k t", k=KC)
        v_ps = bank(1)[:, 0:KTILES * D].rearrange("p (k h d) -> p (k h) d", k=KTILES, d=HD)
        o_heads = misc[:, :, :].rearrange("p s (h d) -> p (s h) d", d=VW)
        parts_w = [scratch["q"], scratch["k"]]
        STACK_DMAS = 4 + 4 + 1 + (kind == "cross_pad")
        FIRST, LAST = 4, 14
        STEPS = B + 3

        def steps(engine, step):
            for t in range(FIRST):
                step(t, t % 2)
            with engine.Fori(0, (LAST - FIRST) // 2) as turn:
                for k in range(2):
                    step(turn * 2 + (FIRST + k), k)
            for t in range(LAST, STEPS):
                step(t, t % 2)

        def active(t, lag):
            return not isinstance(t, int) or 0 <= t - lag < B

        def upto(t, lag, n=1):
            if isinstance(t, int):
                return n * max(0, min(B, t - lag + 1))
            return n * (t - lag + 1)

        def row_of(b, s):
            return x_sb[:, bass.ds(b * ST + s, 1), :].squeeze(1)

        def x_at(b):
            return x_sb[:, bass.ds(b * ST, ST), :]

        with nc.Block() as block:
            @block.sync
            def _(sp):
                if cross:
                    whole = CTX_TILES - 1
                    sp.dma_start(ctx_rows[:, 0:whole, :], context[0:whole * P, :].rearrange("(t p) d -> p t d", p=P))\
                      .then_inc(ctx_loaded, 16)
                    sp.dma_start(ctx_rows[0:B * S2 - whole * P, whole, :], context[whole * P:B * S2, :])\
                      .then_inc(ctx_loaded, 16)
                for name, tile in (("wq", wq), ("wk", wk), ("wv", wv), ("wo", wo)):
                    sp.dma_start(tile[:], w[name].rearrange("(k p) n -> p k n", p=P)).then_inc(loaded, 16)
                if w["bq"] is not None:
                    for name, tile in (("bq", bq), ("bk", bk), ("bv", bv)):
                        with nc.allow_non_contiguous_dma(reason="a bias a partition"):
                            sp.dma_start(tile[:], w[name].rearrange("(k p) -> p k", p=P)).then_inc(loaded, 16)
                    sp.dma_start(bo[:], w["bo"].rearrange("(o n) -> o n", o=1)).then_inc(loaded, 16)
                if kind == "cross_mask":
                    sp.dma_start(mask_u8[:], masks.rearrange("(s p) k -> p s k", p=P)).then_inc(loaded, 16)
                    with nc.allow_non_contiguous_dma(reason="a small mask, transposed"):
                        sp.dma_start(maskT_u8[:], masks.rearrange("q k -> k q")).then_inc(loaded, 16)
                if kind == "cross_pad":
                    sp.dma_start(pad_u8[:], masks).then_inc(loaded, 16)
                    sp.wait_ge(scaled, 3)
                    sp.dma_start(scratch["pad"], pad_f[:]).then_inc(padrow, 16)
                    sp.wait_ge(padrow, 16)

                def m_bounce(b, hf, n):
                    wait(sp, m_lo, n + 1)
                    wait(sp, m_hi, n + 1)
                    sp.dma_start(scratch["m"][hf].rearrange("c h t -> h c t"),
                                 m_parts[:].bitcast(F32)).then_inc(m_out, 16)
                    sp.wait_ge(m_out, (n + 1) * 16)
                    return hf

                def step(t, par):
                    a, b, c = t, t - 1, t - 2
                    if active(t, 2):
                        m_bounce(c, 1, 2 * c + 1)
                        sp.dma_start(q_stack[par][MAX_ROW:MAX_ROW + 2, 8:16, :].bitcast(F32), scratch["m"][1])\
                          .then_inc(m_in[1], 16)
                    if active(t, 0):
                        sp.wait_ge(q_lo, a + 1)
                        sp.wait_ge(q_hi, a + 1)
                        for part in range(2):
                            sp.dma_start(parts_w[0][par, part].rearrange("(k p) t -> p k t", p=P),
                                         q_parts[:, part].bitcast(F32)).then_inc(parts_out, 16)
                        sp.wait_ge(k_lo, a + 1)
                        sp.wait_ge(k_hi, a + 1)
                        for part in range(2):
                            sp.dma_start(parts_w[1][par, part].rearrange("(k p) t -> p k t", p=P),
                                         k_parts[:, part].bitcast(F32)).then_inc(parts_out, 16)
                        sp.wait_ge(parts_out, (a + 1) * 64)
                    for hf in range(2):
                        if active(t, 0):
                            if active(t, 2):
                                sp.wait_ge(s2_mm, c * H + 8 * (hf + 1))
                            hs = slice(8 * hf, 8 * hf + 8)
                            fs = slice(P * hf, P * hf + P)
                            sp.dma_start(q_stack[par][MAX_ROW:MAX_ROW + 2, hs, :].bitcast(F32),
                                         q_stack[par][MAX_ROW + 4:MAX_ROW + 6, hs, :].bitcast(F32)).then_inc(stacked[hf], 16)
                            for n in range(4):
                                rows = slice(HD * n, HD * n + HD)
                                sp.dma_start(q_stack[par][rows, hs, :].bitcast(F32),
                                             parts_w[0][par, n % 2, fs].rearrange("(h d) t -> d h t", d=HD))\
                                  .then_inc(stacked[hf], 16)
                                sp.dma_start(k_stack[par][rows, hs, 0:NK].bitcast(F32),
                                             parts_w[1][par, n // 2, fs].rearrange("(h d) t -> d h t", d=HD))\
                                  .then_inc(stacked[hf], 16)
                            if kind == "cross_pad":
                                row = scratch["pad"][bass.ds(a, 1), :] if not isinstance(a, int) else scratch["pad"][a:a + 1, :]
                                sp.dma_start(k_stack[par][PAD_ROW:PAD_ROW + 1, hs, 0:NK].bitcast(F32),
                                             row.unsqueeze(1).to_broadcast([1, 8, S2]))\
                                  .then_inc(stacked[hf], 16)
                        if hf == 0 and active(t, 1):
                            m_bounce(b, 0, 2 * b)
                            sp.dma_start(q_stack[1 - par][MAX_ROW:MAX_ROW + 2, 0:8, :].bitcast(F32), scratch["m"][0])\
                              .then_inc(m_in[0], 16)

                steps(sp, step)

            @block.gpsimd
            def _(pool):
                nc.gpsimd.memset(ones_row[:], 1.0)
                if cross:
                    nc.gpsimd.memset(prob[:], 0.0)
                if w["bq"] is None:
                    nc.gpsimd.memset(bq[:], 0.0)
                    nc.gpsimd.memset(bk[:], 0.0)
                if kind == "cross_mask":
                    nc.gpsimd.memset(mask1[:], 0.0)
                    nc.gpsimd.memset(mask2[:], 0.0)
                if kind in ("window", "causal"):
                    nc.gpsimd.memset(mask1[:], 0.0)
                    if kind == "causal":
                        nc.gpsimd.memset(mask2[:], 0.0)
                nc.gpsimd.memset(ln["eps"][:], EPS)
                nc.gpsimd.memset(ln["half"][:], -0.5).then_inc(pool_chain, 1)
                pool.wait_ge(pool_chain, 1)
                selects = 0
                if kind == "window":
                    for first, off in ((0, 0), (W1, R)):
                        m = mask1[:, first:first + W1]
                        nc.gpsimd.affine_select(out=m, in_=m, compare_op=ALU.is_ge, fill=MASKED,
                                                base=R - off, pattern=[[1, W1]], channel_multiplier=-1)\
                          .then_inc(pool_chain, 1)
                        selects += 1
                        pool.wait_ge(pool_chain, 1 + selects)
                        nc.gpsimd.affine_select(out=m, in_=m, compare_op=ALU.is_ge, fill=MASKED,
                                                base=R + off, pattern=[[-1, W1]], channel_multiplier=1)\
                          .then_inc(pool_chain, 1)
                        selects += 1
                if kind == "causal":
                    for m, sign in ((mask1, 1), (mask2, -1)):
                        nc.gpsimd.affine_select(out=m[:], in_=m[:], compare_op=ALU.is_ge, fill=MASKED, base=0,
                                                pattern=[[0, 2], [-sign, P]], channel_multiplier=sign)\
                          .then_inc(pool_chain, 1)
                        selects += 1
                pool.wait_ge(pool_chain, 1 + selects)
                pool.sem_inc(consts, 1)

                def layernorm(b, par):
                    pool.wait_ge(stat, b + 1)
                    inverse_deviation(nc, pool, ln, par, pool_chain, 1 + selects + b, scaled_by)

                def add_bias(b):
                    pool.wait_ge(normed, b + 1)
                    pool.wait_ge(bias_done, 1)
                    gate(pool, pool_passed)
                    for s in range(ST):
                        op = nc.gpsimd.tensor_tensor(row_of(b, s), row_of(b, s), out_bias[:], ALU.add)
                    op.then_inc(biased, 1)

                def step(t, par):
                    if cross and active(t, 0):
                        if not isinstance(t, int) or t >= 2:
                            pool.wait_ge(v_mm, t - 1)
                            gate(pool, pool_passed)
                        at = t * S2
                        nc.gpsimd.tensor_copy(ctx_b[par][:], ctxT[:, :, bass.ds(at, S2)]).then_inc(ctx_ready, 1)
                    if w["bq"] is not None and active(t, 0):
                        add_bias(t)
                    if active(t, -1):
                        layernorm(t + 1, 1 - par)
                    if active(t, 0):
                        pool.wait_ge(v_ev, t + 1)
                        if active(t, 2):
                            pool.wait_ge(pv_mm, (t - 1) * H)
                        gate(pool, pool_passed)
                        nc.gpsimd.tensor_copy(v_aug[par][0:KROWS, 0:KTILES].rearrange("p k h d -> p (k h) d")[:, :, 0:HD],
                                              v_stage[0:KROWS]).then_inc(v_in, 1)

                layernorm(0, 0)
                if cross:
                    pool.wait_ge(ctx_copied, CTX_TILES)
                steps(pool, step)

            @block.vector
            def _(dve):
                if cross:
                    for t in range(CTX_TILES):
                        n = min(P, B * S2 - t * P)
                        dve.wait_ge(ctx_turned, t + 1)
                        nc.vector.tensor_copy(ctxT[:, :, t * P:t * P + n],
                                              ps1[:, t % 2, 0:KC * P].rearrange("p (k t) -> p k t", k=KC)[:, :, 0:n])\
                          .then_inc(ctx_copied, 1)
                dve.wait_ge(loaded, N_LOAD)
                dve.wait_ge(consts, 1)
                nc.vector.tensor_scalar(wq[:], wq[:], HD ** -0.5, None, ALU.mult)
                if w["bq"] is not None:
                    nc.vector.tensor_scalar(bq[:], bq[:], HD ** -0.5, None, ALU.mult)
                    nc.vector.tensor_copy(bv_wide[:], bv[:].unsqueeze(2).to_broadcast([P, KC, P]))
                if kind == "cross_mask":
                    nc.vector.tensor_scalar(mask1[:].rearrange("p (s k) -> p s k", s=ST)[:, :, 0:S2], mask_u8[:],
                                            -1.0, -MASKED, ALU.add, ALU.mult)
                    nc.vector.tensor_scalar(mask2[0:S2, :], maskT_u8[:], -1.0, -MASKED, ALU.add, ALU.mult)
                nc.vector.memset(recip[:], 0.0).then_inc(scaled, 2)
                dve.wait_ge(scaled, 2)
                if kind == "cross_pad":
                    nc.vector.tensor_scalar(pad_f[:], pad_u8[:], -1.0, -MASKED, ALU.add, ALU.mult).then_inc(scaled, 1)
                if w["bq"] is not None:
                    dve.wait_ge(bias_mm, 1)
                    nc.vector.tensor_copy(out_bias[:], bank(0)[:, 0:D]).then_inc(bias_done, 1)

                def low_part(out, psum, bias, hi, parts_ready, done, batch):
                    dve.wait_ge(parts_ready, batch + 1)
                    if not isinstance(batch, int) or batch >= 1:
                        dve.wait_ge(parts_out, batch * 64)
                    for k in range(KC):
                        op = nc.vector.scalar_tensor_tensor(out[:, k, :], psum[:, k, :], bias[:, k:k + 1],
                                                            hi[:, k, :].bitcast(F32), ALU.add, ALU.subtract)
                    op.then_inc(done, 1)

                def step(t, par):
                    if active(t, 2):
                        m_low_at(t - 2, 1)
                    for g in range(H):
                        if active(t, 1):
                            n = (t - 1) * H + g
                            dve.wait_ge(s1_mm, n + 1)
                            if g == 0 and active(t, 3):
                                dve.wait_ge(m_mm, (t - 3) * 2 + 2)
                            m = m_tok[1 - par]
                            if kind == "causal":
                                nc.vector.reduce_max(m[:, 1, g:g + 1], ps1[:, g % 2, 0:S], AX.X)
                                op = nc.vector.reduce_max(m[:, 0, g:g + 1], ps1[:, g % 2, S:S + P], AX.X)
                            else:
                                wd = direct[1][3]
                                src = ps1[:, g % 2, 0:2 * wd].rearrange("p (s k) -> p s k", s=2)
                                op = nc.vector.reduce_max(m[:, :, g], src[:, :, 0:min(wd, NK)], AX.X)
                            op.then_inc(s1_max, 1)
                        if g == 3 and active(t, 0):
                            low_part(q_parts[:, 1], q_ps, bq, q_parts[:, 0], q_hi, q_lo, t)
                        if g == 5 and active(t, 0):
                            low_part(k_parts[:, 1], k_ps, bk, k_parts[:, 0], k_hi, k_lo, t)
                        if g == 7 and active(t, 0):
                            dve.wait_ge(v_mm, t + 1)
                            if active(t - 1, 0):
                                wait(dve, v_in, t)
                            nc.vector.tensor_copy(v_stage[0:KROWS], v_ps[0:KROWS]).then_inc(v_ev, 1)
                        if g == 9 and active(t, 1):
                            m_low_at(t - 1, 0)
                        if g == 10 and active(t, -1):
                            statistics(nc, dve, ln, 1 - par, row_of, bn, dve_passed, stat, t + 1)
                        if g == 14 and active(t, -1):
                            dve.wait_ge(scaled_by, t + 2)
                            if active(t, 1):
                                dve.wait_ge(xT_mm, t)
                            normalise(nc, ln, 1 - par, row_of, xn[1 - par], normed, t + 1)
                        if g == 12 and active(t, 3):
                            d = t - 3
                            dve.wait_ge(o_mm, d + 1)
                            nc.vector.reciprocal(recip[:].unsqueeze(2), o_heads[:, :, HD:HD + 1]).then_inc(recip_done, 1)
                            dve.wait_ge(recip_done, d + 1)
                            nc.vector.tensor_tensor(o_tok[:].rearrange("p s h d -> p (s h) d"), o_heads[:, :, 0:HD],
                                                    recip[:].unsqueeze(2).to_broadcast([P, ST * H, HD]), ALU.mult)\
                              .then_inc(o_norm, 1)
                    if active(t, 3):
                        d = t - 3
                        if w["bq"] is not None:
                            dve.wait_ge(biased, d + 1)
                        dve.wait_ge(proj_mm, d + 1)
                        nc.vector.tensor_tensor(x_at(d), x_at(d), bank(1).rearrange("p (s n) -> p s n", s=ST), ALU.add)\
                          .then_inc(added, 1)

                def m_low_at(b, hf):
                    n = b * 2 + hf
                    dve.wait_ge(m_hi, n + 1)
                    nc.vector.scalar_tensor_tensor(m_parts[:, 1, :], bank(hf)[0:8, 0:S], -1.0,
                                                   m_parts[:, 0, :].bitcast(F32), ALU.mult, ALU.subtract)\
                      .then_inc(m_lo, 1)

                statistics(nc, dve, ln, 0, row_of, bn, dve_passed, stat, 0)
                dve.wait_ge(scaled_by, 1)
                normalise(nc, ln, 0, row_of, xn[0], normed, 0)
                steps(dve, step)

            @block.scalar
            def _(act):
                def high_part(out, psum, bias, mm, done, batch):
                    act.wait_ge(mm, batch + 1)
                    if not isinstance(batch, int) or batch >= 1:
                        act.wait_ge(parts_out, batch * 64)
                    for k in range(KC):
                        op = nc.scalar.activation(out[:, k, :], psum[:, k, :], ACT.Identity, bias=bias[:, k:k + 1])
                    op.then_inc(done, 1)

                def m_high(b, hf):
                    n = b * 2 + hf
                    act.wait_ge(m_mm, n + 1)
                    wait(act, m_out, n * 16)
                    nc.scalar.activation(m_parts[:, 0, :], bank(hf)[0:8, 0:S], ACT.Copy, scale=-1.0)\
                      .then_inc(m_hi, 1)

                act.wait_ge(scaled, 2)
                act.wait_ge(consts, 1)

                def step(t, par):
                    if active(t, 2):
                        m_high(t - 2, 1)
                    if active(t, 3):
                        d = t - 3
                        act.wait_ge(pv_mm, (d + 1) * H)
                        if active(t, 4):
                            act.wait_ge(o_mm, d)
                        nc.scalar.activation(o_aug[:].rearrange("p i t -> p (i t)"),
                                             pso[:].rearrange("p i t -> p (i t)"), ACT.Copy).then_inc(o_ev, 1)
                    for g in range(H):
                        if active(t, 2):
                            n = (t - 2) * H + g
                            act.wait_ge(s2_mm, n + 1)
                            if not isinstance(t, int) or n >= 4:
                                act.wait_ge(pv_mm, n - 3)
                            nc.scalar.activation(prob[0:KROWS, g % 4, :], ps2[0:KROWS, g % 2, 0:EW], ACT.Exp)\
                              .then_inc(expd, 1)
                        if g == 1 and active(t, 0):
                            act.wait_ge(xT_mm, t + 1)
                            nc.scalar.activation(xT[:], xT_ps, ACT.Copy).then_inc(xT_ev, 1)
                        if g == 3 and active(t, 0):
                            high_part(q_parts[:, 0], q_ps, bq, q_mm, q_hi, t)
                        if g == 5 and active(t, 0):
                            high_part(k_parts[:, 0], k_ps, bk, k_mm, k_hi, t)
                        if g == 9 and active(t, 1):
                            m_high(t - 1, 0)
                        if g == 13 and active(t, 3):
                            act.wait_ge(oT_mm, t - 2)
                            nc.scalar.activation(oT[:], xT_ps, ACT.Copy).then_inc(oT_ev, 1)

                steps(act, step)

            @block.tensor
            def _(pe):
                if cross:
                    pe.wait_ge(ctx_loaded, 32)
                    for t in range(CTX_TILES):
                        n = min(P, B * S2 - t * P)
                        if t >= 2:
                            pe.wait_ge(ctx_copied, t - 1)
                        for k in range(KC):
                            op = nc.tensor.transpose(ps1[:, t % 2, k * P:k * P + n],
                                                     ctx_rows[0:n, t, k * P:k * P + P], ident[0:n, 0:n])
                        op.then_inc(ctx_turned, 1)
                    pe.wait_ge(ctx_copied, CTX_TILES)
                pe.wait_ge(scaled, 2)
                pe.wait_ge(consts, 1)
                if w["bq"] is not None:
                    for k in range(KC):
                        nc.tensor.matmul(bank(0)[:, 0:D], bv_wide[:, k, :], wo[:, k, :], start=(k == 0), stop=False)
                    nc.tensor.matmul(bank(0)[:, 0:D], ones_row[:], bo[:], start=False, stop=True).then_inc(bias_mm, 1)
                    pe.wait_ge(bias_done, 1)

                def scores(b, par, g):
                    n = b * H + g
                    if g % 8 == 0:
                        pe.wait_ge(stacked[g // 8], (b + 1) * 16 * STACK_DMAS)
                    if not (isinstance(b, int) and n < 2):
                        pe.wait_ge(s1_max, n - 1)
                    dst = ps1[:, g % 2, :]
                    if mask_n:
                        at = mask_at[0]
                        nc.tensor.matmul(dst[:, at:at + mask1.shape[1]], ident_bf[:], mask1[:], start=True, stop=False,
                                         skip_group_check=True)
                    for i, (qt, k0, nk, col) in enumerate(direct):
                        op = nc.tensor.matmul(dst[:, col:col + nk], q_stack[par][:, g, qt * P:qt * P + P],
                                              k_stack[par][:, g, k0:k0 + nk], start=(not mask_n), stop=True,
                                              skip_group_check=True)
                    op.then_inc(s1_mm, 1)

                def shifted(c, par, g):
                    n = c * H + g
                    if g % 8 == 0:
                        pe.wait_ge(m_in[g // 8], (c + 1) * 16)
                    if not (isinstance(c, int) and n < 2):
                        pe.wait_ge(expd, n - 1)
                    dst = ps2[:, g % 2, :]
                    if mask_n:
                        at = mask_at[1]
                        nc.tensor.matmul(dst[0:KROWS, at:at + mask2.shape[1]], ident_bf[:, 0:KROWS], mask2[:],
                                         start=True, stop=False, skip_group_check=True)
                    for i, (kt, q0, nq, col) in enumerate(transposed):
                        op = nc.tensor.matmul(dst[0:KROWS, col:col + nq],
                                              k_stack[par][:, g, kt * P:kt * P + KROWS],
                                              q_stack[par][:, g, q0:q0 + nq], start=(not mask_n), stop=True,
                                              skip_group_check=True)
                    op.then_inc(s2_mm, 1)

                def pv(c, par, g):
                    n = c * H + g
                    pe.wait_ge(expd, n + 1)
                    if g == 0:
                        pe.wait_ge(v_in, c + 1)
                        if not isinstance(c, int) or c >= 1:
                            pe.wait_ge(o_ev, c)
                    i, j = g // 4, g % 4
                    dst = pso[32 * j:32 * j + 32, i // 2, (i % 2) * S:(i % 2) * S + S]
                    order = sorted(transposed)
                    for m, (kt, q0, nq, col) in enumerate(order):
                        op = nc.tensor.matmul(dst[:, q0:q0 + nq], v_at(c, par)[:, kt, g, :], prob[:, g % 4, col:col + nq],
                                              start=(m == 0), stop=(m == len(order) - 1), skip_group_check=True)
                    op.then_inc(pv_mm, 1)

                def v_at(c, par):
                    return v_aug[par]

                def max_out(b, par, hf):
                    pe.wait_ge(s1_max, b * H + 8 * (hf + 1))
                    for s in range(ST):
                        op = nc.tensor.transpose(bank(hf)[0:8, s * P:s * P + P], m_tok[par][:, s, 8 * hf:8 * hf + 8],
                                                 ident[:])
                    op.then_inc(m_mm, 1)

                def step(t, par):
                    a, b, c, d = t, t - 1, t - 2, t - 3
                    if active(t, 2):
                        wait(pe, added, upto(t - 1, 3))
                        wait(pe, v_ev, upto(t - 1, 0))
                        max_out(c, par, 1)
                    for g in range(H):
                        if active(t, 1):
                            scores(b, 1 - par, g)
                        if active(t, 2):
                            shifted(c, par, g)
                            if g >= 2:
                                pv(c, par, g - 2)
                        if g == 1 and active(t, 0):
                            pe.wait_ge(normed, a + 1)
                            wait(pe, oT_ev, upto(t - 1, 3))
                            wait(pe, m_lo, upto(t - 1, 1, 2) - 1)
                            for k in range(KC):
                                for s in range(ST):
                                    op = nc.tensor.transpose(xT_ps[:, k, s * P:s * P + P],
                                                             xn[par][:, s, k * P:k * P + P], ident[:])
                            op.then_inc(xT_mm, 1)
                        if g == 2 and active(t, 0):
                            pe.wait_ge(xT_ev, a + 1)
                            wait(pe, m_lo, upto(t, 2, 2))
                            wait(pe, v_ev, upto(t - 1, 0))
                            for f in range(KC):
                                for k in range(KC):
                                    op = nc.tensor.matmul(q_ps[:, f, :], wq[:, k, f * P:f * P + P], xT[:, k, :],
                                                          start=(k == 0), stop=(k == KC - 1))
                            op.then_inc(q_mm, 1)
                        if g == 4 and active(t, 0):
                            if cross:
                                pe.wait_ge(ctx_ready, a + 1)
                            for f in range(KC):
                                for k in range(KC):
                                    rhs = ctx_b[par][:, k, :] if cross else xT[:, k, :]
                                    op = nc.tensor.matmul(k_ps[:, f, :], wk[:, k, f * P:f * P + P], rhs,
                                                          start=(k == 0), stop=(k == KC - 1))
                            op.then_inc(k_mm, 1)
                        if g == 6 and active(t, 0):
                            pe.wait_ge(q_lo, a + 1)
                            for s in range(KTILES):
                                for k in range(KC):
                                    lhs = ctx_b[par][:, k, :] if cross else xT[:, k, s * P:s * P + P]
                                    op = nc.tensor.matmul(bank(1)[0:KROWS, s * D:s * D + D], lhs, wv[:, k, :],
                                                          start=(k == 0), stop=(k == KC - 1))
                            op.then_inc(v_mm, 1)
                        if g == 8 and active(t, 1):
                            wait(pe, k_lo, upto(t, 0))
                            wait(pe, oT_ev, upto(t - 1, 3))
                            max_out(b, 1 - par, 0)
                        if g == 10 and active(t, 3):
                            pe.wait_ge(o_ev, d + 1)
                            wait(pe, m_lo, upto(t, 1, 2) - (1 if active(t, 1) else 0))
                            wait(pe, v_ev, upto(t, 0))
                            wait(pe, added, upto(t - 1, 3))
                            wait(pe, oT_ev, upto(t - 1, 3))
                            for s in range(ST):
                                for i in range(4):
                                    op = nc.tensor.transpose(bank(s)[:, i * P:i * P + P], o_aug[:, i, s * P:s * P + P],
                                                             ident[:])
                            op.then_inc(o_mm, 1)
                        if g == 12 and active(t, 3):
                            pe.wait_ge(o_norm, d + 1)
                            of = o_tok[:].rearrange("p s h d -> p s (h d)")
                            for k in range(KC):
                                for s in range(ST):
                                    op = nc.tensor.transpose(xT_ps[:, k, s * P:s * P + P], of[:, s, k * P:k * P + P],
                                                             ident[:])
                            op.then_inc(oT_mm, 1)
                        if g == 14 and active(t, 3):
                            pe.wait_ge(oT_ev, d + 1)
                            for s in range(ST):
                                for k in range(KC):
                                    op = nc.tensor.matmul(bank(1)[:, s * D:s * D + D], oT[:, k, s * P:s * P + P],
                                                          wo[:, k, :], start=(k == 0), stop=(k == KC - 1))
                            op.then_inc(proj_mm, 1)
                    if active(t, 2):
                        pv(c, par, H - 2)
                        pv(c, par, H - 1)

                steps(pe, step)


NE, FH = 8, 512
FB = FH // P
TM = 256
TS = TM // P
PAIRS = 2 * B * S
MT = (PAIRS + NE * (TM - 1)) // TM
RING = 3
W1_AT = 0
W2_AT = W1_AT + KC * FH
W3_AT = W2_AT + FB * FH
B1_AT = W3_AT + FB * D
B2_AT = B1_AT + FB
B3_AT = B2_AT + FB
WPACK = B3_AT + D
ROUND = 1.5 * 2.0 ** 23


def experts(nc, a, x_sb, ident, slots_dram, y_dram):
    with ExitStack() as ctx:
        def sb(name, shape, dt):
            return ctx.enter_context(nc.sbuf_tensor(f"moe_{name}", shape, dt))

        sem = ctx.enter_context(semaphores(nc, "moe"))

        pos = sb("pos", [P, TILES, 2], U32)
        gate2 = sb("gate2", [P, TILES, 8], F32)
        tile_expert = sb("tile_expert", [P, MT], I32)

        with ExitStack() as inner:
            def isb(name, shape, dt):
                return inner.enter_context(nc.sbuf_tensor(f"moe_{name}", shape, dt))

            xn = isb("xn", [P, TILES, D], F32)
            gw = isb("gw", [P, KC, NE], F32)
            gb = isb("gb", [P, NE], F32)
            ones = isb("ones", [P, P], F32)
            before = isb("before", [P, P], F32)
            iota_e = isb("iota_e", [P, NE], F32)
            iota_t = isb("iota_t", [P, MT], F32)
            ln = layernorm_tiles(isb)
            xb = [isb(f"xb{i}", [P, ST, D], F32) for i in range(2)]
            xT = [isb(f"xT{i}", [P, KC, S], F32) for i in range(2)]
            g = isb("g", [P, TILES, NE], F32)
            red = isb("red", [P, TILES], F32)
            best = isb("best", [P, TILES, 8], U32)
            best_f = isb("best_f", [P, TILES, 2], F32)
            hot = isb("hot", [P, 2, TILES, NE], F32)
            both = isb("both", [P, TILES, NE], F32)
            total = isb("total", [P, TILES, NE], F32)
            upto_t = isb("upto_t", [P, TILES, NE], F32)
            slot = isb("slot", [P, TILES, NE], F32)
            n_tiles = isb("n_tiles", [P, NE], F32)
            end_tile = isb("end_tile", [P, NE], F32)
            start_tile = isb("start_tile", [P, NE], F32)
            te = isb("te", [P, MT], F32)
            pos_f = isb("pos_f", [P, TILES, 2], F32)
            turned_ps = inner.enter_context(nc.psum_tensor("moe_turned_ps", [P, 2, 512], F32))
            logit_ps = inner.enter_context(nc.psum_tensor("moe_logit_ps", [P, 512], F32))
            rank_ps = inner.enter_context(nc.psum_tensor("moe_rank_ps", [P, 2, 512], F32))
            loaded, consts, stat, bn, chain, normed, turned, copied, logits, dchain, expd, hot_done, ranked, placed, sent = (
                sem(n) for n in ("loaded", "consts", "stat", "bn", "chain", "normed", "turned", "copied", "logits",
                                 "dchain", "expd", "hot_done", "ranked", "placed", "sent"))
            zeros = isb("zeros", [P, TS * D], F32)
            zeroed, zero_filled = sem("zeroed"), sem("zero_filled")
            kept, factors, dve_passed = sem("kept"), sem("factors"), sem("dve_passed")

            row_of = lambda b, s: x_sb[:, bass.ds(b * ST + s, 1), :].squeeze(1)

            with nc.Block() as block:
                @block.sync
                def _(sp):
                    with nc.allow_non_contiguous_dma(reason="eight columns"):
                        sp.dma_start(gw[:], a["L0_ffn_gate_w"].rearrange("(k p) e -> p k e", p=P)).then_inc(loaded, 16)
                        sp.dma_start(gb[:], a["L0_ffn_gate_b"].rearrange("(o e) -> o e", o=1).to_broadcast([P, NE]))\
                          .then_inc(loaded, 16)
                    sp.wait_ge(zeroed, 1)
                    for n in range(MT):
                        sp.dma_start(slots_dram[n * TM:(n + 1) * TM, :].rearrange("(s p) d -> p s d", p=P),
                                     zeros[:].rearrange("p (s d) -> p s d", s=TS)).then_inc(zero_filled, 16)

                @block.gpsimd
                def _(pool):
                    nc.gpsimd.memset(zeros[:], 0.0).then_inc(zeroed, 1)
                    nc.gpsimd.memset(ln["eps"][:], EPS)
                    nc.gpsimd.memset(ln["half"][:], -0.5)
                    nc.gpsimd.memset(ones[:], 1.0)
                    nc.gpsimd.iota(iota_e[:], pattern=[[1, NE]], base=0, channel_multiplier=0,
                                   allow_small_or_imprecise_dtypes=True)
                    nc.gpsimd.iota(iota_t[:], pattern=[[1, MT]], base=0, channel_multiplier=0,
                                   allow_small_or_imprecise_dtypes=True)
                    nc.gpsimd.memset(before[:], 1.0).then_inc(chain, 1)
                    pool.wait_ge(chain, 1)
                    nc.gpsimd.affine_select(out=before[:], in_=before[:], compare_op=ALU.is_gt, fill=0.0, base=0,
                                            pattern=[[1, P]], channel_multiplier=-1).then_inc(consts, 1)
                    with pool.Fori(0, B // 2) as turn:
                        for par in range(2):
                            b = turn * 2 + par
                            pool.wait_ge(stat, b + 1)
                            inverse_deviation(nc, pool, ln, par, chain, b + 1, factors)
                    pool.wait_ge(placed, 1)
                    pool.wait_ge(kept, B)
                    pool.wait_ge(zero_filled, 16 * MT)
                    for t in range(TILES):
                        for k in range(2):
                            nc.gpsimd.indirect_dma_start(
                                out=slots_dram, out_offset=bass.IndirectOffsetOnAxis(ap=pos[:, t, k:k + 1], axis=0),
                                in_=xn[:, t, :], in_offset=None).then_inc(sent, 16)
                    pool.wait_ge(sent, 16 * 2 * TILES)

                @block.tensor
                def _(pe):
                    pe.wait_ge(loaded, 32)
                    def turn_rows(b, par):
                        pe.wait_ge(normed, b + 1)
                        for k in range(KC):
                            for s in range(ST):
                                op = nc.tensor.transpose(turned_ps[:, par, k * S + s * P:k * S + s * P + P],
                                                         xb[par][:, s, k * P:k * P + P], ident[:])
                        op.then_inc(turned, 1)

                    def gate_logits(b, par):
                        pe.wait_ge(copied, b + 1)
                        for s in range(ST):
                            for k in range(KC):
                                op = nc.tensor.matmul(logit_ps[:, bass.ds(b * (ST * NE) + s * NE, NE)],
                                                      xT[par][:, k, s * P:s * P + P], gw[:, k, :],
                                                      start=(k == 0), stop=(k == KC - 1))
                        op.then_inc(logits, 1)

                    turn_rows(0, 0)
                    with pe.Fori(0, B // 2 - 1) as turn:
                        for k in range(2):
                            turn_rows(turn * 2 + (1 + k), 1 - k)
                            gate_logits(turn * 2 + k, k)
                    turn_rows(B - 1, 1)
                    gate_logits(B - 2, 0)
                    gate_logits(B - 1, 1)
                    pe.wait_ge(hot_done, 1)
                    pe.wait_ge(consts, 1)
                    flat = both[:].rearrange("p t e -> p (t e)")
                    nc.tensor.matmul(rank_ps[:, 0, 0:TILES * NE], before[:], flat, start=True, stop=True)
                    nc.tensor.matmul(rank_ps[:, 1, 0:TILES * NE], ones[:], flat, start=True, stop=True)\
                      .then_inc(ranked, 1)

                @block.scalar
                def _(act):
                    with act.Fori(0, B // 2) as turn:
                        for par in range(2):
                            b = turn * 2 + par
                            act.wait_ge(normed, b + 1)
                            nc.scalar.activation(xn[:, bass.ds(b * ST, ST), :], xb[par][:], ACT.Copy).then_inc(kept, 1)
                            act.wait_ge(turned, b + 1)
                            nc.scalar.activation(xT[par][:].rearrange("p k t -> p (k t)"), turned_ps[:, par, :], ACT.Copy)\
                              .then_inc(copied, 1)
                    act.wait_ge(dchain, EXP_AT)
                    nc.scalar.activation(g[:], g[:], ACT.Exp).then_inc(expd, 1)

                @block.vector
                def _(dve):
                    def rows_normed(b, par, more):
                        if more:
                            statistics(nc, dve, ln, 1 - par, row_of, bn, dve_passed, stat, b + 1)
                        dve.wait_ge(factors, b + 1)
                        if not isinstance(b, int) or b >= 2:
                            dve.wait_ge(kept, b - 1)
                            dve.wait_ge(copied, b - 1)
                        normalise(nc, ln, par, row_of, xb[par], normed, b)

                    statistics(nc, dve, ln, 0, row_of, bn, dve_passed, stat, 0)
                    rows_normed(0, 0, True)
                    rows_normed(1, 1, True)
                    with dve.Fori(0, (B - 4) // 2) as turn:
                        for par in range(2):
                            rows_normed(turn * 2 + (2 + par), par, True)
                    rows_normed(B - 2, 0, True)
                    rows_normed(B - 1, 1, False)
                    count = [0]

                    def link(op):
                        count[0] += 1
                        op.then_inc(dchain, 1)
                        dve.wait_ge(dchain, count[0])

                    wide = lambda m: m[:].unsqueeze(2).to_broadcast([P, TILES, NE])
                    dve.wait_ge(logits, B)
                    dve.wait_ge(loaded, 32)
                    dve.wait_ge(consts, 1)
                    link(nc.vector.tensor_tensor(g[:], logit_ps[:, 0:TILES * NE].rearrange("p (t e) -> p t e", e=NE),
                                                 gb[:].unsqueeze(1).to_broadcast([P, TILES, NE]), ALU.add))
                    link(nc.vector.reduce_max(red[:], g[:], AX.X))
                    link(nc.vector.tensor_tensor(g[:], g[:], wide(red), ALU.subtract))
                    assert count[0] == EXP_AT
                    dve.wait_ge(expd, 1)
                    link(nc.vector.reduce_sum(red[:], g[:], AX.X))
                    link(nc.vector.reciprocal(red[:], red[:]))
                    link(nc.vector.tensor_tensor(g[:], g[:], wide(red), ALU.mult))
                    for t in range(TILES):
                        op = nc.vector.max(gate2[:, t, :], g[:, t, :])
                    link(op)
                    for t in range(TILES):
                        op = nc.vector.max_index(best[:, t, :], gate2[:, t, :], g[:, t, :])
                    link(op)
                    link(nc.vector.tensor_copy(best_f[:], best[:, :, 0:2]))
                    for k in range(2):
                        op = nc.vector.tensor_tensor(hot[:, k], iota_e[:].unsqueeze(1).to_broadcast([P, TILES, NE]),
                                                     best_f[:, :, k:k + 1].to_broadcast([P, TILES, NE]), ALU.is_equal)
                    link(op)
                    nc.vector.tensor_tensor(both[:], hot[:, 0], hot[:, 1], ALU.add).then_inc(hot_done, 1)
                    dve.wait_ge(ranked, 1)
                    in_bank = lambda k: rank_ps[:, k, 0:TILES * NE].rearrange("p (t e) -> p t e", e=NE)
                    link(nc.vector.tensor_copy(total[:], in_bank(1)))
                    for e in range(NE):
                        op = nc.vector.tensor_tensor_scan(upto_t[:, :, e], ones[:, 0:TILES], total[:, :, e], 0.0,
                                                          ALU.mult, ALU.add)
                    link(op)
                    link(nc.vector.tensor_scalar(n_tiles[:], upto_t[:, TILES - 1, :], 1.0 / TM, (TM - 1) / 2.0 / TM,
                                                 ALU.mult, ALU.add))
                    link(nc.vector.tensor_scalar(n_tiles[:], n_tiles[:], ROUND, -ROUND, ALU.add, ALU.add))
                    link(nc.vector.tensor_tensor_scan(end_tile[:], ones[:, 0:NE], n_tiles[:], 0.0, ALU.mult, ALU.add))
                    link(nc.vector.tensor_tensor(start_tile[:], end_tile[:], n_tiles[:], ALU.subtract))
                    link(nc.vector.tensor_tensor(slot[:], upto_t[:], total[:], ALU.subtract))
                    link(nc.vector.tensor_tensor(slot[:], slot[:], in_bank(0), ALU.add))
                    link(nc.vector.scalar_tensor_tensor(slot[:], start_tile[:].unsqueeze(1).to_broadcast([P, TILES, NE]),
                                                        float(TM), slot[:], ALU.mult, ALU.add))
                    for k in range(2):
                        op = nc.vector.tensor_tensor(hot[:, k], hot[:, k], slot[:], ALU.mult)
                    link(op)
                    for k in range(2):
                        op = nc.vector.reduce_sum(pos_f[:, :, k], hot[:, k], AX.X)
                    link(op)
                    nc.vector.tensor_copy(pos[:], pos_f[:]).then_inc(placed, 1)
                    link(nc.vector.tensor_scalar(te[:], iota_t[:], start_tile[:, 1:2], None, ALU.is_ge))
                    for e in range(2, NE):
                        link(nc.vector.scalar_tensor_tensor(te[:], iota_t[:], start_tile[:, e:e + 1], te[:],
                                                            ALU.is_ge, ALU.add))
                    nc.vector.tensor_copy(tile_expert[:], te[:])

        with ExitStack() as inner:
            def isb(name, shape, dt):
                return inner.enter_context(nc.sbuf_tensor(f"moe_{name}", shape, dt))

            def ipb(name, banks):
                return inner.enter_context(nc.psum_tensor(f"moe_{name}", [P, banks, 512], F32))

            weights = [isb(f"weights{i}", [P, WPACK], F32) for i in range(RING)]
            rows = [isb(f"rows{i}", [P, TS, D], F32) for i in range(RING)]
            rowsT = isb("rowsT", [P, KC, TM], F32)
            h1 = isb("h1", [P, FB, TM], F32)
            h2 = isb("h2", [P, FB, TM], F32)
            y = [isb(f"y{i}", [P, TS, D], F32) for i in range(RING)]
            turned_ps = ipb("rows_ps", 1)
            h1_ps = ipb("h1_ps", 2)
            h2_ps = ipb("h2_ps", 2)
            y_ps = ipb("y_ps", RING)
            w_in = [sem(f"w_in{i}") for i in range(RING)]
            turned, copied, l1, act1, l2, act2, l3, y_done = (
                sem(n) for n in ("t_turned", "t_copied", "l1", "act1", "l2", "act2", "l3", "y_done"))
            y_out = [sem(f"y_out{i}") for i in range(RING)]

            def views(w):
                return (w[:, W1_AT:W2_AT].rearrange("p (k f) -> p k f", k=KC),
                        w[:, W2_AT:W3_AT].rearrange("p (k f) -> p k f", k=FB),
                        w[:, W3_AT:B1_AT].rearrange("p (k f) -> p k f", k=FB),
                        w[:, B1_AT:B2_AT], w[:, B2_AT:B3_AT], w[:, B3_AT:WPACK])

            def tiles(engine, tile):
                assert MT % RING == 0
                for k in range(RING):
                    tile(k, k, 0)
                with engine.Fori(0, MT // RING - 2) as turn:
                    for k in range(RING):
                        tile(turn * RING + (RING + k), k, turn + 1)
                for k in range(RING):
                    tile(MT - RING + k, k, MT // RING - 1)

            first_turn = lambda j: isinstance(j, int) and j < RING
            has_next = lambda j: not isinstance(j, int) or j + 1 < MT

            with nc.Block() as block:
                @block.sync
                def _(sp):
                    def tile(j, r, uses):
                        if not first_turn(j):
                            sp.wait_ge(y_done, j - (RING - 1))
                        e = sp.value_load(tile_expert[0:1, bass.ds(j, 1)], min_val=0, max_val=NE - 1)
                        sp.dma_start(rows[r][:], slots_dram[bass.ds(j * TM, TM), :].rearrange("(s p) d -> p s d", p=P))\
                          .then_inc(w_in[r], 16)
                        sp.dma_start(weights[r][:], a["moe_w"][bass.ds(e, 1)].squeeze(0)).then_inc(w_in[r], 16)

                    tiles(sp, tile)

                @block.gpsimd
                def _(pool):
                    def tile(j, r, uses):
                        pool.wait_ge(y_done, j + 1)
                        pool.dma_start(y_dram[bass.ds(j * TM, TM), :].rearrange("(s p) d -> p s d", p=P), y[r][:])\
                            .then_inc(y_out[r], 16)

                    tiles(pool, tile)
                    for r in range(RING):
                        pool.wait_ge(y_out[r], MT // RING * 16)

                @block.tensor
                def _(pe):
                    def turn_rows(j, r, uses):
                        pe.wait_ge(w_in[r], uses * 32 + 32)
                        for k in range(KC):
                            for s in range(TS):
                                op = nc.tensor.transpose(turned_ps[:, 0, k * TM + s * P:k * TM + s * P + P],
                                                         rows[r][:, s, k * P:k * P + P], ident[:])
                        op.then_inc(turned, 1)

                    def layer1(j, r):
                        w1 = views(weights[r])[0]
                        pe.wait_ge(copied, j + 1)
                        for f in range(FB):
                            for k in range(KC):
                                op = nc.tensor.matmul(h1_ps[:, f // 2, (f % 2) * TM:(f % 2) * TM + TM],
                                                      w1[:, k, f * P:f * P + P], rowsT[:, k, :],
                                                      start=(k == 0), stop=(k == KC - 1))
                            op.then_inc(l1, 1)

                    def tile(j, r, uses):
                        _, w2, w3, _, _, _ = views(weights[r])
                        after = (r + 1) % RING
                        if isinstance(j, int) and j == 0:
                            turn_rows(0, 0, 0)
                            layer1(0, 0)
                        if has_next(j):
                            turn_rows(j + 1, after, uses + (after == 0))
                        pe.wait_ge(act1, FB * (j + 1))
                        for f in range(FB):
                            for k in range(FB):
                                op = nc.tensor.matmul(h2_ps[:, f // 2, (f % 2) * TM:(f % 2) * TM + TM],
                                                      w2[:, k, f * P:f * P + P], h1[:, k, :],
                                                      start=(k == 0), stop=(k == FB - 1))
                            op.then_inc(l2, 1)
                        if has_next(j):
                            layer1(j + 1, after)
                        pe.wait_ge(act2, FB * (j + 1))
                        if not first_turn(j):
                            pe.wait_ge(y_done, j - (RING - 1))
                        for s in range(TS):
                            for k in range(FB):
                                op = nc.tensor.matmul(y_ps[:, r, s * D:s * D + D], h2[:, k, s * P:s * P + P],
                                                      w3[:, k, :], start=(k == 0), stop=(k == FB - 1))
                        op.then_inc(l3, 1)

                    tiles(pe, tile)

                @block.scalar
                def _(act):
                    def gelu(j, out, psum, bias, mm, done):
                        for f in range(FB):
                            act.wait_ge(mm, FB * j + (f // 2 * 2 + 2))
                            nc.scalar.activation(out[:, f, :], psum[:, f // 2, (f % 2) * TM:(f % 2) * TM + TM],
                                                 ACT.Gelu, bias=bias[:, f:f + 1]).then_inc(done, 1)

                    def tile(j, r, uses):
                        if isinstance(j, int) and j == 0:
                            gelu(0, h1, h1_ps, views(weights[0])[3], l1, act1)
                        gelu(j, h2, h2_ps, views(weights[r])[4], l2, act2)
                        if has_next(j):
                            gelu(j + 1, h1, h1_ps, views(weights[(r + 1) % RING])[3], l1, act1)

                    tiles(act, tile)

                @block.vector
                def _(dve):
                    def columns(j):
                        dve.wait_ge(turned, j + 1)
                        nc.vector.tensor_copy(rowsT[:].rearrange("p k t -> p (k t)"), turned_ps[:, 0, :]).then_inc(copied, 1)

                    def tile(j, r, uses):
                        if isinstance(j, int) and j == 0:
                            columns(0)
                        if has_next(j):
                            columns(j + 1)
                        dve.wait_ge(l3, j + 1)
                        if not first_turn(j):
                            dve.wait_ge(y_out[r], uses * 16)
                        b3 = views(weights[r])[5]
                        nc.vector.tensor_tensor(y[r][:], y_ps[:, r, :].rearrange("p (s d) -> p s d", s=TS),
                                                b3.unsqueeze(1).to_broadcast([P, TS, D]), ALU.add).then_inc(y_done, 1)

                    tiles(dve, tile)

        with ExitStack() as inner:
            SLOTS = 8
            got = [inner.enter_context(nc.sbuf_tensor(f"moe_got{i}", [P, D], F32)) for i in range(SLOTS)]
            here = [sem(f"here{i}") for i in range(SLOTS)]
            summed = sem("summed")
            with nc.Block() as block:
                @block.gpsimd
                def _(pool):
                    for n in range(2 * TILES):
                        if n >= SLOTS:
                            pool.wait_ge(summed, n - SLOTS + 1)
                        nc.gpsimd.indirect_dma_start(
                            out=got[n % SLOTS][:], out_offset=None, in_=y_dram,
                            in_offset=bass.IndirectOffsetOnAxis(ap=pos[:, n // 2, n % 2:n % 2 + 1], axis=0))\
                            .then_inc(here[n % SLOTS], 16)

                @block.vector
                def _(dve):
                    for n in range(2 * TILES):
                        t, k = n // 2, n % 2
                        dve.wait_ge(here[n % SLOTS], 16 * (n // SLOTS + 1))
                        if n >= 1:
                            dve.wait_ge(summed, n)
                        nc.vector.scalar_tensor_tensor(x_sb[:, t, :], got[n % SLOTS][:], gate2[:, t, k:k + 1],
                                                       x_sb[:, t, :], ALU.mult, ALU.add).then_inc(summed, 1)


EXP_AT = 3


FI = 768
IB = FI // P
TOK = B * S
CH = 512
NCH = TOK // CH
QBLOCK = 32
QMAX = 32767.0
LEAST = 1e-12


def quantised_ffn(nc, a, ident, x_dram, out_dram):
    with ExitStack() as ctx:
        def sb(name, shape, dt):
            return ctx.enter_context(nc.sbuf_tensor(f"ffn_{name}", shape, dt))

        sem = ctx.enter_context(semaphores(nc, "ffn"))

        xT = sb("xT", [P, KC, TOK], F32)
        w_gate = sb("w_gate", [P, KC, FI], F32)
        w_up = sb("w_up", [P, KC, FI], F32)
        w_down = sb("w_down", [P, IB, D], F32)
        peak = sb("peak", [P, NCH * IB * 2], F32)
        top = sb("top", [P, 1], F32)
        whole = sb("whole", [P, 1], F32)
        scales = sb("scales", [P, 5], F32)
        inverse = sb("inverse", [P, 5], F32)
        both_scales = sb("both_scales", [P, 1], F32)
        X_, GATE, GATED, UP, PROD = range(5)
        RMAX = bass.bass_isa.ReduceOp.max

        with ExitStack() as inner:
            def isb(name, shape, dt):
                return inner.enter_context(nc.sbuf_tensor(f"ffn_{name}", shape, dt))

            NB = FI // P * D // QBLOCK
            raw = isb("raw", [P, 3, FI // P * D], F32)
            wmax = isb("wmax", [P, 3 * NB], F32)
            wscale = isb("wscale", [P, 3 * NB], F32)
            winv = isb("winv", [P, 3 * NB], F32)
            x_all = isb("x_all", [P, TILES, D], F32)
            xn = [isb(f"xn{i}", [P, ST, D], F32) for i in range(2)]
            ln = layernorm_tiles(isb)
            w_ps = inner.enter_context(nc.psum_tensor("ffn_w_ps", [P, 2, 512], F32))
            x_ps = inner.enter_context(nc.psum_tensor("ffn_x_ps", [P, 2, 512], F32))
            w_in, dchain, quantised, w_turned, w_kept, chain, bn, stat, normed, turned, kept, peaked = (
                sem(n) for n in ("w_in", "dchain", "quantised", "w_turned", "w_kept", "chain", "bn", "stat", "normed",
                                 "turned", "kept", "peaked"))
            x_in, factors, dve_passed = sem("x_in"), sem("factors"), sem("dve_passed")
            row_of = lambda b, s: x_all[:, bass.ds(b * ST + s, 1), :].squeeze(1)
            NTURN = 3 * FI // P * D // P // 4

            def turned_block(n):
                m, r = n // (IB * KC), n % (IB * KC)
                if m < 2:
                    f, k = r // KC, r % KC
                    return raw[:, m, f * D + k * P:f * D + k * P + P], (w_gate, w_up)[m][:, k, f * P:f * P + P]
                o, k = r // IB, r % IB
                return raw[:, 2, o * FI + k * P:o * FI + k * P + P], w_down[:, k, o * P:o * P + P]

            with nc.Block() as block:
                @block.sync
                def _(sp):
                    sp.dma_start(raw[:, 0, :].rearrange("p (f n) -> p f n", n=D),
                                 a["L1_ffn_w_gate"].rearrange("(f p) n -> p f n", p=P)).then_inc(w_in, 16)
                    sp.dma_start(raw[:, 1, :].rearrange("p (f n) -> p f n", n=D),
                                 a["L1_ffn_w_up"].rearrange("(f p) n -> p f n", p=P)).then_inc(w_in, 16)
                    sp.dma_start(raw[:, 2, :].rearrange("p (f n) -> p f n", n=FI),
                                 a["L1_ffn_w_down"].rearrange("(f p) n -> p f n", p=P)).then_inc(w_in, 16)

                    x_view = x_dram.rearrange("(t p) d -> p t d", p=P)
                    for n in range(4):
                        tiles = slice(n * TILES // 4, (n + 1) * TILES // 4)
                        sp.dma_start(x_all[:, tiles, :], x_view[:, tiles, :]).then_inc(x_in, 16)

                @block.gpsimd
                def _(pool):
                    nc.gpsimd.memset(ln["eps"][:], EPS)
                    nc.gpsimd.memset(ln["half"][:], -0.5).then_inc(chain, 1)
                    pool.wait_ge(chain, 1)
                    with pool.Fori(0, B // 2) as turn:
                        for par in range(2):
                            b = turn * 2 + par
                            pool.wait_ge(stat, b + 1)
                            inverse_deviation(nc, pool, ln, par, chain, b + 1, factors)

                @block.tensor
                def _(pe):
                    pe.wait_ge(quantised, 1)
                    for n in range(NTURN):
                        if n >= 2:
                            pe.wait_ge(w_kept, n - 1)
                        for q in range(4):
                            op = nc.tensor.transpose(w_ps[:, n % 2, q * P:q * P + P], turned_block(4 * n + q)[0], ident[:])
                        op.then_inc(w_turned, 1)
                    with pe.Fori(0, B // 2) as turn:
                        for par in range(2):
                            b = turn * 2 + par
                            pe.wait_ge(normed, b + 1)
                            for k in range(KC):
                                for s in range(ST):
                                    op = nc.tensor.transpose(x_ps[:, par, k * S + s * P:k * S + s * P + P],
                                                             xn[par][:, s, k * P:k * P + P], ident[:])
                            op.then_inc(turned, 1)

                @block.scalar
                def _(act):
                    for n in range(NTURN):
                        act.wait_ge(w_turned, n + 1)
                        for q in range(4):
                            op = nc.scalar.activation(turned_block(4 * n + q)[1], w_ps[:, n % 2, q * P:q * P + P], ACT.Copy)
                        op.then_inc(w_kept, 1)
                    with act.Fori(0, B // 2) as turn:
                        for par in range(2):
                            b = turn * 2 + par
                            act.wait_ge(turned, b + 1)
                            nc.scalar.activation(xT[:, :, bass.ds(b * S, S)],
                                                 x_ps[:, par, :].rearrange("p (k t) -> p k t", k=KC), ACT.Copy)\
                              .then_inc(kept, 1)

                @block.vector
                def _(dve):
                    count = [0]

                    def link(op):
                        count[0] += 1
                        op.then_inc(dchain, 1)
                        dve.wait_ge(dchain, count[0])

                    dve.wait_ge(w_in, 48)
                    blocks = raw[:].rearrange("p m (n q) -> p (m n) q", q=QBLOCK)
                    wide = lambda m: m[:].unsqueeze(2).to_broadcast([P, 3 * NB, QBLOCK])
                    link(nc.vector.tensor_reduce(wmax[:], blocks, AX.X, ALU.max, apply_absolute_value=True))
                    link(nc.vector.tensor_scalar(wscale[:], wmax[:], 1.0 / 7.0, LEAST, ALU.mult, ALU.max))
                    link(nc.vector.reciprocal(winv[:], wscale[:]))
                    link(nc.vector.tensor_tensor(blocks, blocks, wide(winv), ALU.mult))
                    link(nc.vector.tensor_scalar(blocks, blocks, ROUND, -ROUND, ALU.add, ALU.add))
                    link(nc.vector.tensor_scalar(blocks, blocks, -8.0, 7.0, ALU.max, ALU.min))
                    nc.vector.tensor_tensor(blocks, blocks, wide(wscale), ALU.mult).then_inc(quantised, 1)
                    dve.wait_ge(x_in, 64)
                    def rows_normed(b, par, more):
                        if more:
                            statistics(nc, dve, ln, 1 - par, row_of, bn, dve_passed, stat, b + 1)
                        dve.wait_ge(factors, b + 1)
                        if not isinstance(b, int) or b >= 2:
                            dve.wait_ge(kept, b - 1)
                        normalise(nc, ln, par, row_of, xn[par], normed, b)

                    statistics(nc, dve, ln, 0, row_of, bn, dve_passed, stat, 0)
                    rows_normed(0, 0, True)
                    rows_normed(1, 1, True)
                    with dve.Fori(0, (B - 4) // 2) as turn:
                        for par in range(2):
                            rows_normed(turn * 2 + (2 + par), par, True)
                    rows_normed(B - 2, 0, True)
                    rows_normed(B - 1, 1, False)
                    dve.wait_ge(kept, B)
                    for c in range(NCH):
                        op = nc.vector.tensor_reduce(peak[:, c:c + 1], xT[:, :, c * CH:(c + 1) * CH], AX.XY, ALU.max,
                                                     apply_absolute_value=True)
                    op.then_inc(peaked, 1)

        def scale_steps(dve, link, found, reduced, at, n_peaks, unit):
            nc.vector.reduce_max(top[:], peak[:, 0:n_peaks], AX.X).then_inc(found, 1)
            dve.wait_ge(reduced, 1)
            one = scales[:, at:at + 1]
            link(nc.vector.tensor_scalar(one, whole[:], unit, None, ALU.mult))
            link(nc.vector.tensor_scalar(one, one, 1.0 / QMAX, LEAST, ALU.mult, ALU.max))
            link(nc.vector.reciprocal(inverse[:, at:at + 1], one))

        def reduce_step(pool, found, reduced):
            pool.wait_ge(found, 1)
            nc.gpsimd.partition_all_reduce(whole[:], top[:], P, RMAX).then_inc(reduced, 1)

        def linker(dve, chain, count):
            def link(op):
                count[0] += 1
                op.then_inc(chain, 1)
                dve.wait_ge(chain, count[0])
            return link

        BANKS = 4
        PAIR = 2
        GROUPS = IB // PAIR
        NG = NCH * GROUPS

        wide_f = sb("wide", [P, IB, TOK], F32)
        gate_q = sb("gate_q", [P, IB, TOK], I16)
        sig = [sb(f"sig{i}", [P, PAIR, CH], F32) for i in range(2)]
        sig_q = [sb(f"sig_q{i}", [P, PAIR, CH], U16) for i in range(2)]
        prod_ps = ctx.enter_context(nc.psum_tensor("ffn_prod_ps", [P, BANKS, 512], F32))

        def products(pe, w, mm, ev):
            with pe.Fori(0, NCH // 2) as turn:
                for i in range(2 * IB):
                    c, f = i // IB, i % IB
                    pe.wait_ge(ev, turn * (2 * IB) + (i + 1))
                    for k in range(KC):
                        op = nc.tensor.matmul(prod_ps[:, i % BANKS, :], w[:, k, f * P:f * P + P],
                                              xT[:, k, bass.ds(turn * (2 * CH) + c * CH, CH)],
                                              start=(k == 0), stop=(k == KC - 1))
                    op.then_inc(mm, 1)

        def take_products(act, turn, i, mm, ev):
            c, f = i // IB, i % IB
            act.wait_ge(mm, turn * (2 * IB) + (i + 1))
            nc.scalar.activation(wide_f[:, f, bass.ds(turn * (2 * CH) + c * CH, CH)], prod_ps[:, i % BANKS, :],
                                 ACT.Copy, scale=scales[:, X_:X_ + 1]).then_inc(ev, 1)

        with ExitStack() as stage, nc.Block() as block:
            found, reduced, chain, xq, mm, ev = (
                sem(f"gate_{n}") for n in ("found", "reduced", "chain", "xq", "mm", "ev"))

            @block.gpsimd
            def _(pool):
                reduce_step(pool, found, reduced)

            @block.vector
            def _(dve):
                link = linker(dve, chain, [0])
                scale_steps(dve, link, found, reduced, X_, NCH, 1.0)
                link(nc.vector.tensor_scalar(xT[:], xT[:], inverse[:, X_:X_ + 1], ROUND, ALU.mult, ALU.add))
                nc.vector.tensor_scalar(xT[:], xT[:], -ROUND, QMAX, ALU.add, ALU.min).then_inc(xq, 1)
                with dve.Fori(0, NCH) as c:
                    for g in range(GROUPS):
                        dve.wait_ge(ev, c * IB + (PAIR * (g + 1) + BANKS))
                        nc.vector.tensor_reduce(peak[:, bass.ds(c * GROUPS + g, 1)],
                                                wide_f[:, PAIR * g:PAIR * g + PAIR, bass.ds(c * CH, CH)],
                                                AX.XY, ALU.max, apply_absolute_value=True)

            @block.tensor
            def _(pe):
                pe.wait_ge(xq, 1)
                products(pe, w_gate, mm, ev)

            @block.scalar
            def _(act):
                act.sem_inc(ev, BANKS)
                act.wait_ge(xq, 1)
                with act.Fori(0, NCH // 2) as turn:
                    for i in range(2 * IB):
                        take_products(act, turn, i, mm, ev)

        with ExitStack() as stage, nc.Block() as block:
            found, reduced, chain, gq, mm, ev, sg, step_done, used = (
                sem(f"up_{n}")
                for n in ("found", "reduced", "chain", "gq", "mm", "ev", "sg", "step_done", "used"))

            @block.gpsimd
            def _(pool):
                reduce_step(pool, found, reduced)

            @block.vector
            def _(dve):
                link = linker(dve, chain, [0])
                scale_steps(dve, link, found, reduced, GATE, NG, 1.0)
                with dve.Fori(0, NCH) as c:
                    cols = bass.ds(c * CH, CH)
                    nc.vector.tensor_scalar(gate_q[:, :, cols], wide_f[:, :, cols], inverse[:, GATE:GATE + 1], None,
                                            ALU.mult).then_inc(gq, 1)
                dve.wait_ge(gq, NCH)
                with dve.Fori(0, NCH // 2) as turn:
                    for i in range(2 * GROUPS):
                        c, g = i // GROUPS, i % GROUPS
                        n = turn * (2 * GROUPS) + i
                        cols = bass.ds(turn * (2 * CH) + c * CH, CH)
                        fs = slice(PAIR * g, PAIR * g + PAIR)
                        dve.wait_ge(sg, n * 2 + 2)
                        nc.vector.scalar_tensor_tensor(sig[i % 2][:], gate_q[:, fs, cols], scales[:, GATE:GATE + 1],
                                                       sig_q[i % 2][:], ALU.mult, ALU.mult).then_inc(step_done, 1)
                        dve.wait_ge(step_done, n + 1)
                        nc.vector.tensor_reduce(peak[:, bass.ds(n, 1)], sig[i % 2][:], AX.XY, ALU.max,
                                                apply_absolute_value=True).then_inc(used, 1)
                        dve.wait_ge(ev, turn * (2 * IB) + (PAIR * (i + 1) + BANKS))
                        nc.vector.tensor_reduce(peak[:, bass.ds(n + NG, 1)], wide_f[:, fs, cols], AX.XY, ALU.max,
                                                apply_absolute_value=True)

            @block.tensor
            def _(pe):
                products(pe, w_up, mm, ev)

            @block.scalar
            def _(act):
                act.sem_inc(ev, BANKS)
                act.sem_inc(used, 2)
                with act.Fori(0, NCH // 2) as turn:
                    for i in range(2 * IB):
                        c, f = i // IB, i % IB
                        if f == 0:
                            act.wait_ge(gq, turn * 2 + (c + 1))
                        take_products(act, turn, i, mm, ev)
                        if f % PAIR == PAIR - 1:
                            g = i // PAIR
                            act.wait_ge(used, turn * (2 * GROUPS) + (g + 1))
                            nc.scalar.activation(sig[g % 2][:],
                                                 gate_q[:, f + 1 - PAIR:f + 1, bass.ds(turn * (2 * CH) + c * CH, CH)],
                                                 ACT.Sigmoid, scale=scales[:, GATE:GATE + 1]).then_inc(sg, 1)
                            act.wait_ge(sg, turn * (4 * GROUPS) + (2 * g + 1))
                            nc.scalar.activation(sig_q[g % 2][:], sig[g % 2][:], ACT.Copy, scale=65536.0)\
                              .then_inc(sg, 1)

        pool_of = xT[:].rearrange("p k t -> p (k t)")
        up_q = [pool_of[:, i * PAIR * CH // 2:(i + 1) * PAIR * CH // 2].bitcast(I16).rearrange("p (f t) -> p f t", f=PAIR)
                for i in range(2)]

        with ExitStack() as stage, nc.Block() as block:
            found, reduced, found2, reduced2, chain, ready, sg, step_done, used = (
                sem(f"product_{n}")
                for n in ("found", "reduced", "found2", "reduced2", "chain", "ready", "sg", "step_done", "used"))
            top2 = stage.enter_context(nc.sbuf_tensor("ffn_top2", [P, 1], F32))
            whole2 = stage.enter_context(nc.sbuf_tensor("ffn_whole2", [P, 1], F32))

            @block.gpsimd
            def _(pool):
                reduce_step(pool, found, reduced)
                pool.wait_ge(found2, 1)
                nc.gpsimd.partition_all_reduce(whole2[:], top2[:], P, RMAX).then_inc(reduced2, 1)

            @block.vector
            def _(dve):
                link = linker(dve, chain, [0])
                nc.vector.reduce_max(top2[:], peak[:, NG:2 * NG], AX.X).then_inc(found2, 1)
                scale_steps(dve, link, found, reduced, GATED, NG, 1.0 / 65536)
                dve.wait_ge(reduced2, 1)
                one = scales[:, UP:UP + 1]
                link(nc.vector.tensor_scalar(one, whole2[:], 1.0 / QMAX, LEAST, ALU.mult, ALU.max))
                link(nc.vector.reciprocal(inverse[:, UP:UP + 1], one))
                link(nc.vector.tensor_tensor(both_scales[:], scales[:, GATED:GATED + 1], one, ALU.mult))
                dve.sem_inc(ready, 1)
                with dve.Fori(0, NCH // 2) as turn:
                    for i in range(2 * GROUPS):
                        c, g = i // GROUPS, i % GROUPS
                        n = turn * (2 * GROUPS) + i
                        cols = bass.ds(turn * (2 * CH) + c * CH, CH)
                        fs = slice(PAIR * g, PAIR * g + PAIR)
                        m = n * 3
                        dve.wait_ge(sg, n * 3 + 3)
                        nc.vector.scalar_tensor_tensor(sig[i % 2][:], gate_q[:, fs, cols], scales[:, GATE:GATE + 1],
                                                       sig_q[i % 2][:], ALU.mult, ALU.mult).then_inc(step_done, 1)
                        dve.wait_ge(step_done, m + 1)
                        nc.vector.tensor_scalar(gate_q[:, fs, cols], sig[i % 2][:], inverse[:, GATED:GATED + 1],
                                                1.0 / 65536, ALU.mult, ALU.mult).then_inc(step_done, 1)
                        dve.wait_ge(step_done, m + 2)
                        nc.vector.tensor_tensor(wide_f[:, fs, cols], gate_q[:, fs, cols], up_q[i % 2], ALU.mult)\
                          .then_inc(step_done, 1)
                        dve.wait_ge(step_done, m + 3)
                        nc.vector.tensor_reduce(peak[:, bass.ds(n, 1)], wide_f[:, fs, cols], AX.XY, ALU.max,
                                                apply_absolute_value=True).then_inc(used, 1)

            @block.scalar
            def _(act):
                act.sem_inc(used, 2)
                act.wait_ge(ready, 1)
                with act.Fori(0, NCH // 2) as turn:
                    for i in range(2 * GROUPS):
                        c, g = i // GROUPS, i % GROUPS
                        act.wait_ge(used, turn * (2 * GROUPS) + (i + 1))
                        nc.scalar.activation(sig[i % 2][:],
                                             gate_q[:, PAIR * g:PAIR * g + PAIR, bass.ds(turn * (2 * CH) + c * CH, CH)],
                                             ACT.Sigmoid, scale=scales[:, GATE:GATE + 1]).then_inc(sg, 1)
                        nc.scalar.activation(up_q[i % 2],
                                             wide_f[:, PAIR * g:PAIR * g + PAIR, bass.ds(turn * (2 * CH) + c * CH, CH)],
                                             ACT.Copy, scale=inverse[:, UP:UP + 1]).then_inc(sg, 1)
                        act.wait_ge(sg, turn * (6 * GROUPS) + (3 * i + 1))
                        nc.scalar.activation(sig_q[i % 2][:], sig[i % 2][:], ACT.Copy, scale=65536.0).then_inc(sg, 1)

        at = [0]

        def piece(*shape):
            n = 1
            for d in shape:
                n *= d
            v = pool_of[:, at[0]:at[0] + n]
            at[0] += n
            return v.rearrange("p (a b) -> p a b", b=shape[-1])

        prod_q = [piece(IB, S) for _ in range(2)]
        x_rows = [piece(ST, D) for _ in range(2)]
        y_rows = [piece(ST, D) for _ in range(2)]
        with ExitStack() as stage, nc.Block() as block:
            found, reduced, chain, rounded, quant, mm, ev = (
                sem(f"down_{n}")
                for n in ("found", "reduced", "chain", "rounded", "quant", "mm", "ev"))
            x_in = [sem(f"down_x_in{i}") for i in range(2)]
            y_out = [sem(f"down_y_out{i}") for i in range(2)]

            @block.sync
            def _(sp):
                with sp.Fori(0, B // 2) as turn:
                    for par in range(2):
                        b = turn * 2 + par
                        sp.wait_ge(ev, b + 1)
                        sp.dma_start(x_rows[par], x_dram[bass.ds(b * S, S), :].rearrange("(s p) d -> p s d", p=P))\
                          .then_inc(x_in[par], 16)

            @block.gpsimd
            def _(pool):
                reduce_step(pool, found, reduced)

            @block.vector
            def _(dve):
                dve.sem_inc(ev, 2)
                link = linker(dve, chain, [0])
                scale_steps(dve, link, found, reduced, PROD, NG, both_scales[:, 0:1])
                link(nc.vector.tensor_tensor(inverse[:, PROD:PROD + 1], inverse[:, PROD:PROD + 1], both_scales[:], ALU.mult))

                def quantise(b, par):
                    cols = bass.ds(b * S, S)
                    nc.vector.tensor_scalar(wide_f[:, :, cols], wide_f[:, :, cols], inverse[:, PROD:PROD + 1], ROUND,
                                            ALU.mult, ALU.add).then_inc(rounded, 1)
                    dve.wait_ge(rounded, b + 1)
                    if not isinstance(b, int) or b >= 2:
                        dve.wait_ge(mm, b - 1)
                    nc.vector.tensor_scalar(prod_q[par], wide_f[:, :, cols], -ROUND, QMAX, ALU.add, ALU.min)\
                      .then_inc(quant, 1)

                def finish(b, par):
                    dve.wait_ge(mm, b + 1)
                    dve.wait_ge(x_in[par], (b - par) * 8 + 16)
                    if not isinstance(b, int) or b >= 2:
                        dve.wait_ge(y_out[par], (b - par) * 8)
                    nc.vector.scalar_tensor_tensor(y_rows[par], prod_ps[:, par, :].rearrange("p (s d) -> p s d", s=ST),
                                                   scales[:, PROD:PROD + 1], x_rows[par], ALU.mult, ALU.add)\
                      .then_inc(ev, 1)

                quantise(0, 0)
                quantise(1, 1)
                finish(0, 0)
                quantise(2, 0)
                finish(1, 1)
                with dve.Fori(0, (B - 4) // 2) as turn:
                    for par in range(2):
                        b = turn * 2 + (2 + par)
                        quantise(b + 1, 1 - par)
                        finish(b, par)
                quantise(B - 1, 1)
                finish(B - 2, 0)
                finish(B - 1, 1)

            @block.tensor
            def _(pe):
                with pe.Fori(0, B // 2) as turn:
                    for par in range(2):
                        b = turn * 2 + par
                        pe.wait_ge(quant, b + 1)
                        pe.wait_ge(ev, b + 1)
                        for s in range(ST):
                            for k in range(IB):
                                op = nc.tensor.matmul(prod_ps[:, par, s * D:s * D + D], prod_q[par][:, k, s * P:s * P + P],
                                                      w_down[:, k, :], start=(k == 0), stop=(k == IB - 1))
                        op.then_inc(mm, 1)

            @block.scalar
            def _(act):
                with act.Fori(0, B // 2) as turn:
                    for par in range(2):
                        b = turn * 2 + par
                        act.wait_ge(ev, b + 3)
                        act.dma_start(out_dram[bass.ds(b * S, S), :].rearrange("(s p) d -> p s d", p=P), y_rows[par])\
                           .then_inc(y_out[par], 16)
                for i in range(2):
                    act.wait_ge(y_out[i], 8 * B)


def program(nc, a, out, phases=(1, 2, 3, 4, 5, 6)):
    with ExitStack() as top:
        ident = top.enter_context(nc.sbuf_tensor("ident", [P, P], F32))
        ident_bf = top.enter_context(nc.sbuf_tensor("ident_bf", [P, P], BF16))
        setup = top.enter_context(nc.semaphore("setup"))
        x_flat = a["x"].rearrange("b s d -> (b s) d")
        out_flat = out.rearrange("b s d -> (b s) d")
        x_dram = nc.dram_tensor("x_before_ffn_dram", [B * S, D], F32).ap() if 6 in phases else out_flat
        with nc.Block() as block:
            @block.gpsimd
            def _(pool):
                for m in (ident, ident_bf):
                    nc.gpsimd.memset(m[:], 0.0).then_inc(setup, 1)
                pool.wait_ge(setup, 2)
                for m in (ident, ident_bf):
                    nc.gpsimd.affine_select(out=m[:], in_=m[:], compare_op=ALU.not_equal, fill=1.0, base=0,
                                            pattern=[[-1, P]], channel_multiplier=1).then_inc(setup, 1)
        if phases != [6]:
            layers(nc, a, ident, ident_bf, x_flat, x_dram, phases)
            x_flat = x_dram
        if 6 in phases:
            quantised_ffn(nc, a, ident, x_flat, out_flat)


def layers(nc, a, ident, ident_bf, x_flat, x_dram, phases):
    with ExitStack() as ctx:
        x_sb = ctx.enter_context(nc.sbuf_tensor("x_sb", [P, TILES, D], F32))
        x_loaded = ctx.enter_context(nc.semaphore("x_loaded"))
        stored = ctx.enter_context(nc.semaphore("stored"))
        q_stack = [ctx.enter_context(nc.sbuf_tensor(f"q_stack{i}", [P, H, S], F32R)) for i in range(2)]
        k_stack = [ctx.enter_context(nc.sbuf_tensor(f"k_stack{i}", [P, H, S], F32R)) for i in range(2)]
        v_aug = [ctx.enter_context(nc.sbuf_tensor(f"v_aug{i}", [P, ST, H, VW], F32)) for i in range(2)]
        q_zeroed, k_zeroed = (ctx.enter_context(nc.semaphore(n)) for n in ("q_zeroed", "k_zeroed"))
        x_view = x_flat.rearrange("(t p) d -> p t d", p=P)
        out_view = x_dram.rearrange("(t p) d -> p t d", p=P)
        with nc.Block() as block:
            @block.sync
            def _(sp):
                for n in range(4):
                    tiles = slice(n * TILES // 4, (n + 1) * TILES // 4)
                    sp.dma_start(x_sb[:, tiles, :], x_view[:, tiles, :]).then_inc(x_loaded, 16)
                sp.wait_ge(x_loaded, 64)

            @block.gpsimd
            def _(pool):
                for i in range(2):
                    nc.gpsimd.memset(v_aug[i][:], 0.0)
                    op = nc.gpsimd.memset(q_stack[i][:].bitcast(F32), 0.0)
                op.then_inc(q_zeroed, 1)
                pool.wait_ge(q_zeroed, 1)
                for i in range(2):
                    op = nc.gpsimd.memset(v_aug[i][:, :, :, HD:HD + 1], 1.0)
                op.then_inc(q_zeroed, 1)
                pool.wait_ge(q_zeroed, 2)
                for i in range(2):
                    nc.gpsimd.memset(q_stack[i][PAD_ROW:PAD_ROW + 1].bitcast(F32), 1.0)

            @block.vector
            def _(dve):
                for i in range(2):
                    op = nc.vector.memset(k_stack[i][:].bitcast(F32), 0.0)
                op.then_inc(k_zeroed, 1)
                dve.wait_ge(k_zeroed, 1)
                for i in range(2):
                    nc.vector.memset(k_stack[i][MAX_ROW:MAX_ROW + 2].bitcast(F32), 1.0)

        scratch = lambda kind, nk: {
            "q": nc.dram_tensor(f"{kind}_q_parts_dram", [2, 2, D, S], F32).ap(),
            "k": nc.dram_tensor(f"{kind}_k_parts_dram", [2, 2, D, nk], F32).ap(),
            "m": nc.dram_tensor(f"{kind}_m_parts_dram", [2, 2, H // 2, S], F32).ap(),
            "pad": nc.dram_tensor(f"{kind}_pad_dram", [B, S2], F32).ap(),
        }
        w = {"wq": a["L0_attn_w_qkv"][:, 0:D], "wk": a["L0_attn_w_qkv"][:, D:2 * D],
             "wv": a["L0_attn_w_qkv"][:, 2 * D:3 * D], "wo": a["L0_attn_w_out"],
             "bq": a["L0_attn_b_qkv"][0:D], "bk": a["L0_attn_b_qkv"][D:2 * D],
             "bv": a["L0_attn_b_qkv"][2 * D:3 * D], "bo": a["L0_attn_b_out"]}
        if 1 in phases:
            attention(nc, "window", x_sb, q_stack, k_stack, v_aug, ident, ident_bf, w, scratch("window", S))
        if 3 in phases:
            slots_dram = nc.dram_tensor("moe_slots_dram", [MT * TM, D], F32).ap()
            y_dram = nc.dram_tensor("moe_y_dram", [MT * TM, D], F32).ap()
        names = {"wq": "Wq", "wk": "Wk", "wv": "Wv", "wo": "Wo", "bq": "bq", "bk": "bk", "bv": "bv", "bo": "bo"}
        for phase, kind, layer, mask in ((2, "cross_pad", "L0_xattn", "mask_BxS2_bk1"),
                                         (3, "experts", None, None), (4, "causal", "L1_attn", None),
                                         (5, "cross_mask", "L1_xattn", "mask_SxS2_bk1")):
            if phase not in phases:
                continue
            if kind == "experts":
                experts(nc, a, x_sb, ident, slots_dram, y_dram)
                continue
            w = {k: a.get(f"{layer}_{n}") for k, n in names.items()}
            if kind == "causal":
                attention(nc, kind, x_sb, q_stack, k_stack, v_aug, ident, ident_bf, w, scratch(kind, S))
            else:
                attention(nc, kind, x_sb, q_stack, k_stack, v_aug, ident, ident_bf, w, scratch(kind, S2),
                          a["ctx_1024"].rearrange("b s d -> (b s) d"), a[mask])
            if kind == "cross_pad":
                with nc.Block() as block:
                    @block.vector
                    def _(dve):
                        for i in range(2):
                            nc.vector.memset(k_stack[i][PAD_ROW:PAD_ROW + 1, :, 0:S2].bitcast(F32), 0.0)
        with nc.Block() as block:
            @block.sync
            def _(sp):
                for n in range(4):
                    tiles = slice(n * TILES // 4, (n + 1) * TILES // 4)
                    sp.dma_start(out_view[:, tiles, :], x_sb[:, tiles, :]).then_inc(stored, 16)
                sp.wait_ge(stored, 64)


def pack(inputs):
    import numpy as np

    a = {n: np.asarray(v) for n, v in inputs.items()}
    rows = lambda w: w.reshape(NE, w.shape[1] // P, P, w.shape[2]).transpose(0, 2, 1, 3).reshape(NE, P, -1)
    cols = lambda b: b.reshape(NE, FB, P).transpose(0, 2, 1)
    a["moe_w"] = np.concatenate(
        [rows(a.pop("L0_ffn_w1")), rows(a.pop("L0_ffn_w2")), rows(a.pop("L0_ffn_w3")), cols(a.pop("L0_ffn_b1")),
         cols(a.pop("L0_ffn_b2")), np.broadcast_to(a.pop("L0_ffn_b3")[:, None, :], (NE, P, D))], axis=2)
    for n in ("Wq", "Wk", "Wv", "Wo"):
        a[f"L1_attn_{n}"] = a[f"L1_attn_{n}"].T
    return {n: np.ascontiguousarray(v) for n, v in a.items()}


_SHAPE = (16, 256, 256)


def kernel(**inputs):
    import numpy as np
    import concourse.bacc as bacc
    from concourse.bass_utils import run_bass_kernel_spmd

    nc = bacc.Bacc("TRN2", target_bir_lowering=False, num_devices=1)
    arrays = pack(inputs)
    arguments = {n: nc.dram_tensor(f"{n}_in", v.shape, mybir.dt.from_np(v.dtype), kind="ExternalInput").ap()
                 for n, v in arrays.items()}
    out = nc.dram_tensor("x_out", _SHAPE, F32, kind="ExternalOutput").ap()
    program(nc, arguments, out)
    result = run_bass_kernel_spmd(nc, [{f"{n}_in": v for n, v in arrays.items()}], core_ids=[0])
    return result.results[0]["x_out"]
```
